# Optimizing a Trainium2 kernel written in Bass

```python
import numpy as np
import jax
import jax.numpy as jnp

def _softmax(x, axis=-1):
    return jax.nn.softmax(x, axis=axis)

def _gelu(x):
    return jax.nn.gelu(x, approximate=True)

def _silu(x):
    return jax.nn.silu(x)

def _sigmoid(x):
    return jax.nn.sigmoid(x)

def _layernorm(x, axis=-1, eps=1e-05):
    m = jnp.mean(x, axis=axis, keepdims=True)
    v = jnp.var(x, axis=axis, keepdims=True)
    return (x - m) / jnp.sqrt(v + eps)

def _scatter_add(tgt, idx, src, axis=0):
    return tgt.at[idx].add(src)

def _segment_sum(src, seg, n):
    return jax.ops.segment_sum(src, seg, n)
kernel_name = 'mk_adaln_d1_jaxref_r8_f94c05'

def setup_inputs(seed: int=0):
    np.random.seed(seed)
    _w = jnp.asarray

    def _L0_attn_setup():
        import jax, jax.numpy as jnp
        import numpy as np
        import math
        E, N, K, R = (128, 16, 4, 64)
        B, L = (2, 256)
        key = jax.random.key(seed)
        ks = jax.random.split(key, 8)
        gn = lambda k, sh, sc: jax.random.normal(k, sh, dtype=jnp.float32) * sc
        W_z = gn(ks[0], (E, E), E ** (-0.5))
        W_params = gn(ks[1], (R + 2 * N, E), E ** (-0.5))
        conv_w = gn(ks[2], (E, 1, K), 0.5)
        dt_std = R ** (-0.5) * 0.1
        W_dt = jax.random.uniform(ks[3], (E, R), jnp.float32, -dt_std, dt_std)
        b_dt = jnp.full((E,), math.log(math.expm1(0.001)), dtype=jnp.float32)
        A_log = jnp.tile(jnp.log(jnp.arange(1, N + 1, dtype=jnp.float32))[None, :], (E, 1))
        D = jnp.ones((E,), dtype=jnp.float32)
        W_out = gn(ks[4], (E, E), E ** (-0.5))
        x = jax.random.normal(ks[5], (B, L, E), dtype=jnp.float32)
        return dict(x=x, W_z=W_z, W_params=W_params, conv_w=conv_w, W_dt=W_dt, b_dt=b_dt, A_log=A_log, D=D, W_out=W_out)
    _L0_attn_in = _L0_attn_setup()

    def _L0_ffn_setup():
        import jax, jax.numpy as jnp
        import numpy as np
        import math
        D_MODEL = 128
        N_EXPERTS = 16
        D_FF = 512
        CAP_FACTOR = 1.25
        MIN_CAPACITY = 4

        def _capacity(num_tokens, num_experts):
            cap = math.floor(CAP_FACTOR * num_tokens / num_experts)
            cap += cap % 2
            return max(cap, MIN_CAPACITY)

        def _top1_router(gate_logits, capacity):
            s, e = gate_logits.shape
            probs = jax.nn.softmax(gate_logits, axis=-1)
            top1 = jnp.argmax(gate_logits, axis=-1)
            mask = jax.nn.one_hot(top1, e, dtype=jnp.int32)
            ranks = jnp.cumsum(mask, axis=0) - 1
            mask = mask * (ranks < capacity).astype(jnp.int32)
            rank1 = jnp.sum(mask * ranks, axis=-1)
            ranks_oh = jax.nn.one_hot(rank1, capacity, dtype=probs.dtype)
            weight = mask.astype(probs.dtype) * probs
            combine_weights = weight[:, :, None] * ranks_oh[:, None, :]
            sec_mask = combine_weights > 0
            return (combine_weights, sec_mask)
        key = jax.random.key(seed)
        k1, k2, k3, k4 = jax.random.split(key, 4)
        x = jax.random.normal(k1, (4, 256, D_MODEL), dtype=jnp.float32)
        gate_w = jax.random.normal(k2, (N_EXPERTS, D_MODEL), dtype=jnp.float32) * math.sqrt(0.1 / D_MODEL)
        w1 = jax.random.normal(k3, (N_EXPERTS, D_MODEL, D_FF), dtype=jnp.float32) * (1.0 / math.sqrt(D_MODEL))
        w2 = jax.random.normal(k4, (N_EXPERTS, D_FF, D_MODEL), dtype=jnp.float32) * (1.0 / math.sqrt(D_FF))
        return {'x': x, 'gate_w': gate_w, 'w1': w1, 'w2': w2}
    _L0_ffn_in = _L0_ffn_setup()
    _L0_c = _w((lambda *s: np.random.randn(*s).astype(np.float32) * 0.05)(8, 128))
    _L0_wmod = _w((lambda *s: np.random.randn(*s).astype(np.float32) * 0.05)(128, 6 * 128) * 128 ** (-0.5))
    _d = {'L0_attn_x': _L0_attn_in['x'], 'L0_attn_W_z': _L0_attn_in['W_z'], 'L0_attn_W_params': _L0_attn_in['W_params'], 'L0_attn_conv_w': _L0_attn_in['conv_w'], 'L0_attn_W_dt': _L0_attn_in['W_dt'], 'L0_attn_b_dt': _L0_attn_in['b_dt'], 'L0_attn_A_log': _L0_attn_in['A_log'], 'L0_attn_D': _L0_attn_in['D'], 'L0_attn_W_out': _L0_attn_in['W_out'], 'L0_ffn_gate_w': _L0_ffn_in['gate_w'], 'L0_ffn_w1': _L0_ffn_in['w1'], 'L0_ffn_w2': _L0_ffn_in['w2'], 'L0_c': _L0_c, 'L0_wmod': _L0_wmod}
    _x0 = _d['L0_attn_x']
    _d['L0_attn_x'] = jax.random.normal(jax.random.fold_in(jax.random.key(seed), 1), (8, 512, 128), dtype=_x0.dtype)
    del _x0
    return _d

def reference(L0_attn_x, L0_attn_W_z, L0_attn_W_params, L0_attn_conv_w, L0_attn_W_dt, L0_attn_b_dt, L0_attn_A_log, L0_attn_D, L0_attn_W_out, L0_ffn_gate_w, L0_ffn_w1, L0_ffn_w2, L0_c, L0_wmod):

    def _L0_attn_ref(x, W_z, W_params, conv_w, W_dt, b_dt, A_log, D, W_out):
        import jax, jax.numpy as jnp
        import numpy as np
        import math
        E, N, K, R = (128, 16, 4, 64)
        B, L = (2, 256)
        b, l, e = x.shape
        n = A_log.shape[1]
        r = W_dt.shape[1]
        k = conv_w.shape[-1]
        z = x @ W_z.T
        params = x @ W_params.T
        dt_unproj = params[..., :r]
        C_proj = params[..., r + n:]
        dt = jax.nn.softplus(dt_unproj @ W_dt.T + b_dt)
        xc = jax.lax.conv_general_dilated(x.transpose(0, 2, 1), conv_w, (1,), [(k - 1, 0)], dimension_numbers=('NCH', 'OIH', 'NCH'), feature_group_count=e)
        u = jax.nn.silu(xc.transpose(0, 2, 1))
        A = -jnp.exp(A_log)
        A_tilde = jnp.exp(dt[..., None] * A[None, None])
        B_tilde = jnp.where(jnp.abs(A)[None, None] < 1e-05, dt[..., None], (A_tilde - 1.0) / (A[None, None] + 1e-10))
        h0 = B_tilde[:, 0] * u[:, 0, :, None]

        def step(h, inp):
            a, bt, uu = inp
            h_new = a * h + bt * uu[..., None]
            return (h_new, h_new)
        xs = (A_tilde[:, :-1].transpose(1, 0, 2, 3), B_tilde[:, :-1].transpose(1, 0, 2, 3), u[:, :-1].transpose(1, 0, 2))
        _, hs = jax.lax.scan(step, h0, xs)
        h = jnp.concatenate([h0[None], hs], axis=0).transpose(1, 0, 2, 3)
        y = jnp.einsum('bln,blen->ble', C_proj, h)
        y_ssm = y + u * D
        y_gated = y_ssm * jax.nn.silu(z)
        return y_gated @ W_out.T

    def _L0_ffn_ref(x, gate_w, w1, w2):
        import jax, jax.numpy as jnp
        import numpy as np
        import math
        D_MODEL = 128
        N_EXPERTS = 16
        D_FF = 512
        CAP_FACTOR = 1.25
        MIN_CAPACITY = 4

        def _capacity(num_tokens, num_experts):
            cap = math.floor(CAP_FACTOR * num_tokens / num_experts)
            cap += cap % 2
            return max(cap, MIN_CAPACITY)

        def _top1_router(gate_logits, capacity):
            s, e = gate_logits.shape
            probs = jax.nn.softmax(gate_logits, axis=-1)
            top1 = jnp.argmax(gate_logits, axis=-1)
            mask = jax.nn.one_hot(top1, e, dtype=jnp.int32)
            ranks = jnp.cumsum(mask, axis=0) - 1
            mask = mask * (ranks < capacity).astype(jnp.int32)
            rank1 = jnp.sum(mask * ranks, axis=-1)
            ranks_oh = jax.nn.one_hot(rank1, capacity, dtype=probs.dtype)
            weight = mask.astype(probs.dtype) * probs
            combine_weights = weight[:, :, None] * ranks_oh[:, None, :]
            sec_mask = combine_weights > 0
            return (combine_weights, sec_mask)
        tokens = x.reshape(-1, D_MODEL)
        s = tokens.shape[0]
        capacity = _capacity(s, N_EXPERTS)
        gate_logits = tokens.astype(jnp.float32) @ gate_w.T
        combine_weights, sec_mask = _top1_router(gate_logits, capacity)
        dispatch = jnp.einsum('sec,sd->ecd', sec_mask.astype(tokens.dtype), tokens)
        h = jax.nn.gelu(jnp.einsum('ecd,edf->ecf', dispatch, w1))
        expert_out = jnp.einsum('ecf,efd->ecd', h, w2)
        out = jnp.einsum('sec,ecd->sd', combine_weights.astype(tokens.dtype), expert_out)
        return out.reshape(x.shape)
    x = L0_attn_x
    mod = (_silu(L0_c) @ L0_wmod).reshape(L0_c.shape[0], 6, 1, -1)
    sa, ca, ga, sb, cb, gb = (mod[:, 0], mod[:, 1], mod[:, 2], mod[:, 3], mod[:, 4], mod[:, 5])
    ga = (2 * (ga >= 0) - 1) * jnp.maximum(jnp.abs(ga), 0.25)
    gb = (2 * (gb >= 0) - 1) * jnp.maximum(jnp.abs(gb), 0.25)
    h = _layernorm(x, axis=-1) * (1 + ca) + sa
    x = x + ga * _L0_attn_ref(h, L0_attn_W_z, L0_attn_W_params, L0_attn_conv_w, L0_attn_W_dt, L0_attn_b_dt, L0_attn_A_log, L0_attn_D, L0_attn_W_out)
    h = _layernorm(x, axis=-1) * (1 + cb) + sb
    x = x + gb * _L0_ffn_ref(h, L0_ffn_gate_w, L0_ffn_w1, L0_ffn_w2)
    return x

_drawn_inputs = setup_inputs


def setup_inputs(seed=0):
    import zlib

    import numpy as np

    out = dict(_drawn_inputs(seed))
    spreads = {'L0_attn_b_dt': (-6.907255172729492, 0.6), 'L0_attn_D': (1.0, 0.6)}
    factors = {'L0_attn_W_params': 3.18,
     'L0_attn_W_dt': 8.0,
     'L0_attn_A_log': 4.796,
     'L0_ffn_gate_w': 3.155,
     'L0_ffn_w1': 3.315,
     'L0_ffn_w2': 2.978}
    for name, (base, spread) in spreads.items():
        noise = np.random.default_rng([zlib.crc32(name.encode()), seed]).standard_normal(out[name].shape)
        drawn = base * np.exp(spread * noise) if base else spread * noise
        out[name] = jnp.asarray(drawn.astype(out[name].dtype))
    for name, factor in factors.items():
        out[name] = (out[name] * factor).astype(out[name].dtype)
    return out
```

```python
from contextlib import ExitStack

import numpy as np

import concourse.bass as bass
from concourse import mybir

F32 = mybir.dt.float32
BF16 = mybir.dt.bfloat16
I32 = mybir.dt.int32
ALU = mybir.AluOpType
ACT = mybir.ActivationFunctionType
AX = mybir.AxisListType

P = 128
BATCH, SEQ, E = 8, 512, 128
TOK = BATCH * SEQ
TILES = TOK // P
NST, RANK, KCONV = 16, 64, 4
GB = 2
GROUPS = BATCH // GB
GT = GB * SEQ
GTILES = GT // P
NEXP, DFF = 16, 512
FC = DFF // P
CAP = int(1.25 * TOK / NEXP)
CAP += CAP % 2
SLOTS = NEXP * CAP
EPS = 1e-5
SMALL_A = 1e-5
SEQ1 = SEQ + 1
HPAD = KCONV - 1
NPART = 3
STEPS = GROUPS * NST
ON_POOL = {1, 3, 5, 7, 9, 11, 13}
RING_A, RING_K, RING_P = 3, 3, 4


def on_pool(m):
    return m % NST in ON_POOL


def pool_before(m):
    return sum(on_pool(i) for i in range(m))


def dve_before(m):
    return m - pool_before(m)


def build(nc, x, w_zT, w_params, w_paramsT, conv_w, w_dtT, b_dt, a_log, a_logT, d_skip, w_outT,
          gate_wT, w1, w2, cT, wmod, ident_in, sel_in, tri_in, em16_in, tok_in, out):
    disp = nc.dram_tensor("disp", [SLOTS + TOK, E], F32, kind="Internal").ap()
    eout = nc.dram_tensor("eout", [SLOTS, E], F32, kind="Internal").ap()
    with ExitStack() as ctx:
        def sb(name, shape, dt=F32):
            return ctx.enter_context(nc.sbuf_tensor(name, shape, dt))

        def ps(name, shape, dt=F32):
            return ctx.enter_context(nc.psum_tensor(name, shape, dt))

        def sem(name):
            return ctx.enter_context(nc.semaphore(name))

        ident = sb("ident", [P, P])
        identb = sb("identb", [P, P], BF16)
        sel = sb("sel", [NPART * NST, NST, P], BF16)
        tri = sb("tri", [P, P], BF16)
        ones = sb("ones", [P, P], BF16)
        em16 = sb("em16", [P, NEXP])
        toki = sb("toki", [P, TILES])
        wz = sb("wz", [P, P])
        wp = sb("wp", [RANK, P])
        wdt = sb("wdt", [RANK, P])
        wdtp = sb("wdtp", [P, P])
        wct = sb("wct", [P, NST])
        wc = sb("wc", [NST, P])
        wgt = sb("wgt", [P, P])
        cw = sb("cw", [P, KCONV])
        dconv = sb("dconv", [P, KCONV, P])
        bdt = sb("bdt", [P, 1])
        dsk = sb("dsk", [P, 1])
        negd = sb("negd", [P, 1])
        wo = sb("wo", [P, P])
        woga = sb("woga", [P, BATCH, P])
        gw = sb("gw", [P, NEXP])
        ct = sb("ct", [P, BATCH])
        cth = sb("cth", [P, BATCH])
        silc = sb("silc", [P, BATCH])
        wm = sb("wm", [P, 6 * P])
        modT = sb("modT", [P, 2, BATCH])
        modb = sb("modb", [P, BATCH, 4, P])
        al = sb("al", [P, NST])
        aneg = sb("aneg", [P, NST])
        amsk = sb("amsk", [P, NST])
        ainv = sb("ainv", [P, NST])
        alT = sb("alT", [NST, P])
        amskT = sb("amskT", [NST, P])
        ainvT = sb("ainvT", [NST, P])
        diag = sb("diag", [P, NST, P])
        halfneg = sb("halfneg", [P, GTILES])

        xs = sb("xs", [P, TILES, E])
        x2 = xs
        ct3 = sb("ct3", [NPART * NST, TOK], BF16)
        gate = sb("gate", [P, 2, GT])
        du = sb("du", [P, 2, GB * SEQ1])
        dtb = sb("dtb", [P, 2, GB, SEQ1])
        base = sb("base", [P, 2, GB, SEQ])
        st6 = sb("st6", [P, GTILES, 6])
        mv = sb("mv", [P, GTILES, 2])
        ve = sb("ve", [P, GTILES])
        rstd = sb("rstd", [P, GTILES])
        xn = sb("xn", [P, GTILES, E])
        hT = sb("hT", [P, GB, HPAD + SEQ])
        wbuf = sb("wbuf", [P, 4, GT])
        th, expx, lnx, rem = (wbuf[:, i, :].rearrange("p (b t) -> p b t", b=GB) for i in range(4))
        ub = sb("ub", [P, GB, SEQ1])
        relx = th
        cs = sb("cs", [P, GTILES, NPART, NST], BF16)
        cr = sb("cr", [P, GTILES, NST])
        av = sb("av", [P, RING_A, GB, SEQ1])
        kv = sb("kv", [P, RING_K, GB * SEQ1])
        pv = sb("pv", [P, RING_P, GT])
        csb = sb("csb", [P, 2, GT])
        yd = sb("yd", [P, GT])
        yg = sb("yg", [P, GT])
        h2T = yd
        zero = yd
        silb = yg[:, :].rearrange("p (b c) -> p b c", b=BATCH)
        st6c = sb("st6c", [P, GTILES, 6])
        mvc = sb("mvc", [P, GTILES, 2])
        vec = sb("vec", [P, GTILES])
        rstdc = sb("rstdc", [P, GTILES])
        xn2 = sb("xn2", [P, GTILES, E])
        h2 = sb("h2", [P, 2, GTILES, E])
        gabs, gsgn = xn, xn2
        mx = sb("mx", [P, GTILES])
        eq = sb("eq", [P, GTILES, NEXP])
        cand = sb("cand", [P, GTILES, NEXP])
        first = sb("first", [P, GTILES])
        oh = sb("oh", [P, GTILES, NEXP], BF16)
        dl = sb("dl", [P, GTILES, NEXP])
        el = sb("el", [P, GTILES, NEXP])
        es = sb("es", [P, GTILES])
        prob = sb("prob", [P, GTILES])
        seen = sb("seen", [P, NEXP])
        seenb = sb("seenb", [P, NEXP], BF16)
        gsum = sb("gsum", [P, NEXP])
        rsel = sb("rsel", [P, GTILES, NEXP])
        rank = sb("rank", [P, GTILES])
        keep = sb("keep", [P, GTILES])
        slot = sb("slot", [P, GTILES])
        slot2 = sb("slot2", [P, GTILES])
        idf = sb("idf", [P, GTILES])
        idf2 = sb("idf2", [P, GTILES])
        gif = sb("gif", [P, GTILES])
        sidx = sb("sidx", [P, TILES], I32)
        gidx = sb("gidx", [P, TILES], I32)
        wtok = sb("wtok", [P, TILES])
        cb = [ps(f"cb{i}", [P, GT]) for i in range(2)]
        yp = ps("yp", [P, GT])
        mp = ps("mp", [P, GT])

        s_w = sem("s_w")
        s_x = [sem(f"s_x{g}") for g in range(GROUPS)]
        s_zero = sem("s_zero")
        s_zf = sem("s_zf")
        s_pc = sem("s_pc")
        vch = sem("vch")
        pch = sem("pch")
        ach = sem("ach")
        s_cth = sem("s_cth")
        s_silc = sem("s_silc")
        s_silb = sem("s_silb")
        s_mm0 = sem("s_mm0")
        s_pro = sem("s_pro")
        s_modb = sem("s_modb")
        s_modp = sem("s_modp")
        s_modg = sem("s_modg")
        s_aexp = sem("s_aexp")
        s_dc = sem("s_dc")
        s_ainv = sem("s_ainv")
        s_ve = sem("s_ve")
        s_rstd = sem("s_rstd")
        s_xn = sem("s_xn")
        s_xT = sem("s_xT")
        s_hT = sem("s_hT")
        s_z = sem("s_z")
        s_thz = sem("s_thz")
        s_gate = sem("s_gate")
        s_cv = sem("s_cv")
        s_thu = sem("s_thu")
        s_u = sem("s_u")
        s_du = sem("s_du")
        s_G = sem("s_G")
        s_Gr = sem("s_Gr")
        s_base = sem("s_base")
        s_xdt = sem("s_xdt")
        s_abs = sem("s_abs")
        s_exp = sem("s_exp")
        s_ln = sem("s_ln")
        s_rel = sem("s_rel")
        s_rem = sem("s_rem")
        s_dt = sem("s_dt")
        s_C = sem("s_C")
        s_cs = sem("s_cs")
        s_cT = sem("s_cT")
        s_ct3 = sem("s_ct3")
        b_exp = sem("b_exp")
        b_cb = sem("b_cb")
        b_csb = sem("b_csb")
        b_scan = sem("b_scan")
        b_pd = sem("b_pd")
        b_pp = sem("b_pp")
        b_sum = sem("b_sum")
        c_yd = sem("c_yd")
        c_yg = sem("c_yg")
        c_o = sem("c_o")
        c_x2 = sem("c_x2")
        c_ve = sem("c_ve")
        c_rstd = sem("c_rstd")
        c_xn = sem("c_xn")
        c_xm = sem("c_xm")
        c_h2 = sem("c_h2")
        c_tr = sem("c_tr")
        c_h2T = sem("c_h2T")
        c_lg = sem("c_lg")
        c_dl = sem("c_dl")
        c_el = sem("c_el")
        c_oh = sem("c_oh")
        c_rk = sem("c_rk")
        c_rt = sem("c_rt")
        c_sc = [sem(f"c_sc{i}") for i in range(2)]


        PAIRS = NEXP // 2
        PT = 2 * CAP // P
        WRING = 4
        w1s = wbuf[:, :, 0:DFF]
        w2s = wbuf[:, :, DFF:2 * DFF].rearrange("p w (f e) -> p w f e", f=FC)
        rows = av[:, :, :, :].rearrange("p a b c -> p (a b c)")[:, 0:2 * PT * E].rearrange("p (a i e) -> p a i e", a=2, e=E)
        rowsT = kv[:, :, :].rearrange("p a b -> p (a b)")[:, 0:4 * CAP].rearrange("p (a t) -> p a t", a=2)
        hid = pv[:, :, :].rearrange("p a b -> p (a b)")[:, 0:2 * FC * CAP].rearrange("p (a f t) -> p a f t", a=2, f=FC)
        eo = csb[:, :, :].rearrange("p a b -> p (a b)")[:, 0:2 * 3 * E].rearrange("p (a c e) -> p a c e", a=2, e=E)
        gx = xn
        GR = 8
        x_w = [sem(f"x_w{i}") for i in range(WRING)]
        x_rows = [sem(f"x_rows{i}") for i in range(2)]
        x_T = sem("x_T")
        x_Tc = sem("x_Tc")
        x_f1 = sem("x_f1")
        x_gelu = sem("x_gelu")
        x_f2 = sem("x_f2")
        x_oc = sem("x_oc")
        x_st = [sem(f"x_st{i}") for i in range(2)]
        x_g = [sem(f"x_g{i}") for i in range(GR)]
        x_fm = sem("x_fm")
        x_fa = sem("x_fa")
        x_out = sem("x_out")

        def load_w(sp, e):
            if e >= WRING:
                sp.wait_ge(x_f2, e - WRING + 1)
            sp.dma_start(w1s[:, e % WRING, :], w1[e]).then_inc(x_w[e % WRING], 16)
            sp.dma_start(w2s[:, e % WRING, :, :], w2[e].rearrange("(f p) d -> p f d", p=P)).then_inc(x_w[e % WRING], 16)

        def load_rows(sp, q):
            if q >= 2:
                sp.wait_ge(x_T, q - 1)
            sp.dma_start(rows[:, q % 2, :, :], disp[q * 2 * CAP:(q + 1) * 2 * CAP, :].rearrange("(i p) e -> p i e", p=P)
                         ).then_inc(x_rows[q % 2], 16)

        def store_rows(sp, e):
            sp.wait_ge(x_oc, e + 1)
            r = eout[e * CAP:(e + 1) * CAP, :]
            sp.dma_start(r[0:2 * P, :].rearrange("(c p) e -> p c e", p=P), eo[:, e % 2, 0:2, :]).then_inc(x_st[e % 2], 16)
            sp.dma_start(r[2 * P:CAP, :], eo[0:CAP - 2 * P, e % 2, 2, :]).then_inc(x_st[e % 2], 16)

        def experts_sync(sp):
            sp.wait_ge(s_dt, GROUPS)
            for e in range(WRING):
                load_w(sp, e)
            for k in range(2):
                sp.wait_ge(c_sc[k], 16 * TILES // 2)
            load_rows(sp, 0)
            load_rows(sp, 1)
            for e in range(NEXP):
                store_rows(sp, e)
                if e + WRING < NEXP:
                    load_w(sp, e + WRING)
                if e % 2 == 0 and e // 2 + 2 < PAIRS:
                    load_rows(sp, e // 2 + 2)
            for g in range(BATCH):
                sp.wait_ge(x_fa, 4 * (g + 1))
                sp.dma_start(out[g].rearrange("(i p) e -> p i e", p=P), x2[:, 4 * g:4 * g + 4, :]).then_inc(x_out, 16)
            sp.wait_ge(x_out, 16 * BATCH)

        def experts_scalar(act):
            for e in range(NEXP):
                for h in range(2):
                    act.wait_ge(x_f1, 2 * e + h + 1)
                    if e >= 2:
                        act.wait_ge(x_f2, e - 1)
                    act.activation(hid[:, e % 2, 2 * h:2 * h + 2, :],
                                   cb[h][:, :].rearrange("p (f t) -> p f t", f=2)[:, :, 0:CAP],
                                   ACT.Gelu_apprx_tanh).then_inc(x_gelu, 1)

        def experts_vector(dve):
            def turn(q):
                dve.wait_ge(x_T, q + 1)
                if q >= 2:
                    dve.wait_ge(x_f1, 4 * (q - 1))
                dve.tensor_copy(rowsT[:, q % 2, :], mp[:, 0:2 * CAP]).then_inc(x_Tc, 1)

            turn(0)
            for e in range(NEXP):
                if e % 2 == 0 and e // 2 + 1 < PAIRS:
                    turn(e // 2 + 1)
                dve.wait_ge(x_f2, e + 1)
                if e >= 2:
                    dve.wait_ge(x_st[e % 2], 32 * (e // 2))
                o = yp[:, (e % 2) * 512:(e % 2) * 512 + 3 * E].rearrange("p (c e) -> p c e", e=E)
                dve.tensor_copy(eo[:, e % 2, 0:2, :], o[:, 0:2, :])
                dve.tensor_copy(eo[0:CAP - 2 * P, e % 2, 2, :], o[0:CAP - 2 * P, 2, :]).then_inc(x_oc, 1)
            for i in range(TILES):
                dve.wait_ge(x_g[i % GR], 16 * (i // GR + 1))
                dve.scalar_tensor_tensor(gx[:, i % GR, :], gx[:, i % GR, :], wtok[:, i:i + 1],
                                         modb[:, i // 4, 3, :], ALU.mult, ALU.mult).then_inc(x_fm, 1)
                dve.wait_ge(x_fm, i + 1)
                dve.tensor_tensor(x2[:, i, :], x2[:, i, :], gx[:, i % GR, :], ALU.add).then_inc(x_fa, 1)

        def experts_gpsimd(pool):
            for k in range(2):
                pool.wait_ge(x_st[k], 32 * (NEXP // 2))
            for i in range(TILES):
                if i >= GR:
                    pool.wait_ge(x_fa, i - GR + 1)
                pool.indirect_dma_start(gx[:, i % GR, :], None, eout,
                                        bass.IndirectOffsetOnAxis(ap=gidx[:, i:i + 1], axis=0)).then_inc(x_g[i % GR], 16)

        def experts_tensor(pe):
            def turn(q):
                pe.wait_ge(x_rows[q % 2], 16 * (q // 2 + 1))
                if q:
                    pe.wait_ge(x_Tc, q)
                for i in range(PT):
                    last = pe.transpose(mp[:, i * P:(i + 1) * P], rows[:, q % 2, i, :], ident[:, :])
                last.then_inc(x_T, 1)

            def up(e):
                q = e // 2
                if e % 2 == 0:
                    pe.wait_ge(x_Tc, q + 1)
                pe.wait_ge(x_w[e % WRING], 32 * (e // WRING + 1))
                for h in range(2):
                    if e:
                        pe.wait_ge(x_gelu, 2 * (e - 1) + h + 1)
                    for f in (2 * h, 2 * h + 1):
                        last = pe.matmul(cb[h][:, (f % 2) * 512:(f % 2) * 512 + CAP], w1s[:, e % WRING, f * P:(f + 1) * P],
                                         rowsT[:, q % 2, (e % 2) * CAP:(e % 2 + 1) * CAP], start=True, stop=True)
                    last.then_inc(x_f1, 1)

            def down(e):
                pe.wait_ge(x_gelu, 2 * e + 2)
                if e >= 2:
                    pe.wait_ge(x_oc, e - 1)
                for c in range(3):
                    n = min(P, CAP - c * P)
                    for f in range(FC):
                        last = pe.matmul(yp[0:n, (e % 2) * 512 + c * E:(e % 2) * 512 + (c + 1) * E],
                                         hid[:, e % 2, f, c * P:c * P + n], w2s[:, e % WRING, f, :],
                                         start=(f == 0), stop=(f == FC - 1))
                last.then_inc(x_f2, 1)

            pe.wait_ge(c_rt, GROUPS)
            turn(0)
            up(0)
            for e in range(NEXP):
                if e % 2 == 0 and e // 2 + 1 < PAIRS:
                    turn(e // 2 + 1)
                if e + 1 < NEXP:
                    up(e + 1)
                down(e)

        block = ctx.enter_context(nc.Block())
        loads_sp = [
            (wz[:, :], w_zT), (wp[:, :], w_params[0:RANK, :]), (wdt[:, :], w_dtT),
            (wct[:, :], w_paramsT[:, RANK + NST:RANK + 2 * NST]),
            (wc[:, :], w_params[RANK + NST:RANK + 2 * NST, :]),
            (cw[:, :], conv_w.rearrange("e a k -> e (a k)")),
            (bdt[:, :], b_dt.rearrange("(e a) -> e a", a=1)),
            (dsk[:, :], d_skip.rearrange("(e a) -> e a", a=1)),
            (wo[:, :], w_outT), (gw[:, :], gate_wT),
        ]
        loads_act = [
            (ct[:, :], cT), (wm[:, :], wmod), (ident[:, :], ident_in), (al[:, :], a_log),
            (alT[:, :], a_logT), (sel[:, :, :], sel_in), (tri[:, :], tri_in),
            (identb[:, :], None), (em16[:, :], em16_in), (toki[:, :], tok_in),
        ]
        NW = 16 * (len(loads_sp) + len(loads_act) - 1)

        @block.sync
        def _(sp):
            def load_x(g):
                sp.dma_start(xs[:, g * GTILES:(g + 1) * GTILES, :],
                             x[GB * g:GB * (g + 1)].rearrange("b (i p) e -> p (b i) e", p=P)).then_inc(s_x[g], 16)
            load_x(0)
            for dst, src in loads_sp:
                sp.dma_start(dst, src).then_inc(s_w, 16)
            for g in range(1, GROUPS):
                load_x(g)
            sp.wait_ge(s_zero, 1)
            sp.dma_start(disp[0:SLOTS, :].rearrange("(r p a) e -> p r (a e)", p=P, a=8),
                         zero[:, :].rearrange("p (r n) -> p r n", r=1).broadcast_to([P, SLOTS // (8 * P), 1024])
                         ).then_inc(s_zf, 16)
            experts_sync(sp)

        @block.scalar
        def _(act):
            for dst, src in loads_act:
                if src is not None:
                    act.dma_start(dst, src).then_inc(s_w, 16)
            act.wait_ge(s_w, NW)
            act.activation(cth[:, :], ct[:, :], ACT.Tanh, scale=0.5).then_inc(s_cth, 1)
            act.activation(aneg[:, :], al[:, :], ACT.Exp).then_inc(s_aexp, 1)
            act.activation(amskT[:, :], alT[:, :], ACT.Exp).then_inc(s_aexp, 1)

            def a_hT(g):
                act.wait_ge(s_xT, g + 1)
                act.wait_ge(s_pro, 2)
                if g:
                    act.wait_ge(s_C, g)
                for j in range(GB):
                    b = GB * g + j
                    last = act.activation(hT[:, j, HPAD:], mp[:, j * SEQ:(j + 1) * SEQ], ACT.Identity,
                                          scale=modT[:, 1, b:b + 1], bias=modT[:, 0, b:b + 1])
                last.then_inc(s_hT, 1)

            def a_thz(g):
                act.wait_ge(s_z, g + 1)
                if g:
                    act.wait_ge(s_dt, g)
                act.activation(th[:, :, :], mp[:, :].rearrange("p (b t) -> p b t", b=GB), ACT.Tanh,
                               scale=0.5).then_inc(s_thz, 1)

            def a_thu(g):
                act.wait_ge(s_cv, g + 1)
                act.wait_ge(s_gate, g + 1)
                act.activation(th[:, :, :], mp[:, :].rearrange("p (b t) -> p b t", b=GB), ACT.Tanh,
                               scale=0.5).then_inc(s_thu, 1)

            def a_soft(g):
                act.wait_ge(s_xdt, g + 1)
                if g:
                    act.wait_ge(s_dt, g)
                act.activation(expx[:, :, :], mp[:, :].rearrange("p (b t) -> p b t", b=GB), ACT.Abs,
                               bias=bdt[:, 0:1]).then_inc(s_abs, 1)
                act.wait_ge(s_abs, g + 1)
                act.activation(expx[:, :, :], expx[:, :, :], ACT.Exp, scale=-1.0).then_inc(s_exp, 1)

            def a_ln(g):
                act.wait_ge(s_exp, g + 1)
                act.activation(lnx[:, :, :], expx[:, :, :], ACT.Ln, bias=1.0).then_inc(s_ln, 1)

            def a_ct3(g):
                act.wait_ge(s_cT, g + 1)
                act.activation(ct3[:, g * GT:(g + 1) * GT], mp[0:NPART * NST, 0:GT // 2].bitcast(BF16),
                               ACT.Copy).then_inc(s_ct3, 1)

            def b_step(m):
                g, n = divmod(m, NST)
                if n == 0:
                    act.wait_ge(s_dt, g + 1)
                if m >= RING_A:
                    act.wait_ge(b_scan, m - RING_A + 1)
                act.activation(av[:, m % RING_A, :, 1:SEQ1], dtb[:, g % 2, :, 0:SEQ], ACT.Exp,
                               scale=aneg[:, n:n + 1]).then_inc(b_exp, 1)

            def b_copy(m):
                if on_pool(m):
                    k = pool_before(m)
                    act.wait_ge(b_cb, m + 1)
                    if k >= 2:
                        act.wait_ge(b_pp, k - 1)
                    act.activation(csb[:, k % 2, :], cb[m % 2][:, :], ACT.Copy).then_inc(b_csb, 1)

            def c_h2Tcopy(g):
                act.wait_ge(c_tr, g + 1)
                if g:
                    act.wait_ge(c_lg, g)
                act.activation(h2T[:, :], mp[:, :], ACT.Copy).then_inc(c_h2T, 1)

            def c_expl(g):
                act.wait_ge(c_dl, g + 1)
                act.activation(el[:, :, :], dl[:, :, :], ACT.Exp).then_inc(c_el, 1)

            a_hT(0)
            a_thz(0)
            a_thu(0)
            a_soft(0)
            a_ln(0)
            a_ct3(0)
            for b in range(BATCH):
                act.wait_ge(s_modp, b + 1)
                act.activation(modb[:, b, :, :], cb[b // 2 % 2][:, (b % 2) * 512:(b % 2) * 512 + 512]
                               .rearrange("p (a e) -> p a e", a=4), ACT.Copy).then_inc(s_modb, 1)
            for m in range(STEPS + 2):
                g, n = divmod(m, NST)
                if m < STEPS:
                    b_step(m)
                if 1 <= m <= STEPS:
                    b_copy(m - 1)
                if g and n == 5:
                    c_h2Tcopy(g - 1)
                if g and n == 7:
                    c_expl(g - 1)
                if g + 1 < GROUPS:
                    if n == 9:
                        a_hT(g + 1)
                    if n == 10:
                        a_thz(g + 1)
                    if n == 11:
                        a_thu(g + 1)
                    if n == 13:
                        a_soft(g + 1)
                        a_ln(g + 1)
                    if n == 15:
                        a_ct3(g + 1)
            c_h2Tcopy(GROUPS - 1)
            c_expl(GROUPS - 1)
            experts_scalar(act)

        @block.gpsimd
        def _(pool):
            pool.memset(zero[:, :], 0.0).then_inc(s_zero, 1)
            pool.memset(halfneg[:, :], -0.5).then_inc(s_pc, 1)
            pool.memset(ones[:, :], 1.0).then_inc(s_pc, 1)
            pool.memset(hT[:, :, 0:HPAD], 0.0).then_inc(s_pc, 1)
            pool.memset(av[:, :, :, 0:1], 0.0).then_inc(s_pc, 1)
            pool.memset(du[:, :, :], 0.0).then_inc(s_pc, 1)
            pool.memset(seen[:, :], 0.0).then_inc(s_pc, 1)
            pool.memset(seenb[:, :], 0.0).then_inc(s_pc, 1)
            pool.wait_ge(s_w, NW)
            pool.tensor_copy(identb[:, :], ident[:, :]).then_inc(s_pc, 1)
            pool.wait_ge(s_pc, 8)

            def a_rstd(g):
                pool.wait_ge(s_ve, g + 1)
                if g:
                    pool.wait_ge(s_xn, g)
                pool.tensor_tensor(rstd[:, :], ve[:, :], halfneg[:, :], ALU.pow).then_inc(s_rstd, 1)

            def a_du(g):
                pool.wait_ge(s_u, g + 1)
                if g >= 2:
                    pool.wait_ge(b_scan, (g - 1) * NST)
                d = du[:, g % 2, :].rearrange("p (b t) -> p b t", b=GB)
                pool.tensor_copy(d[:, :, 1:2], ub[:, :, 0:1]).then_inc(s_du, 1)
                pool.tensor_tensor(d[:, :, 2:SEQ1], ub[:, :, 1:SEQ], ub[:, :, 0:SEQ - 1],
                                   ALU.subtract).then_inc(s_du, 1)

            def a_rem(g):
                pool.wait_ge(s_exp, g + 1)
                if g:
                    pool.wait_ge(s_dt, g)
                pool.tensor_scalar(rem[:, :, :], expx[:, :, :], 1.0, -1.0, ALU.add, ALU.add).then_inc(s_rem, 1)
                pool.wait_ge(s_rem, 2 * g + 1)
                pool.tensor_tensor(rem[:, :, :], expx[:, :, :], rem[:, :, :], ALU.subtract).then_inc(s_rem, 1)

            def b_mult(m):
                if on_pool(m):
                    k = pool_before(m)
                    pool.wait_ge(b_csb, k + 1)
                    pool.wait_ge(b_scan, m + 1)
                    if m >= RING_P:
                        pool.wait_ge(b_sum, m - RING_P + 1)
                    pool.tensor_tensor(pv[:, m % RING_P, :].rearrange("p (b t) -> p b t", b=GB),
                                       kv[:, m % RING_K, :].rearrange("p (b t) -> p b t", b=GB)[:, :, 1:SEQ1],
                                       csb[:, k % 2, :].rearrange("p (b t) -> p b t", b=GB),
                                       ALU.mult).then_inc(b_pp, 1)

            def c_yg_(g):
                pool.wait_ge(c_yd, g + 1)
                if g:
                    pool.wait_ge(c_o, g)
                pool.tensor_tensor(yg[:, :], yd[:, :], gate[:, g % 2, :], ALU.mult).then_inc(c_yg, 1)

            def c_rstd_(g):
                pool.wait_ge(c_ve, g + 1)
                if g:
                    pool.wait_ge(c_xn, g)
                pool.tensor_tensor(rstdc[:, :], vec[:, :], halfneg[:, :], ALU.pow).then_inc(c_rstd, 1)

            def c_mod(g):
                pool.wait_ge(c_xn, g + 1)
                pool.wait_ge(s_modg, 1)
                if g:
                    pool.wait_ge(c_h2, g)
                for j in range(GB):
                    s = slice(j * 4, j * 4 + 4)
                    last = pool.tensor_tensor(xn2[:, s, :], xn2[:, s, :],
                                              modb[:, GB * g + j, 2:3, :].broadcast_to([P, 4, P]), ALU.mult)
                last.then_inc(c_xm, 1)
                pool.wait_ge(c_xm, g + 1)
                if g >= 2:
                    pool.wait_ge(c_sc[g % 2], 16 * GTILES * (g // 2))
                for j in range(GB):
                    s = slice(j * 4, j * 4 + 4)
                    last = pool.tensor_tensor(h2[:, g % 2, s, :], xn2[:, s, :],
                                              modb[:, GB * g + j, 1:2, :].broadcast_to([P, 4, P]), ALU.add)
                last.then_inc(c_h2, 1)

            def c_scatter(g):
                pool.wait_ge(c_rt, g + 1)
                if g == 0:
                    pool.wait_ge(s_zf, 16)
                for j in range(GTILES):
                    i = g * GTILES + j
                    pool.indirect_dma_start(disp, bass.IndirectOffsetOnAxis(ap=sidx[:, i:i + 1], axis=0),
                                            h2[:, g % 2, j, :], None).then_inc(c_sc[g % 2], 16)

            a_rstd(0)
            a_du(0)
            a_rem(0)
            for m in range(STEPS + 2):
                g, n = divmod(m, NST)
                if m >= 1 and m <= STEPS:
                    b_mult(m - 1)
                if g and n == 2:
                    c_yg_(g - 1)
                if g and n == 4:
                    c_rstd_(g - 1)
                    c_mod(g - 1)
                if g and n == 9:
                    c_scatter(g - 1)
                if g + 1 < GROUPS:
                    if n == 7:
                        a_rstd(g + 1)
                    if n == 12:
                        a_du(g + 1)
                    if n == 14:
                        a_rem(g + 1)
            g = GROUPS - 1
            c_yg_(g)
            c_rstd_(g)
            c_mod(g)
            c_scatter(g)
            experts_gpsimd(pool)

        @block.vector
        def _(dve):
            chain = [0]

            def link(ins):
                chain[0] += 1
                ins.then_inc(vch, 1)
                dve.wait_ge(vch, chain[0])

            def a_stats(g):
                dve.wait_ge(s_x[g], 16)
                if g:
                    dve.wait_ge(s_rstd, g)
                    dve.wait_ge(s_xn, g)
                for j in range(GTILES):
                    last = dve.bn_stats(st6[:, j, :], xs[:, g * GTILES + j, :])
                link(last)
                for j in range(GTILES):
                    last = dve.bn_aggr(mv[:, j, :], st6[:, j, :])
                link(last)
                dve.tensor_scalar(ve[:, :], mv[:, :, 1], EPS, None, ALU.add).then_inc(s_ve, 1)

            def a_xn(g):
                dve.wait_ge(s_rstd, g + 1)
                if g:
                    dve.wait_ge(s_xT, g)
                for j in range(GTILES):
                    last = dve.tensor_scalar(xn[:, j, :], xs[:, g * GTILES + j, :], mv[:, j, 0:1],
                                             rstd[:, j:j + 1], ALU.subtract, ALU.mult)
                last.then_inc(s_xn, 1)

            def a_gate(g):
                dve.wait_ge(s_thz, g + 1)
                if g >= 2:
                    dve.wait_ge(c_yg, g - 1)
                dve.scalar_tensor_tensor(gate[:, g % 2, :], th[:, :, :].rearrange("p b t -> p (b t)"), 1.0,
                                         mp[:, :], ALU.add, ALU.mult).then_inc(s_gate, 1)

            def a_u(g):
                dve.wait_ge(s_thu, g + 1)
                if g:
                    dve.wait_ge(s_du, 2 * g)
                    dve.wait_ge(s_base, g)
                link(dve.scalar_tensor_tensor(ub[:, :, 1:SEQ1], th[:, :, :], 1.0,
                                              mp[:, :].rearrange("p (b t) -> p b t", b=GB), ALU.add, ALU.mult))
                dve.tensor_copy(ub[:, :, 0:1], ub[:, :, 1:2]).then_inc(s_u, 1)

            def a_base(g):
                dve.wait_ge(s_G, g + 1)
                dve.wait_ge(s_u, g + 1)
                if g >= 2:
                    dve.wait_ge(c_yd, g - 1)
                dve.tensor_tensor(base[:, g % 2, :, :], mp[:, :].rearrange("p (b t) -> p b t", b=GB),
                                  ub[:, :, 0:SEQ], ALU.mult).then_inc(s_Gr, 1)
                dve.wait_ge(s_Gr, g + 1)
                dve.scalar_tensor_tensor(base[:, g % 2, :, :], ub[:, :, 1:SEQ1], negd[:, 0:1],
                                         base[:, g % 2, :, :], ALU.mult, ALU.add).then_inc(s_base, 1)

            def a_rel(g):
                dve.wait_ge(s_xdt, g + 1)
                dve.wait_ge(s_abs, g + 1)
                dve.tensor_scalar(relx[:, :, :], mp[:, :].rearrange("p (b t) -> p b t", b=GB), bdt[:, 0:1],
                                  0.0, ALU.add, ALU.max).then_inc(s_rel, 1)

            def a_dt(g):
                dve.wait_ge(s_ln, g + 1)
                dve.wait_ge(s_rem, 2 * g + 2)
                dve.wait_ge(s_rel, g + 1)
                if g >= 2:
                    dve.wait_ge(b_exp, (g - 1) * NST)
                link(dve.tensor_tensor(rem[:, :, :], rem[:, :, :], lnx[:, :, :], ALU.add))
                link(dve.tensor_tensor(dtb[:, g % 2, :, 1:SEQ1], rem[:, :, :], relx[:, :, :], ALU.add))
                dve.tensor_copy(dtb[:, g % 2, :, 0:1], dtb[:, g % 2, :, 1:2]).then_inc(s_dt, 1)

            def a_split(g):
                dve.wait_ge(s_C, g + 1)
                if g:
                    dve.wait_ge(s_cT, g)
                c = mp[:, 0:GTILES * NST].rearrange("p (i n) -> p i n", n=NST)
                link(dve.tensor_copy(cs[:, :, 0, :], c))
                link(dve.tensor_tensor(cr[:, :, :], c, cs[:, :, 0, :], ALU.subtract))
                link(dve.tensor_copy(cs[:, :, 1, :], cr[:, :, :]))
                dve.tensor_tensor(cs[:, :, 2, :], cr[:, :, :], cs[:, :, 1, :], ALU.subtract).then_inc(s_cs, 1)

            def b_scan_(m):
                g, n = divmod(m, NST)
                dve.wait_ge(b_exp, m + 1)
                if n == 0:
                    dve.wait_ge(s_du, 2 * g + 2)
                if m >= RING_K:
                    k = m - RING_K
                    if on_pool(k):
                        dve.wait_ge(b_pp, pool_before(k) + 1)
                    else:
                        dve.wait_ge(b_pd, dve_before(k) + 1)
                dve.tensor_tensor_scan(kv[:, m % RING_K, :], du[:, g % 2, :],
                                       av[:, m % RING_A, :, :].rearrange("p b t -> p (b t)"), 0.0,
                                       ALU.add, ALU.mult).then_inc(b_scan, 1)

            def b_mult(m):
                if on_pool(m):
                    return
                dve.wait_ge(b_cb, m + 1)
                dve.wait_ge(b_scan, m + 1)
                if m >= RING_P:
                    dve.wait_ge(b_sum, m - RING_P + 1)
                dve.tensor_tensor(pv[:, m % RING_P, :].rearrange("p (b t) -> p b t", b=GB),
                                  kv[:, m % RING_K, :].rearrange("p (b t) -> p b t", b=GB)[:, :, 1:SEQ1],
                                  cb[m % 2][:, :].rearrange("p (b t) -> p b t", b=GB), ALU.mult).then_inc(b_pd, 1)

            def c_yd_(g):
                dve.wait_ge(b_sum, NST * (g + 1))
                if g == 0:
                    dve.wait_ge(s_zf, 16)
                if g:
                    dve.wait_ge(c_yg, g)
                    dve.wait_ge(c_lg, g)
                dve.tensor_tensor(yd[:, :], yp[:, :], base[:, g % 2, :, :].rearrange("p b t -> p (b t)"),
                                  ALU.subtract).then_inc(c_yd, 1)

            def c_norm(g):
                dve.wait_ge(c_o, g + 1)
                t = slice(g * GTILES, (g + 1) * GTILES)
                dve.tensor_tensor(x2[:, t, :], mp[:, :].rearrange("p (i e) -> p i e", e=E), xs[:, t, :],
                                  ALU.add).then_inc(c_x2, 1)
                dve.wait_ge(c_x2, g + 1)
                if g:
                    dve.wait_ge(c_xn, g)
                for j in range(GTILES):
                    last = dve.bn_stats(st6c[:, j, :], x2[:, g * GTILES + j, :])
                link(last)
                for j in range(GTILES):
                    last = dve.bn_aggr(mvc[:, j, :], st6c[:, j, :])
                link(last)
                dve.tensor_scalar(vec[:, :], mvc[:, :, 1], EPS, None, ALU.add).then_inc(c_ve, 1)

            def c_xn_(g):
                dve.wait_ge(c_rstd, g + 1)
                if g:
                    dve.wait_ge(c_xm, g)
                for j in range(GTILES):
                    last = dve.tensor_scalar(xn2[:, j, :], x2[:, g * GTILES + j, :], mvc[:, j, 0:1],
                                             rstdc[:, j:j + 1], ALU.subtract, ALU.mult)
                last.then_inc(c_xn, 1)

            def c_router(g):
                dve.wait_ge(c_lg, g + 1)
                if g:
                    dve.wait_ge(c_rt, g)
                    dve.wait_ge(c_rk, g)
                lg = mp[:, 0:GTILES * NEXP].rearrange("p (i n) -> p i n", n=NEXP)
                wide = [P, GTILES, NEXP]
                link(dve.tensor_reduce(mx[:, :], lg, AX.X, ALU.max))
                mxb = mx[:, :].rearrange("p (i a) -> p i a", a=1).broadcast_to(wide)
                link(dve.tensor_tensor(dl[:, :, :], lg, mxb, ALU.subtract))
                dve.tensor_scalar(eq[:, :, :], dl[:, :, :], 0.0, None, ALU.is_ge).then_inc(c_dl, 1)
                dve.wait_ge(c_dl, g + 1)
                emb = em16[:, :].rearrange("p (a n) -> p a n", a=1).broadcast_to(wide)
                link(dve.tensor_tensor(cand[:, :, :], eq[:, :, :], emb, ALU.mult))
                link(dve.tensor_reduce(first[:, :], cand[:, :, :], AX.X, ALU.min))
                fb = first[:, :].rearrange("p (i a) -> p i a", a=1).broadcast_to(wide)
                dve.tensor_tensor(oh[:, :, :], emb, fb, ALU.is_equal).then_inc(c_oh, 1)
                dve.wait_ge(c_el, g + 1)
                link(dve.tensor_reduce(es[:, :], el[:, :, :], AX.X, ALU.add))
                link(dve.reciprocal(prob[:, :], es[:, :]))

            def c_slots(g):
                wide = [P, GTILES, NEXP]
                t = slice(g * GTILES, (g + 1) * GTILES)
                dve.wait_ge(c_rk, g + 1)
                rk = mp[:, 512:512 + GTILES * NEXP].rearrange("p (i n) -> p i n", n=NEXP)
                link(dve.tensor_tensor(rsel[:, :, :], rk, oh[:, :, :], ALU.mult))
                link(dve.tensor_reduce(rank[:, :], rsel[:, :, :], AX.X, ALU.add))
                link(dve.tensor_scalar(keep[:, :], rank[:, :], float(CAP), None, ALU.is_lt))
                link(dve.tensor_scalar(slot[:, :], first[:, :], float(CAP), float(NEXP * CAP), ALU.mult, ALU.add))
                link(dve.tensor_tensor(slot2[:, :], slot[:, :], rank[:, :], ALU.add))
                link(dve.tensor_tensor(idf[:, :], slot2[:, :], toki[:, t], ALU.subtract))
                link(dve.tensor_tensor(idf2[:, :], idf[:, :], keep[:, :], ALU.mult))
                link(dve.tensor_tensor(sidx[:, t], idf2[:, :], toki[:, t], ALU.add))
                link(dve.tensor_tensor(gidx[:, t], slot2[:, :], keep[:, :], ALU.mult))
                link(dve.tensor_tensor(wtok[:, t], prob[:, :], keep[:, :], ALU.mult))
                link(dve.tensor_reduce(gsum[:, :], oh[:, :, :].rearrange("p i n -> p n i"), AX.X, ALU.add))
                link(dve.tensor_tensor(seen[:, :], seen[:, :], gsum[:, :], ALU.add))
                dve.tensor_copy(seenb[:, :], seen[:, :]).then_inc(c_rt, 1)

            a_stats(0)
            dve.wait_ge(s_w, NW)
            dve.wait_ge(s_cth, 1)
            dve.wait_ge(s_pc, 8)
            link(dve.scalar_tensor_tensor(silc[:, :], cth[:, :], 1.0, ct[:, :], ALU.add, ALU.mult))
            dve.tensor_scalar(silc[:, :], silc[:, :], 0.5, None, ALU.mult).then_inc(s_silc, 1)
            a_xn(0)
            dve.wait_ge(s_silc, 1)
            dve.tensor_copy(silb, silc[:, :].rearrange("p (b a) -> p b a", a=1).broadcast_to([P, BATCH, P])
                            ).then_inc(s_silb, 1)
            dve.wait_ge(s_mm0, 1)
            dve.tensor_copy(modT[:, 0, :], yp[:, 0:BATCH]).then_inc(s_pro, 1)
            dve.tensor_scalar(modT[:, 1, :], yp[:, BATCH:2 * BATCH], 1.0, None, ALU.add).then_inc(s_pro, 1)
            dve.tensor_tensor(dconv[:, :, :], ident[:, :].rearrange("p (a c) -> p a c", a=1).broadcast_to([P, KCONV, P]),
                              cw[:, :].rearrange("p (k a) -> p k a", a=1).broadcast_to([P, KCONV, P]),
                              ALU.mult).then_inc(s_dc, 1)
            dve.tensor_scalar(negd[:, :], dsk[:, :], -1.0, None, ALU.mult).then_inc(s_dc, 1)
            dve.wait_ge(s_aexp, 2)
            for a, msk, inv in ((aneg, amsk, ainv), (amskT, amskT, ainvT)):
                link(dve.tensor_scalar(inv[:, :], a[:, :], -1.0, 1e-10, ALU.mult, ALU.add))
                link(dve.reciprocal(inv[:, :], inv[:, :]))
                link(dve.tensor_scalar(msk[:, :], a[:, :], SMALL_A, None, ALU.is_ge))
                link(dve.tensor_tensor(inv[:, :], inv[:, :], msk[:, :], ALU.mult))
            dve.tensor_scalar(aneg[:, :], aneg[:, :], -1.0, None, ALU.mult).then_inc(s_ainv, 1)
            dve.wait_ge(s_mm0, 2)
            dve.tensor_copy(wdtp[:, :], yp[:, 512:512 + P]).then_inc(s_pro, 1)
            dve.wait_ge(s_mm0, 3)
            dve.tensor_copy(wgt[:, :], yp[:, P:2 * P]).then_inc(s_pro, 1)
            a_gate(0)
            a_u(0)
            a_base(0)
            a_rel(0)
            a_dt(0)
            a_split(0)
            dve.tensor_tensor(diag[:, :, :], ident[:, :].rearrange("p (a c) -> p a c", a=1).broadcast_to([P, NST, P]),
                              ainv[:, :].rearrange("p (k a) -> p k a", a=1).broadcast_to([P, NST, P]),
                              ALU.mult).then_inc(s_dc, 1)
            dve.wait_ge(s_w, NW)
            dve.wait_ge(s_modb, BATCH)
            for j in (0, 3):
                gv = modb[:, :, j, :]
                link(dve.scalar_tensor_tensor(gabs[:, :, :], gv, -1.0, gv, ALU.mult, ALU.max))
                link(dve.tensor_scalar(gabs[:, :, :], gabs[:, :, :], 0.25, None, ALU.max))
                link(dve.tensor_scalar(gsgn[:, :, :], gv, 0.0, 2.0, ALU.is_ge, ALU.mult))
                link(dve.scalar_tensor_tensor(gv, gsgn[:, :, :], 1.0, gabs[:, :, :], ALU.subtract, ALU.mult))
            link(dve.tensor_scalar(modb[:, :, 2, :], modb[:, :, 2, :], 1.0, None, ALU.add))
            link(dve.tensor_scalar(wo[:, :], wo[:, :], 0.25, None, ALU.mult))
            dve.tensor_tensor(woga[:, :, :], wo[:, :].rearrange("p (a c) -> p a c", a=1).broadcast_to([P, BATCH, P]),
                              modb[:, :, 0, :], ALU.mult).then_inc(s_modg, 1)

            for m in range(STEPS + 2):
                g, n = divmod(m, NST)
                if m < STEPS:
                    b_scan_(m)
                if 1 <= m <= STEPS:
                    b_mult(m - 1)
                if g and n == 1:
                    c_yd_(g - 1)
                if g and n == 3:
                    c_norm(g - 1)
                if g and n == 4:
                    c_xn_(g - 1)
                if g and n == 6:
                    c_router(g - 1)
                if g and n == 8:
                    c_slots(g - 1)
                if g + 1 < GROUPS:
                    if n == 6:
                        a_stats(g + 1)
                    if n == 8:
                        a_xn(g + 1)
                    if n == 10:
                        a_gate(g + 1)
                    if n == 11:
                        a_u(g + 1)
                    if n == 12:
                        a_base(g + 1)
                    if n == 13:
                        a_rel(g + 1)
                    if n == 14:
                        a_split(g + 1)
                        a_dt(g + 1)
            g = GROUPS - 1
            c_norm(g)
            c_xn_(g)
            c_router(g)
            c_slots(g)
            experts_vector(dve)

        @block.tensor
        def _(pe):
            def a_xT(g):
                pe.wait_ge(s_xn, g + 1)
                if g:
                    pe.wait_ge(s_ct3, g)
                if g >= 2:
                    pe.wait_ge(c_rt, g - 1)
                for j in range(GTILES):
                    last = pe.transpose(mp[:, j * P:(j + 1) * P], xn[:, j, :], ident[:, :])
                last.then_inc(s_xT, 1)

            def a_proj(g, w, done, free, value):
                pe.wait_ge(free, value)
                for j in range(GB):
                    last = pe.matmul(mp[:, j * SEQ:(j + 1) * SEQ], w, hT[:, j, HPAD:], start=True, stop=True)
                last.then_inc(done, 1)

            def a_z(g):
                a_proj(g, wz[:, :], s_z, s_hT, g + 1)

            def a_conv(g):
                pe.wait_ge(s_gate, g + 1)
                pe.wait_ge(s_dc, 1)
                for j in range(GB):
                    for k in range(KCONV):
                        last = pe.matmul(mp[:, j * SEQ:(j + 1) * SEQ], dconv[:, k, :], hT[:, j, k:k + SEQ],
                                         start=(k == 0), stop=(k == KCONV - 1))
                last.then_inc(s_cv, 1)

            def a_G(g):
                a_proj(g, wgt[:, :], s_G, s_u, g + 1)

            def a_dtx(g):
                a_proj(g, wdtp[:, :], s_xdt, s_Gr, g + 1)

            def a_C(g):
                pe.wait_ge(s_abs, g + 1)
                pe.wait_ge(s_rel, g + 1)
                for i in range(GTILES):
                    j, t = divmod(i, GTILES // GB)
                    last = pe.matmul(mp[:, i * NST:(i + 1) * NST], hT[:, j, HPAD + t * P:HPAD + (t + 1) * P],
                                     wct[:, :], start=True, stop=True)
                last.then_inc(s_C, 1)

            def a_cT(g):
                pe.wait_ge(s_cs, g + 1)
                v = mp[0:NPART * NST, 0:GT // 2].bitcast(BF16)
                for i in range(GTILES):
                    last = pe.transpose(v[:, i * P:(i + 1) * P],
                                        cs[:, i, :, :].rearrange("p c n -> p (c n)"), identb[:, :])
                last.then_inc(s_cT, 1)

            def b_cb_(m):
                g, n = divmod(m, NST)
                if n == 0:
                    pe.wait_ge(s_ct3, g + 1)
                if m == 0:
                    pe.wait_ge(s_modb, BATCH)
                if m >= 2:
                    k = m - 2
                    if on_pool(k):
                        pe.wait_ge(b_csb, pool_before(k) + 1)
                    else:
                        pe.wait_ge(b_pd, dve_before(k) + 1)
                for j in range(GB):
                    last = pe.matmul(cb[m % 2][:, j * SEQ:(j + 1) * SEQ], sel[:, n, :],
                                     ct3[:, g * GT + j * SEQ:g * GT + (j + 1) * SEQ], start=True, stop=True)
                last.then_inc(b_cb, 1)

            def b_sum_(m):
                g, n = divmod(m, NST)
                if m == 0:
                    pe.wait_ge(s_dc, 3)
                    pe.wait_ge(s_pro, 4)
                if on_pool(m):
                    pe.wait_ge(b_pp, pool_before(m) + 1)
                else:
                    pe.wait_ge(b_pd, dve_before(m) + 1)
                if n == 0 and g:
                    pe.wait_ge(c_yd, g)
                for j in range(GB):
                    last = pe.matmul(yp[:, j * SEQ:(j + 1) * SEQ], diag[:, n, :],
                                     pv[:, m % RING_P, j * SEQ:(j + 1) * SEQ], start=(n == 0), stop=(n == NST - 1))
                last.then_inc(b_sum, 1)

            def c_out(g):
                pe.wait_ge(c_yg, g + 1)
                pe.wait_ge(s_modg, 1)
                pe.wait_ge(s_ct3, min(g + 2, GROUPS))
                for i in range(GTILES):
                    last = pe.matmul(mp[:, i * P:(i + 1) * P], yg[:, i * P:(i + 1) * P],
                                     woga[:, GB * g + i // 4, :], start=True, stop=True)
                last.then_inc(c_o, 1)

            def c_trans(g):
                pe.wait_ge(c_h2, g + 1)
                pe.wait_ge(c_x2, g + 1)
                for i in range(GTILES):
                    last = pe.transpose(mp[:, i * P:(i + 1) * P], h2[:, g % 2, i, :], ident[:, :])
                last.then_inc(c_tr, 1)

            def c_logits(g):
                pe.wait_ge(c_h2T, g + 1)
                for i in range(GTILES):
                    last = pe.matmul(mp[:, i * NEXP:(i + 1) * NEXP], h2T[:, i * P:(i + 1) * P], gw[:, :],
                                     start=True, stop=True)
                last.then_inc(c_lg, 1)

            def c_rank(g):
                pe.wait_ge(c_oh, g + 1)
                if g:
                    pe.wait_ge(c_rt, g)
                o = 512
                wide = GTILES * NEXP
                rk = mp[:, o:o + wide].rearrange("p (i n) -> p i n", n=NEXP)
                pe.matmul(rk, tri[:, :], oh[:, :, :], start=True, stop=False, skip_group_check=True)
                for i in range(GTILES - 1):
                    pe.matmul(rk[:, i + 1:, :], ones[:, :], oh[:, i:i + 1, :].broadcast_to([P, GTILES - 1 - i, NEXP]),
                              start=False, stop=False, skip_group_check=True)
                pe.matmul(rk, ones[:, :], seenb[:, :].rearrange("p (a n) -> p a n", a=1).broadcast_to([P, GTILES, NEXP]),
                          start=False, stop=True, skip_group_check=True).then_inc(c_rk, 1)

            pe.wait_ge(s_w, NW)
            pe.wait_ge(s_pc, 8)
            pe.wait_ge(s_silc, 1)
            pe.matmul(yp[:, 0:BATCH], wm[:, 0:P], silc[:, :], start=True, stop=True)
            pe.matmul(yp[:, BATCH:2 * BATCH], wm[:, P:2 * P], silc[:, :], start=True, stop=True).then_inc(s_mm0, 1)
            a_xT(0)
            pe.matmul(yp[:, 512:512 + P], wp[:, :], wdt[:, :], start=True, stop=True).then_inc(s_mm0, 1)
            pe.wait_ge(s_ainv, 1)
            pe.matmul(yp[:, P:2 * P], wc[:, :], ainvT[:, :], start=True, stop=True).then_inc(s_mm0, 1)
            a_z(0)
            a_conv(0)
            pe.wait_ge(s_pro, 4)
            a_G(0)
            a_dtx(0)
            a_C(0)
            a_cT(0)
            pe.wait_ge(s_silb, 1)
            for b in range(BATCH):
                if b >= 4:
                    pe.wait_ge(s_modb, b - 3)
                pe.matmul(cb[b // 2 % 2][:, (b % 2) * 512:(b % 2) * 512 + 512], silb[:, b, :], wm[:, 2 * P:6 * P],
                          start=True, stop=True).then_inc(s_modp, 1)

            b_cb_(0)
            for m in range(STEPS + 2):
                g, n = divmod(m, NST)
                if m + 1 < STEPS:
                    b_cb_(m + 1)
                if m >= 2:
                    b_sum_(m - 2)
                if g and n == 3:
                    c_out(g - 1)
                if g and n == 5:
                    c_trans(g - 1)
                if g and n == 6:
                    c_logits(g - 1)
                if g and n == 7:
                    c_rank(g - 1)
                if g + 1 < GROUPS:
                    if n == 9:
                        a_xT(g + 1)
                        a_z(g + 1)
                    if n == 10:
                        a_conv(g + 1)
                    if n == 11:
                        a_G(g + 1)
                    if n == 12:
                        a_dtx(g + 1)
                    if n == 13:
                        a_C(g + 1)
                    if n == 14:
                        a_cT(g + 1)
            g = GROUPS - 1
            c_out(g)
            c_trans(g)
            c_logits(g)
            c_rank(g)
            experts_tensor(pe)


def kernel(**inputs):
    import concourse.bacc as bacc
    from concourse.bass_utils import run_bass_kernel_spmd
    import ml_dtypes

    nc = bacc.Bacc("TRN2", target_bir_lowering=False, num_devices=1)
    a = {k: np.asarray(v) for k, v in inputs.items()}
    one = np.arange(NPART * NST)
    i = np.arange(P)
    arrays = {
        "x": a["L0_attn_x"], "w_zT": a["L0_attn_W_z"].T, "w_params": a["L0_attn_W_params"],
        "w_paramsT": a["L0_attn_W_params"].T, "conv_w": a["L0_attn_conv_w"], "w_dtT": a["L0_attn_W_dt"].T,
        "b_dt": a["L0_attn_b_dt"], "a_log": a["L0_attn_A_log"], "a_logT": a["L0_attn_A_log"].T,
        "d_skip": a["L0_attn_D"], "w_outT": a["L0_attn_W_out"].T, "gate_wT": a["L0_ffn_gate_w"].T,
        "w1": a["L0_ffn_w1"], "w2": a["L0_ffn_w2"], "cT": a["L0_c"].T, "wmod": a["L0_wmod"],
        "ident_in": np.eye(P, dtype=np.float32),
        "sel_in": np.ascontiguousarray(np.broadcast_to((one[:, None] % NST == np.arange(NST))[:, :, None],
                                                       (NPART * NST, NST, P))).astype(ml_dtypes.bfloat16),
        "tri_in": (i[:, None] < i[None, :]).astype(ml_dtypes.bfloat16),
        "em16_in": np.broadcast_to(np.arange(NEXP, dtype=np.float32) - NEXP, (P, NEXP)),
        "tok_in": (SLOTS + i[:, None] + P * np.arange(TILES)[None, :]).astype(np.float32),
    }
    arrays = {k: np.ascontiguousarray(v) for k, v in arrays.items()}
    args = [nc.dram_tensor(k, v.shape, mybir.dt.from_np(v.dtype), kind="ExternalInput").ap() for k, v in arrays.items()]
    out = nc.dram_tensor("out", (BATCH, SEQ, E), F32, kind="ExternalOutput").ap()
    build(nc, *args, out)
    r = run_bass_kernel_spmd(nc, [arrays], core_ids=[0])
    return r.results[0]["out"]
```

```python
from contextlib import ExitStack

import numpy as np

import concourse.bass as bass
from concourse import mybir

F32 = mybir.dt.float32
BF16 = mybir.dt.bfloat16
I32 = mybir.dt.int32
ALU = mybir.AluOpType
ACT = mybir.ActivationFunctionType
AX = mybir.AxisListType

P = 128
BATCH, SEQ, E = 8, 512, 128
TOK = BATCH * SEQ
TILES = TOK // P
NST, RANK, KCONV = 16, 64, 4
GB = 2
GROUPS = BATCH // GB
GT = GB * SEQ
GTILES = GT // P
NEXP, DFF = 16, 512
FC = DFF // P
CAP = int(1.25 * TOK / NEXP)
CAP += CAP % 2
SLOTS = NEXP * CAP
EPS = 1e-5
SMALL_A = 1e-5
SEQ1 = SEQ + 1
HPAD = KCONV - 1
NPART = 3
STEPS = GROUPS * NST
ON_POOL = {2, 4, 6, 7, 8, 11, 13, 14}
A_AT = dict(stats=0, rstd=0, nm=0, xn=1, xT=1, hT=2, conv=3, z=2, thu=4, u=4, thz=4, gate=4, du=4, G=4, dtx=4, base=5, t1=5, soft=5, C=5, split=6, cT=6, ct3=7, conv2=3)
LN_AT, REM_AT, DT_AT = 12, 11, 14
C_AT = dict(yd=3, yg=3, out=5, res=6, norm=7, rstd=9, nm=9, xn=10, mod=10, trans=12, h2T=12, logits=14, router=15, expl=14, rank=14, slots=15, gates=15)
CONV_CUT = 2
WARM0, WARM1, WARM2 = 4, 0, 0
PE_ORDER = 0
DVE_ORDER = 0
A_APART = 6
EXP_AHEAD, SCAN_AHEAD = 1, 0
RING_A, RING_K, RING_P, RING_C = 3, 4, 3, 2
ROW = 3 * E + 1
NOTOK = 1 << 20


def on_pool(m):
    return m % NST in ON_POOL


def pool_before(m):
    return sum(on_pool(i) for i in range(m))


def dve_before(m):
    return m - pool_before(m)


def sums_at(m):
    def lag(k):
        return 4 if k % NST == 0 else 4 if on_pool(k) else 2
    return [k for k in range(max(0, m - 6), min(STEPS, m)) if k + lag(k) == m]


SLOTS_B = STEPS + 4
POOL_STEPS = [m for m in range(STEPS) if on_pool(m)]
DVE_STEPS = [m for m in range(STEPS) if not on_pool(m)]
SUM_ORDER = [k for m in range(SLOTS_B) for k in sums_at(m)]
SUM_PLACE = {k: i for i, k in enumerate(SUM_ORDER)}


def build(nc, x, w_zT, w_params, w_paramsT, conv_w, w_dtT, b_dt, a_log, a_logT, d_skip, w_outT,
          gate_wT, w1, w2, cT, wmod, ident_in, sel_in, tri_in, em16_in, tok_in, out):
    disp = nc.dram_tensor("disp", [SLOTS + TOK, ROW], F32, kind="Internal").ap()
    with ExitStack() as ctx:
        def sb(name, shape, dt=F32):
            return ctx.enter_context(nc.sbuf_tensor(name, shape, dt))

        def ps(name, shape, dt=F32):
            return ctx.enter_context(nc.psum_tensor(name, shape, dt))

        def sem(name):
            return ctx.enter_context(nc.semaphore(name))

        ident = sb("ident", [P, P])
        identb = sb("identb", [P, P], BF16)
        sel = sb("sel", [NPART * NST, NST, P], BF16)
        tri = sb("tri", [P, P], BF16)
        ones = sb("ones", [P, P], BF16)
        em16 = sb("em16", [P, NEXP])
        toki = sb("toki", [P, TILES])
        wz = sb("wz", [P, P])
        wp = sb("wp", [RANK, P])
        wdt = sb("wdt", [RANK, P])
        wdtp = sb("wdtp", [P, P])
        wct = sb("wct", [P, NST])
        wc = sb("wc", [NST, P])
        wgt = sb("wgt", [P, P])
        cw = sb("cw", [P, KCONV])
        dconv = sb("dconv", [P, KCONV, P])
        bdt = sb("bdt", [P, 1])
        dsk = sb("dsk", [P, 1])
        negd = sb("negd", [P, 1])
        wo = sb("wo", [P, P])
        woga = sb("woga", [P, BATCH, P])
        gw = sb("gw", [P, NEXP])
        ct = sb("ct", [P, BATCH])
        cth = sb("cth", [P, BATCH])
        silc = sb("silc", [P, BATCH])
        modT = sb("modT", [P, 2, BATCH])
        modb = sb("modb", [P, BATCH, 3, P])
        al = sb("al", [P, NST])
        aneg = sb("aneg", [P, NST])
        amsk = sb("amsk", [P, NST])
        ainv = sb("ainv", [P, NST])
        alT = sb("alT", [NST, P])
        amskT = sb("amskT", [NST, P])
        ainvT = sb("ainvT", [NST, P])
        diag = sb("diag", [P, NST, P])
        small = sb("small", [P, NST])
        smallest = sb("smallest", [P, 1])
        flag = sb("flag", [1, 1], I32)
        halfneg = sb("halfneg", [P, GTILES])

        xs = sb("xs", [P, TILES, E])
        ct3 = sb("ct3", [NPART * NST, TOK], BF16)
        gate = sb("gate", [P, 2, GT])
        du = sb("du", [P, 2, GB * SEQ1])
        dtb = sb("dtb", [P, 2, GB, SEQ1])
        base = sb("base", [P, 2, GB, SEQ])
        st6 = sb("st6", [P, GTILES, 6])
        mv = sb("mv", [P, GTILES, 2])
        ve = sb("ve", [P, GTILES])
        rstd = sb("rstd", [P, GTILES])
        nmr = sb("nmr", [P, GTILES])
        xn = sb("xn", [P, GTILES, E])
        hT = sb("hT", [P, GB, HPAD + SEQ])
        wbuf = sb("wbuf", [P, 4, GT])
        th, expx, lnx, rem = (wbuf[:, i, :].rearrange("p (b t) -> p b t", b=GB) for i in range(4))
        ub = sb("ub", [P, GB, SEQ1])
        relx = th
        cs = sb("cs", [P, GTILES, NPART, NST], BF16)
        cr = sb("cr", [P, GTILES, NST])
        av = sb("av", [P, RING_A, GB, SEQ1])
        kv = sb("kv", [P, RING_K, GB * SEQ1])
        pd = sb("pd", [P, RING_P, GT])
        pp = sb("pp", [P, RING_P, GT])
        wm = pd[:, 0, 0:6 * P]
        csb = sb("csb", [P, 2, GT])
        gab = csb[:, 1, :].rearrange("p (b c) -> p b c", b=BATCH)
        yd = sb("yd", [P, GT])
        yg = sb("yg", [P, GT])
        h2T = yd
        sel8 = yg[0:BATCH, :].rearrange("p (b c) -> p b c", b=BATCH)
        modr, gabs, gsgn = (pd[0:BATCH, 1, i * 4 * P:i * 4 * P + 4 * P].rearrange("p (a c) -> p a c", a=4) if i < 2 else
                            pd[0:BATCH, 2, 0:4 * P].rearrange("p (a c) -> p a c", a=4) for i in range(3))
        st6c = sb("st6c", [P, GTILES, 6])
        mvc = sb("mvc", [P, GTILES, 2])
        vec = sb("vec", [P, GTILES])
        rstdc = sb("rstdc", [P, GTILES])
        nmrc = sb("nmrc", [P, GTILES])
        xn2 = yg[:, :].rearrange("p (i e) -> p i e", e=E)
        rowb = sb("rowb", [P, GTILES, ROW])
        h2, x2, wgb = rowb[:, :, 0:E], rowb[:, :, E:2 * E], rowb[:, :, 2 * E:3 * E]
        zero = rowb[:, :, :].rearrange("p i n -> p (i n)")
        mx = sb("mx", [P, GTILES])
        eq = sb("eq", [P, GTILES, NEXP])
        cand = sb("cand", [P, GTILES, NEXP])
        first = sb("first", [P, GTILES])
        oh = sb("oh", [P, GTILES, NEXP], BF16)
        dl = sb("dl", [P, GTILES, NEXP])
        el = sb("el", [P, GTILES, NEXP])
        es = sb("es", [P, GTILES])
        prob = sb("prob", [P, GTILES])
        seen = sb("seen", [P, NEXP])
        seenb = sb("seenb", [P, NEXP], BF16)
        gsum = sb("gsum", [P, NEXP])
        rsel = sb("rsel", [P, GTILES, NEXP])
        rank = sb("rank", [P, GTILES])
        keep = sb("keep", [P, GTILES])
        slot = sb("slot", [P, GTILES])
        slot2 = sb("slot2", [P, GTILES])
        idf = sb("idf", [P, GTILES])
        idf2 = sb("idf2", [P, GTILES])
        sidx = sb("sidx", [P, TILES], I32)
        wtok = sb("wtok", [P, TILES])
        cball = ps("cball", [P, 3 * SEQ])
        cb = [cball[:, i * SEQ:(i + 1) * SEQ] for i in range(3)]
        yp = ps("yp", [P, GT])
        ab = [ps(f"ab{i}", [P, SEQ]) for i in range(2)]
        cc = ps("cc", [P, SEQ])

        def bank(b, i):
            return (cc[:, :], yp[:, SEQ:])[i] if b == 1 else ab[i][:, :]


        def cbank(b):
            return ab[0] if b == BATCH - 1 else cc

        s_w0 = sem("s_w0")
        s_w = sem("s_w")
        s_x = [sem(f"s_x{g}") for g in range(GROUPS)]
        s_zero = sem("s_zero")
        s_zf = sem("s_zf")
        s_pc = sem("s_pc")
        vch = sem("vch")
        pch = sem("pch")
        ach = sem("ach")
        s_cth = sem("s_cth")
        s_silc = sem("s_silc")
        s_silb = sem("s_silb")
        s_mm0 = sem("s_mm0")
        s_pro = sem("s_pro")
        s_modb = sem("s_modb")
        s_modp = sem("s_modp")
        s_modg = sem("s_modg")
        s_aexp = sem("s_aexp")
        s_dc = sem("s_dc")
        s_diag = sem("s_diag")
        s_ainv = sem("s_ainv")
        s_ve = sem("s_ve")
        s_rstd = sem("s_rstd")
        s_xn = sem("s_xn")
        s_xT = sem("s_xT")
        s_hT = sem("s_hT")
        s_z = sem("s_z")
        s_thz = sem("s_thz")
        s_gate = sem("s_gate")
        s_cv = sem("s_cv")
        s_thu = sem("s_thu")
        s_u = sem("s_u")
        s_du = sem("s_du")
        s_G = sem("s_G")
        s_Gr = sem("s_Gr")
        s_base = sem("s_base")
        s_xdt = sem("s_xdt")
        s_abs = sem("s_abs")
        s_exp = sem("s_exp")
        s_ln = sem("s_ln")
        s_rel = sem("s_rel")
        s_rem = sem("s_rem")
        s_t1 = sem("s_t1")
        s_flag = sem("s_flag")
        f_go = sem("f_go")
        f_exp = sem("f_exp")
        f_cb = sem("f_cb")
        f_used = sem("f_used")
        f_chain = sem("f_chain")
        s_nm = sem("s_nm")
        c_nm = sem("c_nm")
        s_sel8 = sem("s_sel8")
        s_mr = sem("s_mr")
        s_dt = sem("s_dt")
        s_C = sem("s_C")
        s_cs = sem("s_cs")
        s_cT = sem("s_cT")
        s_ct3 = sem("s_ct3")
        b_exp = sem("b_exp")
        b_cb = sem("b_cb")
        b_csb = sem("b_csb")
        b_scan = sem("b_scan")
        b_pd = sem("b_pd")
        b_pp = sem("b_pp")
        b_sum = sem("b_sum")
        c_yd = sem("c_yd")
        c_yg = sem("c_yg")
        c_o = sem("c_o")
        c_x2 = sem("c_x2")
        c_st = sem("c_st")
        c_wgb = sem("c_wgb")
        c_ve = sem("c_ve")
        c_rstd = sem("c_rstd")
        c_xn = sem("c_xn")
        c_xm = sem("c_xm")
        c_h2 = sem("c_h2")
        c_tr = sem("c_tr")
        c_h2T = sem("c_h2T")
        c_lg = sem("c_lg")
        c_dl = sem("c_dl")
        c_el = sem("c_el")
        c_oh = sem("c_oh")
        c_rk = sem("c_rk")
        c_wt = sem("c_wt")
        c_rt = sem("c_rt")
        c_sc = [sem(f"c_sc{i}") for i in range(2)]


        CT = -(-CAP // P)
        CLAST = CAP - (CT - 1) * P
        WRING, RR, XR = 4, 5, 3
        w1s = wbuf[:, :, 0:DFF]
        w2s = wbuf[:, :, DFF:2 * DFF].rearrange("p w (f e) -> p w f e", f=FC)

        def over(t, *shape):
            n = int(np.prod(shape))
            names = " ".join("abcd"[:len(shape)])
            flat = t.rearrange("p " + " ".join("xyz"[:len(t.shape) - 1]) + " -> p (" + " ".join("xyz"[:len(t.shape) - 1]) + ")")
            return flat[:, 0:n].rearrange(f"p ({names}) -> p {names}", **dict(zip("abcd", shape)))

        rows_x, rows_a = over(xs[:, :, :], 3, CT, ROW), over(av[:, :, :, :], 2, CT, ROW)
        rows = [rows_x[:, i] for i in range(3)] + [rows_a[:, i] for i in range(2)]
        rowsT = over(pp[:, :, :], XR, CAP)
        hid = over(kv[:, :, :], XR, FC, CAP)
        res = over(pd[:, :, :], XR, CT, E)
        tokf = sb("tokf", [P, XR, CT])
        tokx = sb("tokx", [P, XR, CT], I32)
        x_w = [sem(f"x_w{i}") for i in range(WRING)]
        x_rows = [sem(f"x_rows{i}") for i in range(RR)]
        x_T = sem("x_T")
        x_Tc = sem("x_Tc")
        x_f1 = sem("x_f1")
        x_gelu = sem("x_gelu")
        x_f2 = sem("x_f2")
        x_tok = sem("x_tok")
        x_m = sem("x_m")
        x_res = sem("x_res")
        x_out = [sem(f"x_out{i}") for i in range(XR)]

        def experts_sync(sp):
            def load_w(e):
                if e >= WRING:
                    sp.wait_ge(x_f2, e - WRING + 1)
                sp.dma_start(w1s[:, e % WRING, :], w1[e]).then_inc(x_w[e % WRING], 16)
                sp.dma_start(w2s[:, e % WRING, :, :], w2[e].rearrange("(f p) d -> p f d", p=P)).then_inc(x_w[e % WRING], 16)

            def load_rows(e):
                if e >= RR:
                    sp.wait_ge(x_res, e - RR + 1)
                r = disp[e * CAP:(e + 1) * CAP, :]
                sp.dma_start(rows[e % RR][:, 0:CT - 1, :], r[0:(CT - 1) * P, :].rearrange("(c p) e -> p c e", p=P)
                             ).then_inc(x_rows[e % RR], 16)
                sp.dma_start(rows[e % RR][0:CLAST, CT - 1, :], r[(CT - 1) * P:CAP, :]).then_inc(x_rows[e % RR], 16)

            sp.wait_ge(s_dt, BATCH)
            for e in range(WRING):
                load_w(e)
            for k in range(2):
                sp.wait_ge(c_sc[k], 16 * TILES // 2)
            for e in range(RR):
                load_rows(e)
            for e in range(NEXP):
                if e + WRING < NEXP:
                    load_w(e + WRING)
                if e + RR < NEXP:
                    load_rows(e + RR)
            for k in range(XR):
                sp.wait_ge(x_out[k], 16 * CT * len(range(k, NEXP, XR)))

        def experts_scalar(act):
            for e in range(NEXP):
                for h in range(2):
                    act.wait_ge(x_f1, 2 * e + h + 1)
                    if e >= XR:
                        act.wait_ge(x_f2, e - XR + 1)
                    act.activation(hid[:, e % XR, 2 * h:2 * h + 2, :], FB[h], ACT.Gelu_apprx_tanh).then_inc(x_gelu, 1)

        def experts_vector(dve):
            def turn(e):
                dve.wait_ge(x_T, e + 1)
                if e >= XR:
                    dve.wait_ge(x_f1, 2 * (e - XR + 1))
                dve.tensor_copy(rowsT[:, e % XR, :], cc[:, 0:CAP]).then_inc(x_Tc, 1)

            turn(0)
            turn(1)
            for e in range(NEXP):
                if e + 2 < NEXP:
                    turn(e + 2)
                dve.wait_ge(x_rows[e % RR], 32 * (e // RR + 1))
                if e >= XR:
                    dve.wait_ge(x_out[e % XR], 16 * CT * (e // XR))
                t = [(slice(0, P), slice(0, CT - 1)), (slice(0, CLAST), slice(CT - 1, CT))]
                for p, c in t:
                    dve.tensor_scalar(tokx[p, e % XR, c], rows[e % RR][p, c, 3 * E:ROW].rearrange("p c a -> p (c a)"),
                                      float(NOTOK), None, ALU.add).then_inc(x_tok, 1)
                dve.wait_ge(x_f2, e + 1)
                o = OB[e % 2].rearrange("p (c e) -> p c e", e=E)
                for p, c in t:
                    dve.tensor_tensor(res[p, e % XR, c, :], o[p, c, :], rows[e % RR][p, c, 2 * E:3 * E],
                                      ALU.mult).then_inc(x_m, 1)
                dve.wait_ge(x_m, 2 * e + 2)
                for p, c in t:
                    last = dve.tensor_tensor(res[p, e % XR, c, :], res[p, e % XR, c, :], rows[e % RR][p, c, E:2 * E],
                                             ALU.add)
                last.then_inc(x_res, 1)

        def experts_gpsimd(pool):
            pool.wait_ge(c_st, 16 * BATCH)
            flat = out.rearrange("b t e -> (b t) e")
            for e in range(NEXP):
                pool.wait_ge(x_tok, 2 * e + 2)
                pool.wait_ge(x_res, e + 1)
                for c in range(CT):
                    n = P if c < CT - 1 else CLAST
                    pool.indirect_dma_start(flat, bass.IndirectOffsetOnAxis(ap=tokx[0:n, e % XR, c:c + 1], axis=0),
                                            res[0:n, e % XR, c, :], None, bounds_check=TOK - 1, oob_is_err=False
                                            ).then_inc(x_out[e % XR], 16)

        FB = [yp[:, :].rearrange("p (f t) -> p f t", f=2)[:, :, 0:CAP], cball[:, 0:2 * SEQ].rearrange("p (f t) -> p f t", f=2)[:, :, 0:CAP]]
        OB = [cb[2][:, 0:CT * E], ab[1][:, 0:CT * E]]

        def experts_tensor(pe):
            def turn(e):
                pe.wait_ge(x_rows[e % RR], 32 * (e // RR + 1))
                if e:
                    pe.wait_ge(x_Tc, e)
                for c in range(CT):
                    n = P if c < CT - 1 else CLAST
                    last = pe.transpose(cc[:, c * P:c * P + n], rows[e % RR][0:n, c, 0:E], ident[0:n, 0:n])
                last.then_inc(x_T, 1)

            def up(e):
                pe.wait_ge(x_Tc, e + 1)
                pe.wait_ge(x_w[e % WRING], 32 * (e // WRING + 1))
                for h in range(2):
                    if e:
                        pe.wait_ge(x_gelu, 2 * (e - 1) + h + 1)
                    for f in (2 * h, 2 * h + 1):
                        last = pe.matmul(FB[h][:, f % 2, :], w1s[:, e % WRING, f * P:(f + 1) * P],
                                         rowsT[:, e % XR, :], start=True, stop=True)
                    last.then_inc(x_f1, 1)

            def down(e):
                pe.wait_ge(x_gelu, 2 * e + 2)
                if e >= 2:
                    pe.wait_ge(x_res, e - 1)
                for c in range(CT):
                    n = P if c < CT - 1 else CLAST
                    for f in range(FC):
                        last = pe.matmul(OB[e % 2][0:n, c * E:(c + 1) * E], hid[:, e % XR, f, c * P:c * P + n],
                                         w2s[:, e % WRING, f, :], start=(f == 0), stop=(f == FC - 1))
                last.then_inc(x_f2, 1)

            pe.wait_ge(c_rt, GROUPS)
            turn(0)
            turn(1)
            up(0)
            for e in range(NEXP):
                if e + 1 < NEXP:
                    up(e + 1)
                if e + 2 < NEXP:
                    turn(e + 2)
                down(e)

        block = ctx.enter_context(nc.Block())
        loads_act = [
            (ct[:, :], cT), (ident[:, :], ident_in), (wm, wmod),
        ]
        loads_sp = [
            (cw[:, :], conv_w.rearrange("e a k -> e (a k)")), (wp[:, :], w_params[0:RANK, :]), (wdt[:, :], w_dtT),
            (al[:, :], a_log), (alT[:, :], a_logT),
        ]
        later_sp = [
            (wz[:, :], w_zT), (wc[:, :], w_params[RANK + NST:RANK + 2 * NST, :]),
            (wct[:, :], w_paramsT[:, RANK + NST:RANK + 2 * NST]),
            (bdt[:, :], b_dt.rearrange("(e a) -> e a", a=1)),
            (dsk[:, :], d_skip.rearrange("(e a) -> e a", a=1)),
            (sel[:, :, :], sel_in), (gw[:, :], gate_wT), (wo[:, :], w_outT),
            (tri[:, :], tri_in), (em16[:, :], em16_in), (toki[:, :], tok_in),
        ]
        NW0 = 16 * (len(loads_sp) + len(loads_act))
        NW = 16 * len(later_sp)

        @block.sync
        def _(sp):
            def load_x(g):
                sp.dma_start(xs[:, g * GTILES:(g + 1) * GTILES, :],
                             x[GB * g:GB * (g + 1)].rearrange("b (i p) e -> p (b i) e", p=P)).then_inc(s_x[g], 16)
            load_x(0)
            for dst, src in loads_sp:
                sp.dma_start(dst, src).then_inc(s_w0, 16)
            for dst, src in later_sp:
                sp.dma_start(dst, src).then_inc(s_w, 16)
            for g in range(1, GROUPS):
                load_x(g)
            sp.wait_ge(s_zero, 1)
            sp.dma_start(disp[0:SLOTS, :].rearrange("(r p a) e -> p r (a e)", p=P, a=8),
                         zero.rearrange("p (r n) -> p r n", r=1).broadcast_to([P, SLOTS // (8 * P), 8 * ROW])
                         ).then_inc(s_zf, 16)
            for g in range(GROUPS):
                for j in range(GB):
                    sp.wait_ge(c_x2, GB * g + j + 1)
                    sp.dma_start(out[GB * g + j].rearrange("(i p) e -> p i e", p=P), x2[:, 4 * j:4 * j + 4, :]
                                 ).then_inc(c_st, 16)
            experts_sync(sp)

        @block.scalar
        def _(act):
            for dst, src in loads_act:
                act.dma_start(dst, src).then_inc(s_w0, 16)

            def a_xn(b):
                act.wait_ge(s_nm, b + 1)
                act.wait_ge(s_x[b // GB], 16)
                if b >= GB:
                    act.wait_ge(s_xT, b - GB + 1)
                for j in range(4):
                    o = 4 * (b % GB) + j
                    last = act.activation(xn[:, o, :], xs[:, 4 * b + j, :], ACT.Identity,
                                          scale=rstd[:, o:o + 1], bias=nmr[:, o:o + 1])
                last.then_inc(s_xn, 1)

            def c_xn_(b):
                act.wait_ge(c_nm, b + 1)
                if b >= GB:
                    act.wait_ge(c_h2, b - GB + 1)
                for j in range(4 * (b % GB), 4 * (b % GB) + 4):
                    last = act.activation(xn2[:, j, :], x2[:, j, :], ACT.Identity,
                                          scale=rstdc[:, j:j + 1], bias=nmrc[:, j:j + 1])
                last.then_inc(c_xn, 1)

            def c_gates(g):
                act.wait_ge(c_wt, g + 1)
                for j in range(GTILES):
                    act.activation(wgb[:, j, :], modb[:, GB * g + j // 4, 2, :], ACT.Copy,
                                   scale=wtok[:, g * GTILES + j:g * GTILES + j + 1]).then_inc(c_wgb, 1)

            def a_hT(b):
                act.wait_ge(s_xT, b + 1)
                if b == 0:
                    act.wait_ge(s_pro, 2)
                if b >= GB:
                    act.wait_ge(s_C, b - GB + 1)
                act.activation(hT[:, b % GB, HPAD:], bank(b, 0)[:, :], ACT.Identity,
                               scale=modT[:, 1, b:b + 1], bias=modT[:, 0, b:b + 1]).then_inc(s_hT, 1)

            def a_thz(b):
                act.wait_ge(s_z, b + 1)
                if b >= GB:
                    act.wait_ge(s_rem, 2 * (b - GB) + 1)
                act.activation(expx[:, b % GB, :], bank(b, 1)[:, :], ACT.Tanh, scale=0.5).then_inc(s_thz, 1)

            def a_thu(b):
                act.wait_ge(s_cv, b + 1)
                if b >= GB:
                    act.wait_ge(s_dt, b - GB + 1)
                act.activation(th[:, b % GB, :], bank(b, 0)[:, :], ACT.Tanh, scale=0.5).then_inc(s_thu, 1)

            def a_soft(b):
                act.wait_ge(s_xdt, b + 1)
                act.wait_ge(s_gate, b + 1)
                act.activation(expx[:, b % GB, :], bank(b, 0)[:, :], ACT.Abs, bias=bdt[:, 0:1]).then_inc(s_abs, 1)
                act.wait_ge(s_abs, b + 1)
                act.activation(expx[:, b % GB, :], expx[:, b % GB, :], ACT.Exp, scale=-1.0).then_inc(s_exp, 1)
                act.activation(relx[:, b % GB, :], bank(b, 0)[:, :], ACT.Relu, bias=bdt[:, 0:1]).then_inc(s_rel, 1)

            def a_ln(b):
                act.wait_ge(s_exp, b + 1)
                act.activation(lnx[:, b % GB, :], expx[:, b % GB, :], ACT.Ln, bias=1.0).then_inc(s_ln, 1)

            def a_ct3(b):
                act.wait_ge(s_cT, b + 1)
                act.activation(ct3[:, b * SEQ:(b + 1) * SEQ], bank(b, 1)[0:NPART * NST, 128:128 + SEQ // 2].bitcast(BF16),
                               ACT.Copy).then_inc(s_ct3, 1)

            def b_step(m):
                g, n = divmod(m, NST)
                if n == 0:
                    act.wait_ge(s_dt, GB * (g + 1))
                if m >= RING_A:
                    act.wait_ge(b_scan, m - RING_A + 1)
                act.activation(av[:, m % RING_A, :, 1:SEQ1], dtb[:, g % 2, :, 0:SEQ], ACT.Exp,
                               scale=aneg[:, n:n + 1]).then_inc(b_exp, 1)

            def b_copy(m):
                if on_pool(m):
                    k = pool_before(m)
                    if k == 0:
                        act.wait_ge(s_modg, 1)
                    if k >= 2:
                        act.wait_ge(b_pp, k - 1)
                    for j in range(GB):
                        act.wait_ge(b_cb, GB * m + j + 1)
                        act.activation(csb[:, k % 2, j * SEQ:(j + 1) * SEQ], cb[(GB * m + j) % 3],
                                       ACT.Copy).then_inc(b_csb, 1)

            def c_h2Tcopy(b):
                act.wait_ge(c_tr, b + 1)
                if b >= GB:
                    act.wait_ge(c_lg, b // GB)
                act.activation(h2T[:, b % GB * SEQ:(b % GB + 1) * SEQ], cbank(b)[:, :], ACT.Copy).then_inc(c_h2T, 1)

            def c_expl(g):
                act.wait_ge(c_dl, g + 1)
                act.activation(el[:, :, :], dl[:, :, :], ACT.Exp).then_inc(c_el, 1)

            def p_modb(b):
                act.wait_ge(s_modp, b + 1)
                act.activation(gab[:, b, :], cb[b % 3][:, 0:P], ACT.Copy).then_inc(s_modb, 1)
                act.activation(modb[:, b, :, :], cb[b % 3][:, P:4 * P].rearrange("p (a e) -> p a e", a=3),
                               ACT.Copy).then_inc(s_modb, 1)

            a_xn(0)
            act.wait_ge(s_w0, NW0)
            act.activation(cth[:, :], ct[:, :], ACT.Tanh, scale=0.5).then_inc(s_cth, 1)
            a_xn(1)
            act.activation(aneg[:, :], al[:, :], ACT.Exp).then_inc(s_aexp, 1)
            act.activation(amskT[:, :], alT[:, :], ACT.Exp).then_inc(s_aexp, 1)
            for b in range(GB):
                a_hT(b)
            act.wait_ge(s_w, NW)
            for b in range(GB):
                a_thu(b)
            for b in range(GB):
                a_thz(b)
            for b in range(3):
                p_modb(b)
            for b in range(GB):
                a_soft(b)
            for b in range(3, BATCH):
                p_modb(b)
            for b in range(GB):
                a_ln(b)
            for b in range(GB):
                a_ct3(b)
            act.wait_ge(s_flag, 1)
            smalls = act.value_load(flag[0:1, 0:1])

            def small_a(g):
                with act.If(smalls > 0):
                    act.wait_ge(s_dt, GB * (g + 1))
                    act.wait_ge(f_go, g + 1)
                    for i in range(GB * NST):
                        n, j = divmod(i, GB)
                        k = g * GB * NST + i
                        if k >= GB:
                            act.wait_ge(f_used, k - GB + 1)
                        act.activation(expx[:, j, :], dtb[:, g % 2, j, 0:SEQ], ACT.Exp,
                                       scale=aneg[:, n:n + 1]).then_inc(f_exp, 1)
                    act.wait_ge(f_used, (g + 1) * GB * NST)

            for m in range(EXP_AHEAD):
                b_step(m)
            for m in range(SLOTS_B):
                g, n = divmod(m, NST)
                if n == 0 and g < GROUPS:
                    small_a(g)
                if m + EXP_AHEAD < STEPS:
                    b_step(m + EXP_AHEAD)
                if 1 <= m <= STEPS:
                    b_copy(m - 1)
                if g + 1 < GROUPS:
                    for j in range(GB):
                        b, p = GB * (g + 1) + j, n - A_APART * j
                        if p == A_AT["xn"]:
                            a_xn(b)
                        if p == A_AT["hT"]:
                            a_hT(b)
                        if p == A_AT["thu"]:
                            a_thu(b)
                        if p == A_AT["thz"]:
                            a_thz(b)
                        if p == A_AT["soft"]:
                            a_soft(b)
                        if p == A_AT["ct3"]:
                            a_ct3(b)
                    if n == LN_AT:
                        a_ln(GB * g + GB)
                        a_ln(GB * g + GB + 1)
                if g and g < GROUPS:
                    for j in range(GB):
                        if n == C_AT["xn"] + j:
                            c_xn_(GB * (g - 1) + j)
                        if n == C_AT["h2T"] + j:
                            c_h2Tcopy(GB * (g - 1) + j)
                    if n == C_AT["expl"]:
                        c_expl(g - 1)
                    if n == C_AT["gates"]:
                        c_gates(g - 1)
            c_xn_(BATCH - 2)
            c_xn_(BATCH - 1)
            c_h2Tcopy(BATCH - 2)
            c_h2Tcopy(BATCH - 1)
            c_expl(GROUPS - 1)
            c_gates(GROUPS - 1)
            experts_scalar(act)

        @block.gpsimd
        def _(pool):
            pool.memset(halfneg[:, :], -0.5).then_inc(s_pc, 1)
            pool.memset(du[:, :, :], 0.0).then_inc(s_pc, 1)
            pool.memset(ones[:, :], 1.0).then_inc(s_pc, 1)
            pool.memset(hT[:, :, 0:HPAD], 0.0).then_inc(s_pc, 1)
            pool.memset(av[:, :, :, 0:1], 0.0).then_inc(s_pc, 1)
            pool.memset(seen[:, :], 0.0).then_inc(s_pc, 1)
            pool.memset(seenb[:, :], 0.0).then_inc(s_pc, 1)

            def a_rstd(b):
                pool.wait_ge(s_ve, b + 1)
                if b >= GB:
                    pool.wait_ge(s_xn, b - GB + 1)
                j = slice(4 * (b % GB), 4 * (b % GB) + 4)
                pool.tensor_tensor(rstd[:, j], ve[:, j], halfneg[:, 0:4], ALU.pow).then_inc(s_rstd, 1)

            def a_du(b):
                pool.wait_ge(s_u, b + 1)
                if b >= 2 * GB:
                    pool.wait_ge(b_scan, (b // GB - 1) * NST)
                d, u = du[:, b // GB % 2, (b % GB) * SEQ1:(b % GB + 1) * SEQ1], ub[:, b % GB, :]
                pool.tensor_copy(d[:, 1:2], u[:, 0:1]).then_inc(s_du, 1)
                pool.tensor_tensor(d[:, 2:SEQ1], u[:, 1:SEQ], u[:, 0:SEQ - 1], ALU.subtract).then_inc(s_du, 1)

            def a_rem(b):
                r, t = rem[:, b % GB, :], expx[:, b % GB, :]
                pool.wait_ge(s_t1, b + 1)
                pool.tensor_tensor(r, t, r, ALU.subtract).then_inc(s_rem, 1)
                pool.wait_ge(s_rem, 2 * b + 1)
                pool.wait_ge(s_ln, b + 1)
                pool.tensor_tensor(r, r, lnx[:, b % GB, :], ALU.add).then_inc(s_rem, 1)

            def b_mult(m):
                if on_pool(m):
                    k = pool_before(m)
                    pool.wait_ge(b_csb, GB * (k + 1))
                    pool.wait_ge(b_scan, m + 1)
                    if k >= RING_P:
                        pool.wait_ge(b_sum, SUM_PLACE[POOL_STEPS[k - RING_P]] + 1)
                    pool.tensor_tensor(pp[:, k % RING_P, :].rearrange("p (b t) -> p b t", b=GB),
                                       kv[:, m % RING_K, :].rearrange("p (b t) -> p b t", b=GB)[:, :, 1:SEQ1],
                                       csb[:, k % 2, :].rearrange("p (b t) -> p b t", b=GB),
                                       ALU.mult).then_inc(b_pp, 1)

            def c_yg_(g):
                pool.wait_ge(c_yd, g + 1)
                if g:
                    pool.wait_ge(c_h2, GB * g)
                pool.tensor_tensor(yg[:, :], yd[:, :], gate[:, g % 2, :], ALU.mult).then_inc(c_yg, 1)

            def c_rstd_(b):
                t = slice(4 * (b % GB), 4 * (b % GB) + 4)
                pool.wait_ge(c_ve, b + 1)
                if b >= GB:
                    pool.wait_ge(c_xn, b - GB + 1)
                pool.tensor_tensor(rstdc[:, t], vec[:, t], halfneg[:, t], ALU.pow).then_inc(c_rstd, 1)

            def c_mod(b, add):
                j = slice(4 * (b % GB), 4 * (b % GB) + 4)
                if not add:
                    pool.wait_ge(c_xn, b + 1)
                    pool.wait_ge(s_modg, 1)
                    pool.tensor_tensor(xn2[:, j, :], xn2[:, j, :], modb[:, b, 1:2, :].broadcast_to([P, 4, P]),
                                       ALU.mult).then_inc(c_xm, 1)
                else:
                    pool.wait_ge(c_xm, b + 1)
                    pool.tensor_tensor(h2[:, j, :], xn2[:, j, :], modb[:, b, 0:1, :].broadcast_to([P, 4, P]),
                                       ALU.add).then_inc(c_h2, 1)

            def c_scatter(g, tiles):
                pool.wait_ge(c_rt, g + 1)
                if g == 0:
                    pool.wait_ge(s_zf, 16)
                for j in tiles:
                    pool.wait_ge(c_wgb, GTILES * g + j + 1)
                    pool.indirect_dma_start(disp, bass.IndirectOffsetOnAxis(ap=sidx[:, g * GTILES + j:g * GTILES + j + 1], axis=0),
                                            rowb[:, j, :], None).then_inc(c_sc[g % 2], 16)

            pool.wait_ge(s_pc, 7)
            for b in range(GB):
                a_rstd(b)
            pool.memset(zero, 0.0).then_inc(s_zero, 1)
            pool.wait_ge(s_w0, NW0)
            pool.tensor_copy(identb[:, :], ident[:, :]).then_inc(s_pc, 1)
            pool.wait_ge(s_ainv, 1)
            pool.tensor_tensor(diag[:, :, :], ident[:, :].rearrange("p (a c) -> p a c", a=1).broadcast_to([P, NST, P]),
                               ainv[:, :].rearrange("p (k a) -> p k a", a=1).broadcast_to([P, NST, P]),
                               ALU.mult).then_inc(s_diag, 1)
            for b in range(GB):
                a_du(b)
            for b in range(GB):
                a_rem(b)
            for m in range(SLOTS_B):
                g, n = divmod(m, NST)
                b = GB * (g - 1)
                if g and g < GROUPS:
                    if n == C_AT["yg"]:
                        c_yg_(g - 1)
                    for j in range(GB):
                        if n == C_AT["rstd"] + j:
                            c_rstd_(b + j)
                if m >= 1 and m <= STEPS:
                    b_mult(m - 1)
                if g and g < GROUPS:
                    for j in range(GB):
                        if n == C_AT["mod"] + j:
                            c_mod(b + j, False)
                            c_mod(b + j, True)
                if 2 <= g < GROUPS and n < 2:
                    c_scatter(g - 2, range(4 * n, 4 * n + 4))
                if g + 1 < GROUPS:
                    for j in range(GB):
                        b, p = GB * (g + 1) + j, n - A_APART * j
                        if p == A_AT["rstd"]:
                            a_rstd(b)
                        if p == A_AT["du"]:
                            a_du(b)
                    if n == REM_AT:
                        a_rem(GB * g + GB)
                        a_rem(GB * g + GB + 1)
            g = GROUPS - 1
            c_scatter(g - 1, range(GTILES))
            c_yg_(g)
            for b in range(GB * g, BATCH):
                c_rstd_(b)
            for b in range(GB * g, BATCH):
                c_mod(b, False)
                c_mod(b, True)
            c_scatter(g, range(GTILES))
            experts_gpsimd(pool)

        @block.vector
        def _(dve):
            chain = [0]

            def link(ins):
                chain[0] += 1
                ins.then_inc(vch, 1)
                dve.wait_ge(vch, chain[0])

            def a_stats(b):
                dve.wait_ge(s_x[b // GB], 16)
                if b >= GB:
                    dve.wait_ge(s_rstd, b - GB + 1)
                    dve.wait_ge(s_xn, b - GB + 1)
                o = 4 * (b % GB)
                for j in range(4):
                    last = dve.bn_stats(st6[:, o + j, :], xs[:, 4 * b + j, :])
                link(last)
                for j in range(4):
                    last = dve.bn_aggr(mv[:, o + j, :], st6[:, o + j, :])
                link(last)
                dve.tensor_scalar(ve[:, o:o + 4], mv[:, o:o + 4, 1], EPS, None, ALU.add).then_inc(s_ve, 1)

            def a_nm(b):
                dve.wait_ge(s_rstd, b + 1)
                if b >= GB:
                    dve.wait_ge(s_xn, b - GB + 1)
                j = slice(4 * (b % GB), 4 * (b % GB) + 4)
                dve.scalar_tensor_tensor(nmr[:, j], mv[:, j, 0], -1.0, rstd[:, j], ALU.mult, ALU.mult).then_inc(s_nm, 1)

            def a_gate(b):
                dve.wait_ge(s_thz, b + 1)
                g, j = divmod(b, GB)
                if g >= 2:
                    dve.wait_ge(c_yg, g - 1)
                dve.scalar_tensor_tensor(gate[:, g % 2, j * SEQ:(j + 1) * SEQ], expx[:, j, :], 1.0,
                                         bank(b, 1)[:, :], ALU.add, ALU.mult).then_inc(s_gate, 1)

            def a_u(b):
                dve.wait_ge(s_thu, b + 1)
                j = b % GB
                if b >= GB:
                    dve.wait_ge(s_du, 2 * (b - GB + 1))
                    dve.wait_ge(s_base, b - GB + 1)
                link(dve.scalar_tensor_tensor(ub[:, j, 1:SEQ1], th[:, j, :], 1.0, bank(b, 0)[:, :], ALU.add, ALU.mult))
                dve.tensor_copy(ub[:, j, 0:1], ub[:, j, 1:2]).then_inc(s_u, 1)

            def a_base(b):
                dve.wait_ge(s_G, b + 1)
                dve.wait_ge(s_u, b + 1)
                g, j = divmod(b, GB)
                if g >= 2:
                    dve.wait_ge(c_yd, g - 1)
                dve.tensor_tensor(base[:, g % 2, j, :], bank(b, 1)[:, :], ub[:, j, 0:SEQ], ALU.mult).then_inc(s_Gr, 1)
                dve.wait_ge(s_Gr, b + 1)
                dve.scalar_tensor_tensor(base[:, g % 2, j, :], ub[:, j, 1:SEQ1], negd[:, 0:1],
                                         base[:, g % 2, j, :], ALU.mult, ALU.add).then_inc(s_base, 1)

            def a_t1(b):
                dve.wait_ge(s_exp, b + 1)
                dve.tensor_scalar(rem[:, b % GB, :], expx[:, b % GB, :], 1.0, -1.0, ALU.add, ALU.add).then_inc(s_t1, 1)

            def a_dt(b):
                dve.wait_ge(s_rem, 2 * b + 2)
                dve.wait_ge(s_rel, b + 1)
                g, j = divmod(b, GB)
                if g >= 2:
                    dve.wait_ge(b_exp, (g - 1) * NST)
                link(dve.tensor_tensor(dtb[:, g % 2, j, 1:SEQ1], rem[:, j, :], relx[:, j, :], ALU.add))
                dve.tensor_copy(dtb[:, g % 2, j, 0:1], dtb[:, g % 2, j, 1:2]).then_inc(s_dt, 1)

            def a_split(b):
                dve.wait_ge(s_C, b + 1)
                if b >= GB:
                    dve.wait_ge(s_cT, b - GB + 1)
                j = slice(4 * (b % GB), 4 * (b % GB) + 4)
                c = bank(b, 1)[:, 0:4 * NST].rearrange("p (i n) -> p i n", n=NST)
                link(dve.tensor_copy(cs[:, j, 0, :], c))
                link(dve.tensor_tensor(cr[:, j, :], c, cs[:, j, 0, :], ALU.subtract))
                link(dve.tensor_copy(cs[:, j, 1, :], cr[:, j, :]))
                dve.tensor_tensor(cs[:, j, 2, :], cr[:, j, :], cs[:, j, 1, :], ALU.subtract).then_inc(s_cs, 1)

            def b_scan_(m):
                g, n = divmod(m, NST)
                dve.wait_ge(b_exp, m + 1)
                if n == 0:
                    dve.wait_ge(s_du, 2 * GB * (g + 1))
                if m >= RING_K:
                    k = m - RING_K
                    if on_pool(k):
                        dve.wait_ge(b_pp, pool_before(k) + 1)
                    else:
                        dve.wait_ge(b_pd, GB * (dve_before(k) + 1))
                dve.tensor_tensor_scan(kv[:, m % RING_K, :], du[:, g % 2, :],
                                       av[:, m % RING_A, :, :].rearrange("p b t -> p (b t)"), 0.0,
                                       ALU.add, ALU.mult).then_inc(b_scan, 1)

            def b_mult(m):
                if on_pool(m):
                    return
                k = dve_before(m)
                dve.wait_ge(b_scan, m + 1)
                if k >= RING_P:
                    dve.wait_ge(b_sum, SUM_PLACE[DVE_STEPS[k - RING_P]] + 1)
                for j in range(GB):
                    dve.wait_ge(b_cb, GB * m + j + 1)
                    dve.tensor_tensor(pd[:, k % RING_P, j * SEQ:(j + 1) * SEQ],
                                      kv[:, m % RING_K, j * SEQ1 + 1:(j + 1) * SEQ1],
                                      cb[(GB * m + j) % 3], ALU.mult).then_inc(b_pd, 1)

            def c_yd_(g):
                dve.wait_ge(b_sum, NST * (g + 1))
                if g:
                    dve.wait_ge(c_yg, g)
                    dve.wait_ge(c_lg, g)
                dve.tensor_tensor(yd[:, :], yp[:, :], base[:, g % 2, :, :].rearrange("p b t -> p (b t)"),
                                  ALU.subtract).then_inc(c_yd, 1)

            def c_res(b):
                dve.wait_ge(c_o, b + 1)
                if b == 0:
                    dve.wait_ge(s_zf, 16)
                if b >= GB:
                    g = b // GB - 1
                    dve.wait_ge(c_sc[g % 2], 16 * GTILES * (g // 2 + 1))
                    dve.wait_ge(c_st, 16 * GB * (g + 1))
                j = slice(4 * (b % GB), 4 * (b % GB) + 4)
                dve.tensor_tensor(x2[:, j, :], cbank(b)[:, :].rearrange("p (i e) -> p i e", e=E), xs[:, 4 * b:4 * b + 4, :],
                                  ALU.add).then_inc(c_x2, 1)

            def c_norm(b):
                t = slice(4 * (b % GB), 4 * (b % GB) + 4)
                dve.wait_ge(c_x2, b + 1)
                if b >= GB:
                    dve.wait_ge(c_xn, b - GB + 1)
                for j in range(t.start, t.stop):
                    last = dve.bn_stats(st6c[:, j, :], x2[:, j, :])
                link(last)
                for j in range(t.start, t.stop):
                    last = dve.bn_aggr(mvc[:, j, :], st6c[:, j, :])
                link(last)
                dve.tensor_scalar(vec[:, t], mvc[:, t, 1], EPS, None, ALU.add).then_inc(c_ve, 1)

            def c_nm_(b):
                t = slice(4 * (b % GB), 4 * (b % GB) + 4)
                dve.wait_ge(c_rstd, b + 1)
                dve.scalar_tensor_tensor(nmrc[:, t], mvc[:, t, 0], -1.0, rstdc[:, t], ALU.mult, ALU.mult).then_inc(c_nm, 1)

            def c_router(g):
                dve.wait_ge(c_lg, g + 1)
                if g:
                    dve.wait_ge(c_rt, g)
                    dve.wait_ge(c_rk, g)
                lg = cc[:, 0:GTILES * NEXP].rearrange("p (i n) -> p i n", n=NEXP)
                wide = [P, GTILES, NEXP]
                link(dve.tensor_reduce(mx[:, :], lg, AX.X, ALU.max))
                mxb = mx[:, :].rearrange("p (i a) -> p i a", a=1).broadcast_to(wide)
                link(dve.tensor_tensor(dl[:, :, :], lg, mxb, ALU.subtract))
                dve.tensor_scalar(eq[:, :, :], dl[:, :, :], 0.0, None, ALU.is_ge).then_inc(c_dl, 1)
                dve.wait_ge(c_dl, g + 1)
                emb = em16[:, :].rearrange("p (a n) -> p a n", a=1).broadcast_to(wide)
                link(dve.tensor_tensor(cand[:, :, :], eq[:, :, :], emb, ALU.mult))
                link(dve.tensor_reduce(first[:, :], cand[:, :, :], AX.X, ALU.min))
                fb = first[:, :].rearrange("p (i a) -> p i a", a=1).broadcast_to(wide)
                dve.tensor_tensor(oh[:, :, :], emb, fb, ALU.is_equal).then_inc(c_oh, 1)
                dve.wait_ge(c_el, g + 1)
                link(dve.tensor_reduce(es[:, :], el[:, :, :], AX.X, ALU.add))
                link(dve.reciprocal(prob[:, :], es[:, :]))

            def c_slots(g):
                wide = [P, GTILES, NEXP]
                t = slice(g * GTILES, (g + 1) * GTILES)
                dve.wait_ge(c_rk, g + 1)
                rk = cc[:, 256:256 + GTILES * NEXP].rearrange("p (i n) -> p i n", n=NEXP)
                link(dve.tensor_tensor(rsel[:, :, :], rk, oh[:, :, :], ALU.mult))
                link(dve.tensor_reduce(rank[:, :], rsel[:, :, :], AX.X, ALU.add))
                link(dve.tensor_scalar(keep[:, :], rank[:, :], float(CAP), None, ALU.is_lt))
                link(dve.tensor_scalar(slot[:, :], first[:, :], float(CAP), float(NEXP * CAP), ALU.mult, ALU.add))
                link(dve.tensor_tensor(slot2[:, :], slot[:, :], rank[:, :], ALU.add))
                dve.tensor_tensor(wtok[:, t], prob[:, :], keep[:, :], ALU.mult).then_inc(c_wt, 1)
                link(dve.tensor_tensor(idf[:, :], slot2[:, :], toki[:, t], ALU.subtract))
                link(dve.tensor_tensor(idf2[:, :], idf[:, :], keep[:, :], ALU.mult))
                link(dve.tensor_tensor(sidx[:, t], idf2[:, :], toki[:, t], ALU.add))
                link(dve.tensor_reduce(gsum[:, :], oh[:, :, :].rearrange("p i n -> p n i"), AX.X, ALU.add))
                link(dve.tensor_tensor(seen[:, :], seen[:, :], gsum[:, :], ALU.add))
                link(dve.tensor_scalar(rowb[:, :, 3 * E:ROW], toki[:, t].rearrange("p (i a) -> p i a", a=1),
                                       float(-SLOTS - NOTOK), None, ALU.add))
                dve.tensor_copy(seenb[:, :], seen[:, :]).then_inc(c_rt, 1)

            for b in range(GB):
                a_stats(b)
            for b in range(GB):
                a_nm(b)
            dve.wait_ge(s_w0, NW0)
            dve.wait_ge(s_cth, 1)
            dve.wait_ge(s_pc, 7)
            link(dve.scalar_tensor_tensor(silc[:, :], cth[:, :], 1.0, ct[:, :], ALU.add, ALU.mult))
            dve.tensor_scalar(silc[:, :], silc[:, :], 0.5, None, ALU.mult).then_inc(s_silc, 1)
            dve.tensor_tensor(dconv[:, :, :], ident[:, :].rearrange("p (a c) -> p a c", a=1).broadcast_to([P, KCONV, P]),
                              cw[:, :].rearrange("p (k a) -> p k a", a=1).broadcast_to([P, KCONV, P]),
                              ALU.mult).then_inc(s_dc, 1)
            dve.wait_ge(s_mm0, 1)
            dve.tensor_copy(modT[:, 0, :], yp[:, 0:BATCH]).then_inc(s_pro, 1)
            dve.tensor_scalar(modT[:, 1, :], yp[:, BATCH:2 * BATCH], 1.0, None, ALU.add).then_inc(s_pro, 1)
            dve.tensor_copy(wdtp[:, :], yp[:, 2 * P:3 * P]).then_inc(s_pro, 1)
            dve.wait_ge(s_aexp, 2)
            for a, msk, inv in ((aneg, amsk, ainv), (amskT, amskT, ainvT)):
                link(dve.tensor_scalar(inv[:, :], a[:, :], -1.0, 1e-10, ALU.mult, ALU.add))
                link(dve.reciprocal(inv[:, :], inv[:, :]))
                link(dve.tensor_scalar(msk[:, :], a[:, :], SMALL_A, None, ALU.is_ge))
                link(dve.tensor_tensor(inv[:, :], inv[:, :], msk[:, :], ALU.mult))
            link(dve.tensor_scalar(small[:, :], amsk[:, :], 1.0, None, ALU.subtract))
            link(dve.tensor_reduce(smallest[:, :], small[:, :], AX.X, ALU.min))
            dve.tensor_scalar(aneg[:, :], aneg[:, :], -1.0, None, ALU.mult).then_inc(s_ainv, 1)
            dve.wait_ge(s_w, NW)
            dve.tensor_scalar(negd[:, :], dsk[:, :], -1.0, None, ALU.mult).then_inc(s_dc, 1)
            link(dve.tensor_copy(modr[:, :, :], cb[0][0:BATCH, :].rearrange("p (a c) -> p a c", a=4)))
            for a in (0, 3):
                link(dve.scalar_tensor_tensor(gabs[:, a, :], modr[:, a, :], -1.0, modr[:, a, :], ALU.mult, ALU.max))
                link(dve.tensor_scalar(gabs[:, a, :], gabs[:, a, :], 0.25, None, ALU.max))
                link(dve.tensor_scalar(gsgn[:, a, :], modr[:, a, :], 0.0, 2.0, ALU.is_ge, ALU.mult))
                link(dve.scalar_tensor_tensor(modr[:, a, :], gsgn[:, a, :], 1.0, gabs[:, a, :], ALU.subtract, ALU.mult))
            link(dve.tensor_scalar(modr[:, 2, :], modr[:, 2, :], 1.0, None, ALU.add))
            dve.tensor_copy(sel8, ident[0:BATCH, 0:BATCH].rearrange("p (b a) -> p b a", a=1).broadcast_to([BATCH, BATCH, P])
                            ).then_inc(s_mr, 1)
            for b in range(GB):
                a_u(b)
            dve.wait_ge(s_mm0, 2)
            dve.tensor_scalar(flag[:, :], yp[0:1, 3 * P:3 * P + 1], 2.0, None, ALU.mult).then_inc(s_flag, 1)
            dve.tensor_copy(wgt[:, :], yp[:, P:2 * P]).then_inc(s_pro, 1)
            for b in range(GB):
                a_gate(b)
            for b in range(GB):
                a_t1(b)
            for b in range(GB):
                a_base(b)
            for b in range(GB):
                a_split(b)
            for b in range(GB):
                a_dt(b)

            def fold_gates():
                dve.wait_ge(s_modb, 2 * BATCH)
                link(dve.tensor_scalar(wo[:, :], wo[:, :], 0.25, None, ALU.mult))
                dve.tensor_tensor(woga[:, :, :], wo[:, :].rearrange("p (a c) -> p a c", a=1).broadcast_to([P, BATCH, P]),
                                  gab, ALU.mult).then_inc(s_modg, 1)

            dve.wait_ge(s_flag, 1)
            smalls = dve.value_load(flag[0:1, 0:1])

            def small_a(g):
                step = [g * (GB + 2 * GB * NST)]

                def then(ins):
                    step[0] += 1
                    ins.then_inc(f_chain, 1)
                    dve.wait_ge(f_chain, step[0])

                with dve.If(smalls > 0):
                    dve.wait_ge(s_dt, GB * (g + 1))
                    dve.sem_inc(f_go, 1)
                    for j in range(GB):
                        then(dve.tensor_tensor(rem[:, j, :], dtb[:, g % 2, j, 0:SEQ], ub[:, j, 0:SEQ], ALU.mult))
                    for i in range(GB * NST):
                        n, j = divmod(i, GB)
                        k = g * GB * NST + i
                        dve.wait_ge(f_exp, k + 1)
                        then(dve.tensor_tensor_scan(lnx[:, j, :], expx[:, j, :], rem[:, j, :], 0.0, ALU.mult, ALU.add))
                        dve.wait_ge(f_cb, k + 1)
                        then(dve.tensor_tensor(lnx[:, j, :], lnx[:, j, :], cc[:, :], ALU.mult))
                        dve.scalar_tensor_tensor(base[:, g % 2, j, :], lnx[:, j, :], small[:, n:n + 1],
                                                 base[:, g % 2, j, :], ALU.mult, ALU.add).then_inc(f_used, 1)
                        dve.wait_ge(f_used, k + 1)

            for m in range(SCAN_AHEAD):
                b_scan_(m)
            for m in range(SLOTS_B):
                g, n = divmod(m, NST)
                if n == 0 and g < GROUPS:
                    small_a(g)
                if DVE_ORDER and 1 <= m <= STEPS:
                    b_mult(m - 1)
                if m + SCAN_AHEAD < STEPS:
                    b_scan_(m + SCAN_AHEAD)
                if m == 1:
                    fold_gates()
                if g and n == C_AT["yd"]:
                    c_yd_(g - 1)
                if not DVE_ORDER and 1 <= m <= STEPS:
                    b_mult(m - 1)
                if g and g < GROUPS:
                    for j in range(GB):
                        if n == C_AT["res"] + j:
                            c_res(GB * (g - 1) + j)
                        if n == C_AT["norm"] + j:
                            c_norm(GB * (g - 1) + j)
                        if n == C_AT["nm"] + j:
                            c_nm_(GB * (g - 1) + j)
                    if n == C_AT["router"]:
                        c_router(g - 1)
                    if n == C_AT["slots"]:
                        c_slots(g - 1)
                if g + 1 < GROUPS:
                    for j in range(GB):
                        b, p = GB * (g + 1) + j, n - A_APART * j
                        if p == A_AT["stats"]:
                            a_stats(b)
                        if p == A_AT["nm"]:
                            a_nm(b)
                        if p == A_AT["u"]:
                            a_u(b)
                        if p == A_AT["gate"]:
                            a_gate(b)
                        if p == A_AT["base"]:
                            a_base(b)
                        if p == A_AT["t1"]:
                            a_t1(b)
                        if p == A_AT["split"]:
                            a_split(b)
                    if n == DT_AT:
                        a_dt(GB * g + GB)
                        a_dt(GB * g + GB + 1)
            g = GROUPS - 1
            for b in range(GB * g, BATCH):
                c_res(b)
                c_norm(b)
            for b in range(GB * g, BATCH):
                c_nm_(b)
            c_router(g)
            c_slots(g)
            experts_vector(dve)

        @block.tensor
        def _(pe):
            def a_xT(b):
                pe.wait_ge(s_xn, b + 1)
                if b >= GB:
                    pe.wait_ge(s_abs, b)
                    pe.wait_ge(s_rel, b)
                for j in range(4):
                    last = pe.transpose(bank(b, 0)[:, j * P:(j + 1) * P], xn[:, 4 * (b % GB) + j, :], ident[:, :])
                last.then_inc(s_xT, 1)

            def a_proj(b, i, w, done):
                pe.matmul(bank(b, i), w, hT[:, b % GB, HPAD:], start=True, stop=True).then_inc(done, 1)

            def a_z(b):
                if b >= GB:
                    pe.wait_ge(s_ct3, b)
                pe.wait_ge(s_hT, b + 1)
                a_proj(b, 1, wz[:, :], s_z)

            def a_conv(b, taps=range(KCONV)):
                if taps[0] == 0:
                    pe.wait_ge(s_hT, b + 1)
                    pe.wait_ge(s_dc, 1)
                for k in taps:
                    last = pe.matmul(bank(b, 0)[:, :], dconv[:, k, :], hT[:, b % GB, k:k + SEQ],
                                     start=(k == 0), stop=(k == KCONV - 1))
                if k == KCONV - 1:
                    last.then_inc(s_cv, 1)

            def a_G(b):
                pe.wait_ge(s_gate, b + 1)
                a_proj(b, 1, wgt[:, :], s_G)

            def a_dtx(b):
                pe.wait_ge(s_u, b + 1)
                a_proj(b, 0, wdtp[:, :], s_xdt)

            def a_C(b):
                pe.wait_ge(s_Gr, b + 1)
                for t in range(4):
                    last = pe.matmul(bank(b, 1)[:, t * NST:(t + 1) * NST], hT[:, b % GB, HPAD + t * P:HPAD + (t + 1) * P],
                                     wct[:, :], start=True, stop=True)
                last.then_inc(s_C, 1)

            def a_cT(b):
                pe.wait_ge(s_cs, b + 1)
                v = bank(b, 1)[0:NPART * NST, 128:128 + SEQ // 2].bitcast(BF16)
                for t in range(4):
                    last = pe.transpose(v[:, t * P:(t + 1) * P],
                                        cs[:, 4 * (b % GB) + t, :, :].rearrange("p c n -> p (c n)"), identb[:, :])
                last.then_inc(s_cT, 1)

            def b_cb_(h):
                m, j = divmod(h, GB)
                g, n = divmod(m, NST)
                if n == 0 and j == 0:
                    pe.wait_ge(s_ct3, GB * (g + 1))
                if h == 0:
                    pe.wait_ge(s_modb, 2 * BATCH)
                if h >= 3:
                    k, i = divmod(h - 3, GB)
                    if on_pool(k):
                        pe.wait_ge(b_csb, GB * pool_before(k) + i + 1)
                    else:
                        pe.wait_ge(b_pd, GB * dve_before(k) + i + 1)
                pe.matmul(cb[h % 3], sel[:, n, :], ct3[:, g * GT + j * SEQ:g * GT + (j + 1) * SEQ],
                          start=True, stop=True).then_inc(b_cb, 1)

            def b_sum_(m):
                g, n = divmod(m, NST)
                if m == 0:
                    pe.wait_ge(s_diag, 1)
                    pe.wait_ge(s_pro, 4)
                if on_pool(m):
                    pe.wait_ge(b_pp, pool_before(m) + 1)
                    src = pp[:, pool_before(m) % RING_P, :]
                else:
                    pe.wait_ge(b_pd, GB * (dve_before(m) + 1))
                    src = pd[:, dve_before(m) % RING_P, :]
                place = SUM_PLACE[m] % NST
                if place == 0 and g:
                    pe.wait_ge(c_yd, g)
                for j in range(GB):
                    last = pe.matmul(yp[:, j * SEQ:(j + 1) * SEQ], diag[:, n, :], src[:, j * SEQ:(j + 1) * SEQ],
                                     start=(place == 0), stop=(place == NST - 1))
                last.then_inc(b_sum, 1)

            def c_out(b):
                pe.wait_ge(c_yg, b // GB + 1)
                if b == 0:
                    pe.wait_ge(s_modg, 1)
                if b == BATCH - 1:
                    pe.wait_ge(s_rel, BATCH)
                elif b % GB:
                    pe.wait_ge(c_x2, b)
                elif b:
                    pe.wait_ge(c_rt, b // GB)
                for i in range(4):
                    t = (4 * (b % GB) + i) * P
                    last = pe.matmul(cbank(b)[:, i * P:(i + 1) * P], yg[:, t:t + P], woga[:, b, :], start=True, stop=True)
                last.then_inc(c_o, 1)

            def c_trans(b):
                pe.wait_ge(c_h2, b + 1)
                pe.wait_ge(c_x2, GB * (b // GB + 1))
                if b % GB and b < BATCH - 1:
                    pe.wait_ge(c_h2T, b)
                for i in range(4):
                    last = pe.transpose(cbank(b)[:, i * P:(i + 1) * P], h2[:, 4 * (b % GB) + i, :], ident[:, :])
                last.then_inc(c_tr, 1)

            def c_logits(g):
                pe.wait_ge(c_h2T, GB * (g + 1))
                for i in range(GTILES):
                    last = pe.matmul(cc[:, i * NEXP:(i + 1) * NEXP], h2T[:, i * P:(i + 1) * P], gw[:, :],
                                     start=True, stop=True)
                last.then_inc(c_lg, 1)

            def c_rank(g):
                pe.wait_ge(c_oh, g + 1)
                if g:
                    pe.wait_ge(c_rt, g)
                rk = cc[:, 256:256 + GTILES * NEXP].rearrange("p (i n) -> p i n", n=NEXP)
                pe.matmul(rk, tri[:, :], oh[:, :, :], start=True, stop=False, skip_group_check=True)
                for i in range(GTILES - 1):
                    pe.matmul(rk[:, i + 1:, :], ones[:, :], oh[:, i:i + 1, :].broadcast_to([P, GTILES - 1 - i, NEXP]),
                              start=False, stop=False, skip_group_check=True)
                pe.matmul(rk, ones[:, :], seenb[:, :].rearrange("p (a n) -> p a n", a=1).broadcast_to([P, GTILES, NEXP]),
                          start=False, stop=True, skip_group_check=True).then_inc(c_rk, 1)

            zeros512 = av[:, 0, 0, 0:1].broadcast_to([P, SEQ])

            def keep_warm(n):
                for _ in range(n):
                    pe.matmul(cb[2][0:GTILES, :], halfneg[:, :], zeros512, start=True, stop=True)

            pe.wait_ge(s_pc, 7)
            keep_warm(WARM0)
            pe.wait_ge(s_w0, NW0)
            pe.wait_ge(s_silc, 1)
            pe.matmul(yp[:, 0:BATCH], wm[:, 0:P], silc[:, :], start=True, stop=True)
            pe.matmul(yp[:, BATCH:2 * BATCH], wm[:, P:2 * P], silc[:, :], start=True, stop=True)
            pe.matmul(cb[0][0:BATCH, :], silc[:, :], wm[:, 2 * P:6 * P], start=True, stop=True)
            pe.matmul(yp[:, 2 * P:3 * P], wp[:, :], wdt[:, :], start=True, stop=True).then_inc(s_mm0, 1)
            a_xT(0)
            a_xT(1)
            for b in range(GB):
                a_conv(b)
            pe.wait_ge(s_ainv, 1)
            pe.wait_ge(s_w, NW)
            pe.matmul(yp[0:1, 3 * P:3 * P + 1], smallest[:, :], halfneg[:, 0:1], start=True, stop=True)
            pe.matmul(yp[:, P:2 * P], wc[:, :], ainvT[:, :], start=True, stop=True).then_inc(s_mm0, 1)
            for b in range(GB):
                a_z(b)
            def p_modp(b):
                pe.wait_ge(s_mr, 1)
                if b >= 3:
                    pe.wait_ge(s_modb, 2 * (b - 2))
                pe.matmul(cb[b % 3], sel8[:, b, :], modr[:, :, :], start=True, stop=True).then_inc(s_modp, 1)

            for b in range(GB):
                a_dtx(b)
            for b in range(3):
                p_modp(b)
            pe.wait_ge(s_pro, 4)
            for b in range(GB):
                a_G(b)
            for b in range(3, BATCH):
                p_modp(b)
            for b in range(GB):
                a_C(b)
            pe.wait_ge(s_pc, 8)
            for b in range(GB):
                a_cT(b)
            pe.wait_ge(s_flag, 1)
            smalls = pe.value_load(flag[0:1, 0:1])

            def small_a(g):
                with pe.If(smalls > 0):
                    pe.wait_ge(s_ct3, GB * (g + 1))
                    pe.wait_ge(f_go, g + 1)
                    for i in range(GB * NST):
                        n, j = divmod(i, GB)
                        k = g * GB * NST + i
                        if k:
                            pe.wait_ge(f_used, k)
                        pe.matmul(cc[:, :], sel[:, n, :], ct3[:, g * GT + j * SEQ:g * GT + (j + 1) * SEQ],
                                  start=True, stop=True).then_inc(f_cb, 1)
                    pe.wait_ge(f_used, (g + 1) * GB * NST)

            b_cb_(0)
            for m in range(SLOTS_B):
                g, n = divmod(m, NST)
                if n == 0 and g < GROUPS:
                    small_a(g)
                hs, ks = [h for h in (GB * m - 1, GB * m) if 0 < h < GB * STEPS], sums_at(m)
                if PE_ORDER == 0:
                    for h in hs:
                        b_cb_(h)
                    for k in ks:
                        b_sum_(k)
                elif PE_ORDER == 1:
                    for h in hs[:1]:
                        b_cb_(h)
                    for k in ks:
                        b_sum_(k)
                    for h in hs[1:]:
                        b_cb_(h)
                elif PE_ORDER == 2:
                    for h in hs[:1]:
                        b_cb_(h)
                else:
                    for k in ks:
                        b_sum_(k)
                    for h in hs:
                        b_cb_(h)
                if g and g < GROUPS:
                    for j in range(GB):
                        if n == C_AT["out"] + j:
                            c_out(GB * (g - 1) + j)
                        if n == C_AT["trans"] + j:
                            c_trans(GB * (g - 1) + j)
                    if n == C_AT["logits"]:
                        c_logits(g - 1)
                    if n == C_AT["rank"]:
                        c_rank(g - 1)
                if g + 1 < GROUPS:
                    for j in range(GB):
                        b, p = GB * (g + 1) + j, n - A_APART * j
                        if p == A_AT["xT"]:
                            a_xT(b)
                        if p == A_AT["conv"]:
                            a_conv(b, range(CONV_CUT))
                        if p == A_AT["conv2"]:
                            a_conv(b, range(CONV_CUT, KCONV))
                        if p == A_AT["z"]:
                            a_z(b)
                        if p == A_AT["dtx"]:
                            a_dtx(b)
                        if p == A_AT["G"]:
                            a_G(b)
                        if p == A_AT["C"]:
                            a_C(b)
                        if p == A_AT["cT"]:
                            a_cT(b)
                if PE_ORDER == 2:
                    for k in ks:
                        b_sum_(k)
                    for h in hs[1:]:
                        b_cb_(h)
            g = GROUPS - 1
            for b in range(GB * g, BATCH):
                c_out(b)
            keep_warm(WARM1)
            for b in range(GB * g, BATCH):
                c_trans(b)
            c_logits(g)
            c_rank(g)
            keep_warm(WARM2)
            experts_tensor(pe)


def kernel(**inputs):
    import concourse.bacc as bacc
    from concourse.bass_utils import run_bass_kernel_spmd
    import ml_dtypes

    nc = bacc.Bacc("TRN2", target_bir_lowering=False, num_devices=1)
    a = {k: np.asarray(v) for k, v in inputs.items()}
    one = np.arange(NPART * NST)
    i = np.arange(P)
    arrays = {
        "x": a["L0_attn_x"], "w_zT": a["L0_attn_W_z"].T, "w_params": a["L0_attn_W_params"],
        "w_paramsT": a["L0_attn_W_params"].T, "conv_w": a["L0_attn_conv_w"], "w_dtT": a["L0_attn_W_dt"].T,
        "b_dt": a["L0_attn_b_dt"], "a_log": a["L0_attn_A_log"], "a_logT": a["L0_attn_A_log"].T,
        "d_skip": a["L0_attn_D"], "w_outT": a["L0_attn_W_out"].T, "gate_wT": a["L0_ffn_gate_w"].T,
        "w1": a["L0_ffn_w1"], "w2": a["L0_ffn_w2"], "cT": a["L0_c"].T, "wmod": a["L0_wmod"],
        "ident_in": np.eye(P, dtype=np.float32),
        "sel_in": np.ascontiguousarray(np.broadcast_to((one[:, None] % NST == np.arange(NST))[:, :, None],
                                                       (NPART * NST, NST, P))).astype(ml_dtypes.bfloat16),
        "tri_in": (i[:, None] < i[None, :]).astype(ml_dtypes.bfloat16),
        "em16_in": np.broadcast_to(np.arange(NEXP, dtype=np.float32) - NEXP, (P, NEXP)),
        "tok_in": (SLOTS + i[:, None] + P * np.arange(TILES)[None, :]).astype(np.float32),
    }
    arrays = {k: np.ascontiguousarray(v) for k, v in arrays.items()}
    args = [nc.dram_tensor(k, v.shape, mybir.dt.from_np(v.dtype), kind="ExternalInput").ap() for k, v in arrays.items()]
    out = nc.dram_tensor("out", (BATCH, SEQ, E), F32, kind="ExternalOutput").ap()
    build(nc, *args, out)
    r = run_bass_kernel_spmd(nc, [arrays], core_ids=[0])
    return r.results[0]["out"]
```

```python
from contextlib import ExitStack

import numpy as np

import concourse.bass as bass
from concourse import mybir

F32 = mybir.dt.float32
BF16 = mybir.dt.bfloat16
I32 = mybir.dt.int32
ALU = mybir.AluOpType
ACT = mybir.ActivationFunctionType
AX = mybir.AxisListType

P = 128
BATCH, SEQ, E = 8, 512, 128
TOK = BATCH * SEQ
TILES = TOK // P
NST, RANK, KCONV = 16, 64, 4
GB = 2
GROUPS = BATCH // GB
GT = GB * SEQ
GTILES = GT // P
NEXP, DFF = 16, 512
FC = DFF // P
CAP = int(1.25 * TOK / NEXP)
CAP += CAP % 2
SLOTS = NEXP * CAP
EPS = 1e-5
SMALL_A = 1e-5
FAST_A = 0.25
SEQ1 = SEQ + 1
HPAD = KCONV - 1
NPART = 3
STEPS = GROUPS * NST
ON_POOL = {2, 4, 6, 7, 8, 11, 13, 14}
A_APART = 6
A_AT = dict(stats=0, rstd=0, nm=0, xn=1, xT=1, hT=2, conv=2, z=2, thu=4, u=4, thz=4, gate=4, du=4, G=4, dtx=4,
            base=5, t1=5, soft=5, C=5, split=6, cT=6, ct3=8, conv2=3)
LN_AT, REM_AT, DT_AT = 12, 11, 14
C_AT = dict(yd=3, yg=3, out=5, res=6, norm=7, rstd=9, nm=9, xn=9, mod=10, trans=12, h2T=12, logits=13, router=15,
            expl=14, rank=14, slots=15, gates=15)
EXP_AHEAD = 1
C_AHEAD = 0
SUM_LAG = (4, 4, 4)
CONV_CUT = 2
WARM_START, WARM_PROJ, WARM_ROUTED = 4, 9, 17
RING_A, RING_K, RING_P = 3, 4, 3
ROW = 3 * E + 1
NOTOK = 1 << 20


def on_pool(m):
    return m % NST in ON_POOL


def pool_before(m):
    return sum(on_pool(i) for i in range(m))


def dve_before(m):
    return m - pool_before(m)


def sums_at(m):
    def lag(k):
        return SUM_LAG[0 if k % NST == 0 else 1 if on_pool(k) else 2]
    return [k for k in range(max(0, m - max(SUM_LAG)), min(STEPS, m)) if k + lag(k) == m]


SLOTS_B = STEPS + max(SUM_LAG)
POOL_STEPS = [m for m in range(STEPS) if on_pool(m)]
DVE_STEPS = [m for m in range(STEPS) if not on_pool(m)]
SUM_ORDER = [k for m in range(SLOTS_B) for k in sums_at(m)]
SUM_PLACE = {k: i for i, k in enumerate(SUM_ORDER)}


def build(nc, x, w_zT, w_params, w_paramsT, conv_w, w_dtT, b_dt, a_log, a_logT, d_skip, w_outT,
          gate_wT, w1, w2, cT, wmod, ident_in, sel_in, tri_in, em16_in, tok_in, out):
    disp = nc.dram_tensor("disp", [SLOTS + TOK, ROW], F32, kind="Internal").ap()
    with ExitStack() as ctx:
        def sb(name, shape, dt=F32):
            return ctx.enter_context(nc.sbuf_tensor(name, shape, dt))

        def ps(name, shape, dt=F32):
            return ctx.enter_context(nc.psum_tensor(name, shape, dt))

        def sem(name):
            return ctx.enter_context(nc.semaphore(name))

        ident = sb("ident", [P, P])
        identb = sb("identb", [P, P], BF16)
        sel = sb("sel", [NPART * NST, NST, P], BF16)
        tri = sb("tri", [P, P], BF16)
        ones = sb("ones", [P, P], BF16)
        em16 = sb("em16", [P, NEXP])
        toki = sb("toki", [P, TILES])
        wz = sb("wz", [P, P])
        wp = sb("wp", [RANK, P])
        wdt = sb("wdt", [RANK, P])
        wdtp = sb("wdtp", [P, P])
        wct = sb("wct", [P, NST])
        wc = sb("wc", [NST, P])
        wgt = sb("wgt", [P, P])
        cw = sb("cw", [P, KCONV])
        dconv = sb("dconv", [P, KCONV, P])
        bdt = sb("bdt", [P, 1])
        dsk = sb("dsk", [P, 1])
        negd = sb("negd", [P, 1])
        wo = sb("wo", [P, P])
        woga = sb("woga", [P, BATCH, P])
        gw = sb("gw", [P, NEXP])
        ct = sb("ct", [P, BATCH])
        cth = sb("cth", [P, BATCH])
        silc = sb("silc", [P, BATCH])
        modT = sb("modT", [P, 2, BATCH])
        modb = sb("modb", [P, BATCH, 3, P])
        al = sb("al", [P, NST])
        aneg = sb("aneg", [P, NST])
        amsk = sb("amsk", [P, NST])
        ainv = sb("ainv", [P, NST])
        alT = sb("alT", [NST, P])
        amskT = sb("amskT", [NST, P])
        ainvT = sb("ainvT", [NST, P])
        diag = sb("diag", [P, NST, P])
        small = sb("small", [P, NST])
        araw = sb("araw", [P, NST])
        tiny = sb("tiny", [P, NST])
        nottiny = sb("nottiny", [P, NST])
        slow = sb("slow", [P, NST])
        smallest = sb("smallest", [P, 1])
        flag = sb("flag", [1, 1], I32)
        halfneg = sb("halfneg", [P, GTILES])

        xs = sb("xs", [P, TILES, E])
        ct3 = sb("ct3", [NPART * NST, TOK], BF16)
        gate = sb("gate", [P, 2, GT])
        du = sb("du", [P, 2, GB * SEQ1])
        dtb = sb("dtb", [P, 2, GB, SEQ1])
        base = sb("base", [P, 2, GB, SEQ])
        st6 = sb("st6", [P, GTILES, 6])
        mv = sb("mv", [P, GTILES, 2])
        ve = sb("ve", [P, GTILES])
        rstd = sb("rstd", [P, GTILES])
        nmr = sb("nmr", [P, GTILES])
        xn = sb("xn", [P, GTILES, E])
        hT = sb("hT", [P, GB, HPAD + SEQ])
        wbuf = sb("wbuf", [P, 4, GT])
        th, expx, lnx, rem = (wbuf[:, i, :].rearrange("p (b t) -> p b t", b=GB) for i in range(4))
        ub = sb("ub", [P, GB, SEQ1])
        relx = th
        cs = sb("cs", [P, GTILES, NPART, NST], BF16)
        cr = sb("cr", [P, GTILES, NST])
        av = sb("av", [P, RING_A, GB, SEQ1])
        kv = sb("kv", [P, RING_K, GB * SEQ1])
        pd = sb("pd", [P, RING_P, GT])
        pp = sb("pp", [P, RING_P, GT])
        wm = pd[:, 0, 0:6 * P]
        csb = sb("csb", [P, 2, GT])
        gab = csb[:, 1, :].rearrange("p (b c) -> p b c", b=BATCH)
        yd = sb("yd", [P, GT])
        yg = sb("yg", [P, GT])
        h2T = yd
        sel8 = yg[0:BATCH, :].rearrange("p (b c) -> p b c", b=BATCH)
        modr, gabs, gsgn = (pd[0:BATCH, i, k:k + 4 * P].rearrange("p (a c) -> p a c", a=4)
                            for i, k in ((1, 0), (1, 4 * P), (2, 0)))
        st6c = sb("st6c", [P, GTILES, 6])
        mvc = sb("mvc", [P, GTILES, 2])
        vec = sb("vec", [P, GTILES])
        rstdc = sb("rstdc", [P, GTILES])
        nmrc = sb("nmrc", [P, GTILES])
        xn2 = yg[:, :].rearrange("p (i e) -> p i e", e=E)
        rowb = sb("rowb", [P, GTILES, ROW])
        h2, x2, wgb = rowb[:, :, 0:E], rowb[:, :, E:2 * E], rowb[:, :, 2 * E:3 * E]
        zero = rowb[:, :, :].rearrange("p i n -> p (i n)")
        mx = sb("mx", [P, GTILES])
        eq = sb("eq", [P, GTILES, NEXP])
        cand = sb("cand", [P, GTILES, NEXP])
        first = sb("first", [P, GTILES])
        oh = sb("oh", [P, GTILES, NEXP], BF16)
        dl = sb("dl", [P, GTILES, NEXP])
        el = sb("el", [P, GTILES, NEXP])
        es = sb("es", [P, GTILES])
        prob = sb("prob", [P, GTILES])
        seen = sb("seen", [P, NEXP])
        seenb = sb("seenb", [P, NEXP], BF16)
        gsum = sb("gsum", [P, NEXP])
        rsel = sb("rsel", [P, GTILES, NEXP])
        rank = sb("rank", [P, GTILES])
        keep = sb("keep", [P, GTILES])
        slot = sb("slot", [P, GTILES])
        slot2 = sb("slot2", [P, GTILES])
        idf = sb("idf", [P, GTILES])
        idf2 = sb("idf2", [P, GTILES])
        sidx = sb("sidx", [P, TILES], I32)
        wtok = sb("wtok", [P, TILES])
        cball = ps("cball", [P, 3 * SEQ])
        cb = [cball[:, i * SEQ:(i + 1) * SEQ] for i in range(3)]
        yp = ps("yp", [P, GT])
        ab = [ps(f"ab{i}", [P, SEQ]) for i in range(2)]
        cc = ps("cc", [P, SEQ])

        def bank(b, i):
            return (cc[:, :], yp[:, SEQ:])[i] if b == 1 else ab[i][:, :]

        def cbank(b):
            return ab[0] if b == BATCH - 1 else cc

        first_loaded = sem("first_loaded")
        weights_loaded = sem("weights_loaded")
        x_loaded = [sem(f"x_loaded{i}") for i in range(GROUPS)]
        zeros_set = sem("zeros_set")
        slots_zeroed = sem("slots_zeroed")
        consts_set = sem("consts_set")
        dve_chain = sem("dve_chain")
        tanh_c = sem("tanh_c")
        silu_c = sem("silu_c")
        pro_products = sem("pro_products")
        pro_copied = sem("pro_copied")
        mod_rows = sem("mod_rows")
        mod_spread = sem("mod_spread")
        mod_copied = sem("mod_copied")
        wout_ready = sem("wout_ready")
        exp_alog = sem("exp_alog")
        a_ready = sem("a_ready")
        conv_diag = sem("conv_diag")
        weight_diag = sem("weight_diag")
        flag_set = sem("flag_set")
        small_go = sem("small_go")
        small_decay = sem("small_decay")
        small_C = sem("small_C")
        small_used = sem("small_used")
        small_chain = sem("small_chain")
        var_a = sem("var_a")
        rstd_a = sem("rstd_a")
        nmean_a = sem("nmean_a")
        normed_a = sem("normed_a")
        turned_a = sem("turned_a")
        hT_ready = sem("hT_ready")
        z_ready = sem("z_ready")
        tanh_z = sem("tanh_z")
        gate_ready = sem("gate_ready")
        conv_ready = sem("conv_ready")
        tanh_u = sem("tanh_u")
        u_ready = sem("u_ready")
        du_ready = sem("du_ready")
        G_ready = sem("G_ready")
        G_used = sem("G_used")
        base_ready = sem("base_ready")
        dtx_ready = sem("dtx_ready")
        abs_ready = sem("abs_ready")
        expx_ready = sem("expx_ready")
        t1_ready = sem("t1_ready")
        relu_ready = sem("relu_ready")
        ln_ready = sem("ln_ready")
        rem_ready = sem("rem_ready")
        dt_ready = sem("dt_ready")
        C_ready = sem("C_ready")
        C_split = sem("C_split")
        C_turned = sem("C_turned")
        C_copied = sem("C_copied")
        decay_ready = sem("decay_ready")
        C_spread = sem("C_spread")
        C_spread_copied = sem("C_spread_copied")
        scanned = sem("scanned")
        dve_product = sem("dve_product")
        pool_product = sem("pool_product")
        summed = sem("summed")
        y_ready = sem("y_ready")
        gated = sem("gated")
        projected = sem("projected")
        x2_ready = sem("x2_ready")
        x2_stored = sem("x2_stored")
        var_c = sem("var_c")
        rstd_c = sem("rstd_c")
        nmean_c = sem("nmean_c")
        normed_c = sem("normed_c")
        scaled = sem("scaled")
        h2_last = sem("h2_last")
        h2_ready = sem("h2_ready")
        h2_turned = sem("h2_turned")
        h2T_ready = sem("h2T_ready")
        logits_ready = sem("logits_ready")
        dlogits_ready = sem("dlogits_ready")
        onehot_ready = sem("onehot_ready")
        explog_ready = sem("explog_ready")
        ranks_ready = sem("ranks_ready")
        token_weight = sem("token_weight")
        gates_ready = sem("gates_ready")
        routed = sem("routed")
        rows_stored = [sem(f"rows_stored{i}") for i in range(2)]

        CT = -(-CAP // P)
        CLAST = CAP - (CT - 1) * P
        WRING, RR, XR = 4, 5, 3
        w1s = wbuf[:, :, 0:DFF]
        w2s = wbuf[:, :, DFF:2 * DFF].rearrange("p w (f e) -> p w f e", f=FC)

        def over(t, *shape):
            n = int(np.prod(shape))
            names, old = " ".join("abcd"[:len(shape)]), " ".join("xyz"[:len(t.shape) - 1])
            flat = t.rearrange(f"p {old} -> p ({old})")
            return flat[:, 0:n].rearrange(f"p ({names}) -> p {names}", **dict(zip("abcd", shape)))

        rows_x, rows_a = over(xs[:, :, :], 3, CT, ROW), over(av[:, :, :, :], 2, CT, ROW)
        rows = [rows_x[:, i] for i in range(3)] + [rows_a[:, i] for i in range(2)]
        rowsT = over(pp[:, :, :], XR, CAP)
        hid = over(kv[:, :, :], XR, FC, CAP)
        res = over(pd[:, :, :], XR, CT, E)
        tokx = sb("tokx", [P, XR, CT], I32)
        w_landed = [sem(f"w_landed{i}") for i in range(WRING)]
        rows_landed = [sem(f"rows_landed{i}") for i in range(RR)]
        rows_turned = sem("rows_turned")
        rowsT_ready = sem("rowsT_ready")
        up_ready = sem("up_ready")
        hid_ready = sem("hid_ready")
        down_ready = sem("down_ready")
        dest_ready = sem("dest_ready")
        scaled_out = sem("scaled_out")
        res_ready = sem("res_ready")
        rows_out = [sem(f"rows_out{i}") for i in range(XR)]

        def experts_sync(sp):
            def load_w(e):
                if e >= WRING:
                    sp.wait_ge(down_ready, e - WRING + 1)
                sp.dma_start(w1s[:, e % WRING, :], w1[e]).then_inc(w_landed[e % WRING], 16)
                sp.dma_start(w2s[:, e % WRING, :, :], w2[e].rearrange("(f p) d -> p f d", p=P)
                             ).then_inc(w_landed[e % WRING], 16)

            def load_rows(e):
                if e >= RR:
                    sp.wait_ge(res_ready, e - RR + 1)
                r = disp[e * CAP:(e + 1) * CAP, :]
                sp.dma_start(rows[e % RR][:, 0:CT - 1, :], r[0:(CT - 1) * P, :].rearrange("(c p) e -> p c e", p=P)
                             ).then_inc(rows_landed[e % RR], 16)
                sp.dma_start(rows[e % RR][0:CLAST, CT - 1, :], r[(CT - 1) * P:CAP, :]
                             ).then_inc(rows_landed[e % RR], 16)

            sp.wait_ge(dt_ready, BATCH)
            for e in range(WRING):
                load_w(e)
            for k in range(2):
                sp.wait_ge(rows_stored[k], 16 * TILES // 2)
            for e in range(RR):
                load_rows(e)
            for e in range(NEXP):
                if e + WRING < NEXP:
                    load_w(e + WRING)
                if e + RR < NEXP:
                    load_rows(e + RR)
            for k in range(XR):
                sp.wait_ge(rows_out[k], 16 * CT * len(range(k, NEXP, XR)))

        def experts_scalar(act):
            for e in range(NEXP):
                for h in range(2):
                    act.wait_ge(up_ready, 2 * e + h + 1)
                    if e >= XR:
                        act.wait_ge(down_ready, e - XR + 1)
                    act.activation(hid[:, e % XR, 2 * h:2 * h + 2, :], FB[h],
                                   ACT.Gelu_apprx_tanh).then_inc(hid_ready, 1)

        def experts_vector(dve):
            def turn(e):
                dve.wait_ge(rows_turned, e + 1)
                if e >= XR:
                    dve.wait_ge(up_ready, 2 * (e - XR + 1))
                dve.tensor_copy(rowsT[:, e % XR, :], cc[:, 0:CAP]).then_inc(rowsT_ready, 1)

            turn(0)
            turn(1)
            for e in range(NEXP):
                if e + 2 < NEXP:
                    turn(e + 2)
                dve.wait_ge(rows_landed[e % RR], 32 * (e // RR + 1))
                if e >= XR:
                    dve.wait_ge(rows_out[e % XR], 16 * CT * (e // XR))
                t = [(slice(0, P), slice(0, CT - 1)), (slice(0, CLAST), slice(CT - 1, CT))]
                for p, c in t:
                    dve.tensor_scalar(tokx[p, e % XR, c], rows[e % RR][p, c, 3 * E:ROW].rearrange("p c a -> p (c a)"),
                                      float(NOTOK), None, ALU.add).then_inc(dest_ready, 1)
                dve.wait_ge(down_ready, e + 1)
                o = OB[e % 2].rearrange("p (c e) -> p c e", e=E)
                for p, c in t:
                    dve.tensor_tensor(res[p, e % XR, c, :], o[p, c, :], rows[e % RR][p, c, 2 * E:3 * E],
                                      ALU.mult).then_inc(scaled_out, 1)
                dve.wait_ge(scaled_out, 2 * e + 2)
                for p, c in t:
                    last = dve.tensor_tensor(res[p, e % XR, c, :], res[p, e % XR, c, :], rows[e % RR][p, c, E:2 * E],
                                             ALU.add)
                last.then_inc(res_ready, 1)

        def experts_gpsimd(pool):
            pool.wait_ge(x2_stored, 16 * BATCH)
            flat = out.rearrange("b t e -> (b t) e")
            for e in range(NEXP):
                pool.wait_ge(dest_ready, 2 * e + 2)
                pool.wait_ge(res_ready, e + 1)
                for c in range(CT):
                    n = P if c < CT - 1 else CLAST
                    pool.indirect_dma_start(flat, bass.IndirectOffsetOnAxis(ap=tokx[0:n, e % XR, c:c + 1], axis=0),
                                            res[0:n, e % XR, c, :], None, bounds_check=TOK - 1, oob_is_err=False
                                            ).then_inc(rows_out[e % XR], 16)

        FB = [t.rearrange("p (f t) -> p f t", f=2)[:, :, 0:CAP] for t in (yp[:, :], cball[:, 0:2 * SEQ])]
        OB = [cb[2][:, 0:CT * E], ab[1][:, 0:CT * E]]

        def experts_tensor(pe):
            def turn(e):
                pe.wait_ge(rows_landed[e % RR], 32 * (e // RR + 1))
                if e:
                    pe.wait_ge(rowsT_ready, e)
                for c in range(CT):
                    n = P if c < CT - 1 else CLAST
                    last = pe.transpose(cc[:, c * P:c * P + n], rows[e % RR][0:n, c, 0:E], ident[0:n, 0:n])
                last.then_inc(rows_turned, 1)

            def up(e):
                pe.wait_ge(rowsT_ready, e + 1)
                pe.wait_ge(w_landed[e % WRING], 32 * (e // WRING + 1))
                for h in range(2):
                    if e:
                        pe.wait_ge(hid_ready, 2 * (e - 1) + h + 1)
                    for f in (2 * h, 2 * h + 1):
                        last = pe.matmul(FB[h][:, f % 2, :], w1s[:, e % WRING, f * P:(f + 1) * P],
                                         rowsT[:, e % XR, :], start=True, stop=True)
                    last.then_inc(up_ready, 1)

            def down(e):
                pe.wait_ge(hid_ready, 2 * e + 2)
                if e >= 2:
                    pe.wait_ge(res_ready, e - 1)
                for c in range(CT):
                    n = P if c < CT - 1 else CLAST
                    for f in range(FC):
                        last = pe.matmul(OB[e % 2][0:n, c * E:(c + 1) * E], hid[:, e % XR, f, c * P:c * P + n],
                                         w2s[:, e % WRING, f, :], start=(f == 0), stop=(f == FC - 1))
                last.then_inc(down_ready, 1)

            pe.wait_ge(routed, GROUPS)
            turn(0)
            turn(1)
            up(0)
            for e in range(NEXP):
                if e + 1 < NEXP:
                    up(e + 1)
                if e + 2 < NEXP:
                    turn(e + 2)
                down(e)

        block = ctx.enter_context(nc.Block())
        loads_act = [
            (ct[:, :], cT), (ident[:, :], ident_in), (wm, wmod),
        ]
        loads_sp = [
            (cw[:, :], conv_w.rearrange("e a k -> e (a k)")), (wp[:, :], w_params[0:RANK, :]), (wdt[:, :], w_dtT),
            (al[:, :], a_log), (alT[:, :], a_logT),
        ]
        later_sp = [
            (wz[:, :], w_zT), (wc[:, :], w_params[RANK + NST:RANK + 2 * NST, :]),
            (wct[:, :], w_paramsT[:, RANK + NST:RANK + 2 * NST]),
            (bdt[:, :], b_dt.rearrange("(e a) -> e a", a=1)),
            (dsk[:, :], d_skip.rearrange("(e a) -> e a", a=1)),
            (sel[:, :, :], sel_in), (gw[:, :], gate_wT), (wo[:, :], w_outT),
            (tri[:, :], tri_in), (em16[:, :], em16_in), (toki[:, :], tok_in),
        ]
        NW0 = 16 * (len(loads_sp) + len(loads_act))
        NW = 16 * len(later_sp)

        @block.sync
        def _(sp):
            def load_x(g):
                sp.dma_start(xs[:, g * GTILES:(g + 1) * GTILES, :],
                             x[GB * g:GB * (g + 1)].rearrange("b (i p) e -> p (b i) e", p=P)).then_inc(x_loaded[g], 16)
            load_x(0)
            for dst, src in loads_sp:
                sp.dma_start(dst, src).then_inc(first_loaded, 16)
            for dst, src in later_sp:
                sp.dma_start(dst, src).then_inc(weights_loaded, 16)
            for g in range(1, GROUPS):
                load_x(g)
            sp.wait_ge(zeros_set, 1)
            sp.dma_start(disp[0:SLOTS, :].rearrange("(r p a) e -> p r (a e)", p=P, a=8),
                         zero.rearrange("p (r n) -> p r n", r=1).broadcast_to([P, SLOTS // (8 * P), 8 * ROW])
                         ).then_inc(slots_zeroed, 16)
            for g in range(GROUPS):
                for j in range(GB):
                    sp.wait_ge(x2_ready, GB * g + j + 1)
                    sp.dma_start(out[GB * g + j].rearrange("(i p) e -> p i e", p=P), x2[:, 4 * j:4 * j + 4, :]
                                 ).then_inc(x2_stored, 16)
            experts_sync(sp)

        @block.scalar
        def _(act):
            for dst, src in loads_act:
                act.dma_start(dst, src).then_inc(first_loaded, 16)

            def a_xn(b):
                act.wait_ge(nmean_a, b + 1)
                act.wait_ge(x_loaded[b // GB], 16)
                if b >= GB:
                    act.wait_ge(turned_a, b - GB + 1)
                for j in range(4):
                    o = 4 * (b % GB) + j
                    last = act.activation(xn[:, o, :], xs[:, 4 * b + j, :], ACT.Identity,
                                          scale=rstd[:, o:o + 1], bias=nmr[:, o:o + 1])
                last.then_inc(normed_a, 1)

            def c_xn_(b):
                act.wait_ge(nmean_c, b + 1)
                if b >= GB:
                    act.wait_ge(h2_ready, b - GB + 1)
                for j in range(4 * (b % GB), 4 * (b % GB) + 4):
                    last = act.activation(xn2[:, j, :], x2[:, j, :], ACT.Identity,
                                          scale=rstdc[:, j:j + 1], bias=nmrc[:, j:j + 1])
                last.then_inc(normed_c, 1)

            def c_gates(g):
                act.wait_ge(token_weight, g + 1)
                for j in range(GTILES):
                    act.activation(wgb[:, j, :], modb[:, GB * g + j // 4, 2, :], ACT.Copy,
                                   scale=wtok[:, g * GTILES + j:g * GTILES + j + 1]).then_inc(gates_ready, 1)

            def a_hT(b):
                act.wait_ge(turned_a, b + 1)
                if b == 0:
                    act.wait_ge(pro_copied, 2)
                if b >= GB:
                    act.wait_ge(C_ready, b - GB + 1)
                act.activation(hT[:, b % GB, HPAD:], bank(b, 0)[:, :], ACT.Identity,
                               scale=modT[:, 1, b:b + 1], bias=modT[:, 0, b:b + 1]).then_inc(hT_ready, 1)

            def a_thz(b):
                act.wait_ge(z_ready, b + 1)
                if b >= GB:
                    act.wait_ge(rem_ready, 2 * (b - GB) + 1)
                act.activation(expx[:, b % GB, :], bank(b, 1)[:, :], ACT.Tanh, scale=0.5).then_inc(tanh_z, 1)

            def a_thu(b):
                act.wait_ge(conv_ready, b + 1)
                if b >= GB:
                    act.wait_ge(dt_ready, b - GB + 1)
                act.activation(th[:, b % GB, :], bank(b, 0)[:, :], ACT.Tanh, scale=0.5).then_inc(tanh_u, 1)

            def a_soft(b):
                act.wait_ge(dtx_ready, b + 1)
                act.wait_ge(gate_ready, b + 1)
                act.activation(expx[:, b % GB, :], bank(b, 0)[:, :], ACT.Abs, bias=bdt[:, 0:1]).then_inc(abs_ready, 1)
                act.wait_ge(abs_ready, b + 1)
                act.activation(expx[:, b % GB, :], expx[:, b % GB, :], ACT.Exp, scale=-1.0).then_inc(expx_ready, 1)
                act.activation(relx[:, b % GB, :], bank(b, 0)[:, :], ACT.Relu, bias=bdt[:, 0:1]).then_inc(relu_ready, 1)

            def a_ln(b):
                act.wait_ge(expx_ready, b + 1)
                act.activation(lnx[:, b % GB, :], expx[:, b % GB, :], ACT.Ln, bias=1.0).then_inc(ln_ready, 1)

            def a_ct3(b):
                act.wait_ge(C_turned, b + 1)
                act.activation(ct3[:, b * SEQ:(b + 1) * SEQ], bank(b, 1)[0:NPART * NST, 128:128 + SEQ // 2].bitcast(BF16),
                               ACT.Copy).then_inc(C_copied, 1)

            def b_step(m):
                g, n = divmod(m, NST)
                if n == 0:
                    act.wait_ge(dt_ready, GB * (g + 1))
                if m >= RING_A:
                    act.wait_ge(scanned, m - RING_A + 1)
                act.activation(av[:, m % RING_A, :, 1:SEQ1], dtb[:, g % 2, :, 0:SEQ], ACT.Exp,
                               scale=aneg[:, n:n + 1]).then_inc(decay_ready, 1)

            def b_copy(m):
                if on_pool(m):
                    k = pool_before(m)
                    if k == 0:
                        act.wait_ge(wout_ready, 1)
                    if k >= 2:
                        act.wait_ge(pool_product, k - 1)
                    for j in range(GB):
                        act.wait_ge(C_spread, GB * m + j + 1)
                        act.activation(csb[:, k % 2, j * SEQ:(j + 1) * SEQ], cb[(GB * m + j) % 3],
                                       ACT.Copy).then_inc(C_spread_copied, 1)

            def c_h2Tcopy(b):
                act.wait_ge(h2_turned, b + 1)
                if b >= GB:
                    act.wait_ge(logits_ready, b // GB)
                act.activation(h2T[:, b % GB * SEQ:(b % GB + 1) * SEQ], cbank(b)[:, :], ACT.Copy).then_inc(h2T_ready, 1)

            def c_expl(g):
                act.wait_ge(dlogits_ready, g + 1)
                act.activation(el[:, :, :], dl[:, :, :], ACT.Exp).then_inc(explog_ready, 1)

            def p_modb(b):
                act.wait_ge(mod_spread, b + 1)
                act.activation(gab[:, b, :], cb[b % 3][:, 0:P], ACT.Copy).then_inc(mod_copied, 1)
                act.activation(modb[:, b, :, :], cb[b % 3][:, P:4 * P].rearrange("p (a e) -> p a e", a=3),
                               ACT.Copy).then_inc(mod_copied, 1)

            a_xn(0)
            act.wait_ge(first_loaded, NW0)
            act.activation(cth[:, :], ct[:, :], ACT.Tanh, scale=0.5).then_inc(tanh_c, 1)
            a_xn(1)
            act.activation(aneg[:, :], al[:, :], ACT.Exp).then_inc(exp_alog, 1)
            act.activation(amskT[:, :], alT[:, :], ACT.Exp).then_inc(exp_alog, 1)
            for b in range(GB):
                a_hT(b)
            act.wait_ge(weights_loaded, NW)
            for b in range(GB):
                a_thu(b)
            for b in range(GB):
                a_thz(b)
            for b in range(3):
                p_modb(b)
            for b in range(GB):
                a_soft(b)
            for b in range(3, BATCH):
                p_modb(b)
            for b in range(GB):
                a_ln(b)
            for b in range(GB):
                a_ct3(b)
            act.wait_ge(flag_set, 1)
            smalls = act.value_load(flag[0:1, 0:1])

            def small_a(g):
                with act.If(smalls > 0):
                    act.wait_ge(dt_ready, GB * (g + 1))
                    act.wait_ge(small_go, g + 1)
                    for i in range(GB * NST):
                        n, j = divmod(i, GB)
                        k = g * GB * NST + i
                        if k >= GB:
                            act.wait_ge(small_used, k - GB + 1)
                        act.activation(expx[:, j, :], dtb[:, g % 2, j, 0:SEQ], ACT.Exp,
                                       scale=aneg[:, n:n + 1]).then_inc(small_decay, 1)
                    act.wait_ge(small_used, (g + 1) * GB * NST)

            for m in range(EXP_AHEAD):
                b_step(m)
            for m in range(SLOTS_B):
                g, n = divmod(m, NST)
                if n == 0 and g < GROUPS:
                    small_a(g)
                if m + EXP_AHEAD < STEPS:
                    b_step(m + EXP_AHEAD)
                if 1 <= m <= STEPS:
                    b_copy(m - 1)
                if g + 1 < GROUPS:
                    for j in range(GB):
                        b, p = GB * (g + 1) + j, n - A_APART * j
                        if p == A_AT["xn"]:
                            a_xn(b)
                        if p == A_AT["hT"]:
                            a_hT(b)
                        if p == A_AT["thu"]:
                            a_thu(b)
                        if p == A_AT["thz"]:
                            a_thz(b)
                        if p == A_AT["soft"]:
                            a_soft(b)
                        if p == A_AT["ct3"]:
                            a_ct3(b)
                    if n == LN_AT:
                        a_ln(GB * g + GB)
                        a_ln(GB * g + GB + 1)
                if g and g < GROUPS:
                    for j in range(GB):
                        if n == C_AT["xn"] + j:
                            c_xn_(GB * (g - 1) + j)
                        if n == C_AT["h2T"] + j:
                            c_h2Tcopy(GB * (g - 1) + j)
                    if n == C_AT["expl"]:
                        c_expl(g - 1)
                    if n == C_AT["gates"]:
                        c_gates(g - 1)
            c_xn_(BATCH - 2)
            c_xn_(BATCH - 1)
            c_h2Tcopy(BATCH - 2)
            c_h2Tcopy(BATCH - 1)
            c_expl(GROUPS - 1)
            c_gates(GROUPS - 1)
            experts_scalar(act)

        @block.gpsimd
        def _(pool):
            pool.memset(halfneg[:, :], -0.5).then_inc(consts_set, 1)
            pool.memset(du[:, :, :], 0.0).then_inc(consts_set, 1)
            pool.memset(ones[:, :], 1.0).then_inc(consts_set, 1)
            pool.memset(hT[:, :, 0:HPAD], 0.0).then_inc(consts_set, 1)
            pool.memset(av[:, :, :, 0:1], 0.0).then_inc(consts_set, 1)
            pool.memset(seen[:, :], 0.0).then_inc(consts_set, 1)
            pool.memset(seenb[:, :], 0.0).then_inc(consts_set, 1)

            def a_rstd(b):
                pool.wait_ge(var_a, b + 1)
                if b >= GB:
                    pool.wait_ge(normed_a, b - GB + 1)
                j = slice(4 * (b % GB), 4 * (b % GB) + 4)
                pool.tensor_tensor(rstd[:, j], ve[:, j], halfneg[:, 0:4], ALU.pow).then_inc(rstd_a, 1)

            def a_du(b):
                pool.wait_ge(u_ready, b + 1)
                if b >= 2 * GB:
                    pool.wait_ge(scanned, (b // GB - 1) * NST)
                d, u = du[:, b // GB % 2, (b % GB) * SEQ1:(b % GB + 1) * SEQ1], ub[:, b % GB, :]
                pool.tensor_copy(d[:, 1:2], u[:, 0:1]).then_inc(du_ready, 1)
                pool.tensor_tensor(d[:, 2:SEQ1], u[:, 1:SEQ], u[:, 0:SEQ - 1], ALU.subtract).then_inc(du_ready, 1)

            def a_rem(b):
                r, t = rem[:, b % GB, :], expx[:, b % GB, :]
                pool.wait_ge(t1_ready, b + 1)
                pool.tensor_tensor(r, t, r, ALU.subtract).then_inc(rem_ready, 1)
                pool.wait_ge(rem_ready, 2 * b + 1)
                pool.wait_ge(ln_ready, b + 1)
                pool.tensor_tensor(r, r, lnx[:, b % GB, :], ALU.add).then_inc(rem_ready, 1)

            def b_mult(m):
                if on_pool(m):
                    k = pool_before(m)
                    pool.wait_ge(C_spread_copied, GB * (k + 1))
                    pool.wait_ge(scanned, m + 1)
                    if k >= RING_P:
                        pool.wait_ge(summed, SUM_PLACE[POOL_STEPS[k - RING_P]] + 1)
                    pool.tensor_tensor(pp[:, k % RING_P, :].rearrange("p (b t) -> p b t", b=GB),
                                       kv[:, m % RING_K, :].rearrange("p (b t) -> p b t", b=GB)[:, :, 1:SEQ1],
                                       csb[:, k % 2, :].rearrange("p (b t) -> p b t", b=GB),
                                       ALU.mult).then_inc(pool_product, 1)

            def c_yg_(g):
                pool.wait_ge(y_ready, g + 1)
                if g:
                    pool.wait_ge(h2_ready, GB * g)
                pool.tensor_tensor(yg[:, :], yd[:, :], gate[:, g % 2, :], ALU.mult).then_inc(gated, 1)

            def c_rstd_(b):
                t = slice(4 * (b % GB), 4 * (b % GB) + 4)
                pool.wait_ge(var_c, b + 1)
                if b >= GB:
                    pool.wait_ge(normed_c, b - GB + 1)
                pool.tensor_tensor(rstdc[:, t], vec[:, t], halfneg[:, t], ALU.pow).then_inc(rstd_c, 1)

            def c_mod(b, add):
                j = slice(4 * (b % GB), 4 * (b % GB) + 4)
                if not add:
                    pool.wait_ge(normed_c, b + 1)
                    pool.wait_ge(wout_ready, 1)
                    pool.tensor_tensor(xn2[:, j, :], xn2[:, j, :], modb[:, b, 1:2, :].broadcast_to([P, 4, P]),
                                       ALU.mult).then_inc(scaled, 1)
                else:
                    pool.wait_ge(scaled, b + 1)
                    pool.tensor_tensor(h2[:, j, :], xn2[:, j, :], modb[:, b, 0:1, :].broadcast_to([P, 4, P]),
                                       ALU.add).then_inc(h2_ready, 1)

            def c_scatter(g, tiles):
                pool.wait_ge(routed, g + 1)
                if g == 0:
                    pool.wait_ge(slots_zeroed, 16)
                if g == GROUPS - 1:
                    pool.wait_ge(h2_last, 1)
                for j in tiles:
                    pool.wait_ge(gates_ready, GTILES * g + j + 1)
                    k = g * GTILES + j
                    pool.indirect_dma_start(disp, bass.IndirectOffsetOnAxis(ap=sidx[:, k:k + 1], axis=0),
                                            rowb[:, j, :], None).then_inc(rows_stored[g % 2], 16)

            pool.wait_ge(consts_set, 7)
            for b in range(GB):
                a_rstd(b)
            pool.memset(zero, 0.0).then_inc(zeros_set, 1)
            pool.wait_ge(first_loaded, NW0)
            pool.tensor_copy(identb[:, :], ident[:, :]).then_inc(consts_set, 1)
            pool.wait_ge(a_ready, 1)
            pool.tensor_tensor(diag[:, :, :], ident[:, :].rearrange("p (a c) -> p a c", a=1).broadcast_to([P, NST, P]),
                               ainv[:, :].rearrange("p (k a) -> p k a", a=1).broadcast_to([P, NST, P]),
                               ALU.mult).then_inc(weight_diag, 1)
            for b in range(GB):
                a_du(b)
            for b in range(GB):
                a_rem(b)
            for m in range(SLOTS_B):
                g, n = divmod(m, NST)
                if g and g < GROUPS:
                    if n == C_AT["yg"]:
                        c_yg_(g - 1)
                    for j in range(GB):
                        if n == C_AT["rstd"] + j:
                            c_rstd_(GB * (g - 1) + j)
                if m >= 1 and m <= STEPS:
                    b_mult(m - 1)
                if g and g < GROUPS:
                    for j in range(GB):
                        if n == C_AT["mod"] + j:
                            c_mod(GB * (g - 1) + j, False)
                            c_mod(GB * (g - 1) + j, True)
                if 2 <= g < GROUPS and n < 2:
                    c_scatter(g - 2, range(4 * n, 4 * n + 4))
                if g + 1 < GROUPS:
                    for j in range(GB):
                        b, p = GB * (g + 1) + j, n - A_APART * j
                        if p == A_AT["rstd"]:
                            a_rstd(b)
                        if p == A_AT["du"]:
                            a_du(b)
                    if n == REM_AT:
                        a_rem(GB * g + GB)
                        a_rem(GB * g + GB + 1)
            g = GROUPS - 1
            c_scatter(g - 1, range(GTILES))
            for b in range(GB * g, BATCH):
                c_rstd_(b)
            c_mod(GB * g, False)
            c_mod(GB * g, True)
            c_scatter(g, range(GTILES))
            experts_gpsimd(pool)

        @block.vector
        def _(dve):
            chain = [0]

            def link(ins):
                chain[0] += 1
                ins.then_inc(dve_chain, 1)
                dve.wait_ge(dve_chain, chain[0])

            def a_stats(b):
                dve.wait_ge(x_loaded[b // GB], 16)
                if b >= GB:
                    dve.wait_ge(rstd_a, b - GB + 1)
                    dve.wait_ge(normed_a, b - GB + 1)
                o = 4 * (b % GB)
                for j in range(4):
                    last = dve.bn_stats(st6[:, o + j, :], xs[:, 4 * b + j, :])
                link(last)
                for j in range(4):
                    last = dve.bn_aggr(mv[:, o + j, :], st6[:, o + j, :])
                link(last)
                dve.tensor_scalar(ve[:, o:o + 4], mv[:, o:o + 4, 1], EPS, None, ALU.add).then_inc(var_a, 1)

            def a_nm(b):
                dve.wait_ge(rstd_a, b + 1)
                if b >= GB:
                    dve.wait_ge(normed_a, b - GB + 1)
                j = slice(4 * (b % GB), 4 * (b % GB) + 4)
                dve.scalar_tensor_tensor(nmr[:, j], mv[:, j, 0], -1.0, rstd[:, j], ALU.mult, ALU.mult).then_inc(nmean_a, 1)

            def a_gate(b):
                dve.wait_ge(tanh_z, b + 1)
                g, j = divmod(b, GB)
                if g >= 2:
                    dve.wait_ge(gated, g - 1)
                dve.scalar_tensor_tensor(gate[:, g % 2, j * SEQ:(j + 1) * SEQ], expx[:, j, :], 1.0,
                                         bank(b, 1)[:, :], ALU.add, ALU.mult).then_inc(gate_ready, 1)

            def a_u(b):
                dve.wait_ge(tanh_u, b + 1)
                j = b % GB
                if b >= GB:
                    dve.wait_ge(du_ready, 2 * (b - GB + 1))
                    dve.wait_ge(base_ready, b - GB + 1)
                link(dve.scalar_tensor_tensor(ub[:, j, 1:SEQ1], th[:, j, :], 1.0, bank(b, 0)[:, :], ALU.add, ALU.mult))
                dve.tensor_copy(ub[:, j, 0:1], ub[:, j, 1:2]).then_inc(u_ready, 1)

            def a_base(b):
                dve.wait_ge(G_ready, b + 1)
                dve.wait_ge(u_ready, b + 1)
                g, j = divmod(b, GB)
                if g >= 2:
                    dve.wait_ge(y_ready, g - 1)
                dve.tensor_tensor(base[:, g % 2, j, :], bank(b, 1)[:, :], ub[:, j, 0:SEQ], ALU.mult).then_inc(G_used, 1)
                dve.wait_ge(G_used, b + 1)
                dve.scalar_tensor_tensor(base[:, g % 2, j, :], ub[:, j, 1:SEQ1], negd[:, 0:1],
                                         base[:, g % 2, j, :], ALU.mult, ALU.add).then_inc(base_ready, 1)

            def a_t1(b):
                dve.wait_ge(expx_ready, b + 1)
                dve.tensor_scalar(rem[:, b % GB, :], expx[:, b % GB, :], 1.0, -1.0, ALU.add, ALU.add).then_inc(t1_ready, 1)

            def a_dt(b):
                dve.wait_ge(rem_ready, 2 * b + 2)
                dve.wait_ge(relu_ready, b + 1)
                g, j = divmod(b, GB)
                if g >= 2:
                    dve.wait_ge(decay_ready, (g - 1) * NST)
                link(dve.tensor_tensor(dtb[:, g % 2, j, 1:SEQ1], rem[:, j, :], relx[:, j, :], ALU.add))
                dve.tensor_copy(dtb[:, g % 2, j, 0:1], dtb[:, g % 2, j, 1:2]).then_inc(dt_ready, 1)

            def a_split(b):
                dve.wait_ge(C_ready, b + 1)
                if b >= GB:
                    dve.wait_ge(C_turned, b - GB + 1)
                j = slice(4 * (b % GB), 4 * (b % GB) + 4)
                c = bank(b, 1)[:, 0:4 * NST].rearrange("p (i n) -> p i n", n=NST)
                link(dve.tensor_copy(cs[:, j, 0, :], c))
                link(dve.tensor_tensor(cr[:, j, :], c, cs[:, j, 0, :], ALU.subtract))
                link(dve.tensor_copy(cs[:, j, 1, :], cr[:, j, :]))
                dve.tensor_tensor(cs[:, j, 2, :], cr[:, j, :], cs[:, j, 1, :], ALU.subtract).then_inc(C_split, 1)

            def b_scan_(m):
                g, n = divmod(m, NST)
                dve.wait_ge(decay_ready, m + 1)
                if n == 0:
                    dve.wait_ge(du_ready, 2 * GB * (g + 1))
                if m >= RING_K:
                    k = m - RING_K
                    if on_pool(k):
                        dve.wait_ge(pool_product, pool_before(k) + 1)
                    else:
                        dve.wait_ge(dve_product, GB * (dve_before(k) + 1))
                dve.tensor_tensor_scan(kv[:, m % RING_K, :], du[:, g % 2, :],
                                       av[:, m % RING_A, :, :].rearrange("p b t -> p (b t)"), 0.0,
                                       ALU.add, ALU.mult).then_inc(scanned, 1)

            def b_mult(m):
                if on_pool(m):
                    return
                k = dve_before(m)
                dve.wait_ge(scanned, m + 1)
                if k >= RING_P:
                    dve.wait_ge(summed, SUM_PLACE[DVE_STEPS[k - RING_P]] + 1)
                for j in range(GB):
                    dve.wait_ge(C_spread, GB * m + j + 1)
                    dve.tensor_tensor(pd[:, k % RING_P, j * SEQ:(j + 1) * SEQ],
                                      kv[:, m % RING_K, j * SEQ1 + 1:(j + 1) * SEQ1],
                                      cb[(GB * m + j) % 3], ALU.mult).then_inc(dve_product, 1)

            def c_yd_(g):
                dve.wait_ge(summed, NST * (g + 1))
                if g:
                    dve.wait_ge(gated, g)
                    dve.wait_ge(logits_ready, g)
                dve.tensor_tensor(yd[:, :], yp[:, :], base[:, g % 2, :, :].rearrange("p b t -> p (b t)"),
                                  ALU.subtract).then_inc(y_ready, 1)

            def c_res(b):
                dve.wait_ge(projected, b + 1)
                if b == 0:
                    dve.wait_ge(slots_zeroed, 16)
                if b >= GB:
                    g = b // GB - 1
                    dve.wait_ge(rows_stored[g % 2], 16 * GTILES * (g // 2 + 1))
                    dve.wait_ge(x2_stored, 16 * GB * (g + 1))
                j = slice(4 * (b % GB), 4 * (b % GB) + 4)
                dve.tensor_tensor(x2[:, j, :], cbank(b)[:, :].rearrange("p (i e) -> p i e", e=E), xs[:, 4 * b:4 * b + 4, :],
                                  ALU.add).then_inc(x2_ready, 1)

            def c_norm(b):
                t = slice(4 * (b % GB), 4 * (b % GB) + 4)
                dve.wait_ge(x2_ready, b + 1)
                if b >= GB:
                    dve.wait_ge(normed_c, b - GB + 1)
                for j in range(t.start, t.stop):
                    last = dve.bn_stats(st6c[:, j, :], x2[:, j, :])
                link(last)
                for j in range(t.start, t.stop):
                    last = dve.bn_aggr(mvc[:, j, :], st6c[:, j, :])
                link(last)
                dve.tensor_scalar(vec[:, t], mvc[:, t, 1], EPS, None, ALU.add).then_inc(var_c, 1)

            def c_nm_(b):
                t = slice(4 * (b % GB), 4 * (b % GB) + 4)
                dve.wait_ge(rstd_c, b + 1)
                dve.scalar_tensor_tensor(nmrc[:, t], mvc[:, t, 0], -1.0, rstdc[:, t], ALU.mult, ALU.mult).then_inc(nmean_c, 1)

            def c_router(g):
                dve.wait_ge(logits_ready, g + 1)
                if g:
                    dve.wait_ge(routed, g)
                    dve.wait_ge(ranks_ready, g)
                lg = cc[:, 0:GTILES * NEXP].rearrange("p (i n) -> p i n", n=NEXP)
                wide = [P, GTILES, NEXP]
                link(dve.tensor_reduce(mx[:, :], lg, AX.X, ALU.max))
                mxb = mx[:, :].rearrange("p (i a) -> p i a", a=1).broadcast_to(wide)
                link(dve.tensor_tensor(dl[:, :, :], lg, mxb, ALU.subtract))
                dve.tensor_scalar(eq[:, :, :], dl[:, :, :], 0.0, None, ALU.is_ge).then_inc(dlogits_ready, 1)
                dve.wait_ge(dlogits_ready, g + 1)
                emb = em16[:, :].rearrange("p (a n) -> p a n", a=1).broadcast_to(wide)
                link(dve.tensor_tensor(cand[:, :, :], eq[:, :, :], emb, ALU.mult))
                link(dve.tensor_reduce(first[:, :], cand[:, :, :], AX.X, ALU.min))
                fb = first[:, :].rearrange("p (i a) -> p i a", a=1).broadcast_to(wide)
                dve.tensor_tensor(oh[:, :, :], emb, fb, ALU.is_equal).then_inc(onehot_ready, 1)
                dve.wait_ge(explog_ready, g + 1)
                link(dve.tensor_reduce(es[:, :], el[:, :, :], AX.X, ALU.add))
                link(dve.reciprocal(prob[:, :], es[:, :]))

            def c_slots(g):
                wide = [P, GTILES, NEXP]
                t = slice(g * GTILES, (g + 1) * GTILES)
                dve.wait_ge(ranks_ready, g + 1)
                rk = cc[:, 256:256 + GTILES * NEXP].rearrange("p (i n) -> p i n", n=NEXP)
                link(dve.tensor_tensor(rsel[:, :, :], rk, oh[:, :, :], ALU.mult))
                link(dve.tensor_reduce(rank[:, :], rsel[:, :, :], AX.X, ALU.add))
                link(dve.tensor_scalar(keep[:, :], rank[:, :], float(CAP), None, ALU.is_lt))
                link(dve.tensor_scalar(slot[:, :], first[:, :], float(CAP), float(NEXP * CAP), ALU.mult, ALU.add))
                link(dve.tensor_tensor(slot2[:, :], slot[:, :], rank[:, :], ALU.add))
                dve.tensor_tensor(wtok[:, t], prob[:, :], keep[:, :], ALU.mult).then_inc(token_weight, 1)
                link(dve.tensor_tensor(idf[:, :], slot2[:, :], toki[:, t], ALU.subtract))
                link(dve.tensor_tensor(idf2[:, :], idf[:, :], keep[:, :], ALU.mult))
                link(dve.tensor_tensor(sidx[:, t], idf2[:, :], toki[:, t], ALU.add))
                last = dve.tensor_scalar(rowb[:, :, 3 * E:ROW], toki[:, t].rearrange("p (i a) -> p i a", a=1),
                                         float(-SLOTS - NOTOK), None, ALU.add)
                if g + 1 < GROUPS:
                    link(last)
                    link(dve.tensor_reduce(gsum[:, :], oh[:, :, :].rearrange("p i n -> p n i"), AX.X, ALU.add))
                    link(dve.tensor_tensor(seen[:, :], seen[:, :], gsum[:, :], ALU.add))
                    last = dve.tensor_copy(seenb[:, :], seen[:, :])
                last.then_inc(routed, 1)

            for b in range(GB):
                a_stats(b)
            for b in range(GB):
                a_nm(b)
            dve.wait_ge(first_loaded, NW0)
            dve.wait_ge(tanh_c, 1)
            dve.wait_ge(consts_set, 7)
            link(dve.scalar_tensor_tensor(silc[:, :], cth[:, :], 1.0, ct[:, :], ALU.add, ALU.mult))
            dve.tensor_scalar(silc[:, :], silc[:, :], 0.5, None, ALU.mult).then_inc(silu_c, 1)
            dve.tensor_tensor(dconv[:, :, :], ident[:, :].rearrange("p (a c) -> p a c", a=1).broadcast_to([P, KCONV, P]),
                              cw[:, :].rearrange("p (k a) -> p k a", a=1).broadcast_to([P, KCONV, P]),
                              ALU.mult).then_inc(conv_diag, 1)
            dve.wait_ge(pro_products, 1)
            dve.tensor_copy(modT[:, 0, :], yp[:, 0:BATCH]).then_inc(pro_copied, 1)
            dve.tensor_scalar(modT[:, 1, :], yp[:, BATCH:2 * BATCH], 1.0, None, ALU.add).then_inc(pro_copied, 1)
            dve.tensor_copy(wdtp[:, :], yp[:, 2 * P:3 * P]).then_inc(pro_copied, 1)
            dve.wait_ge(exp_alog, 2)
            for a, msk, inv in ((aneg, amsk, ainv), (amskT, amskT, ainvT)):
                link(dve.tensor_scalar(inv[:, :], a[:, :], -1.0, 1e-10, ALU.mult, ALU.add))
                link(dve.reciprocal(inv[:, :], inv[:, :]))
                if inv is ainv:
                    dve.tensor_copy(araw[:, :], inv[:, :])
                    dve.tensor_scalar(tiny[:, :], a[:, :], SMALL_A, None, ALU.is_lt)
                    dve.tensor_scalar(nottiny[:, :], a[:, :], SMALL_A, None, ALU.is_ge)
                link(dve.tensor_scalar(msk[:, :], a[:, :], FAST_A, None, ALU.is_ge))
                link(dve.tensor_tensor(inv[:, :], inv[:, :], msk[:, :], ALU.mult))
            link(dve.tensor_scalar(small[:, :], amsk[:, :], 1.0, None, ALU.subtract))
            link(dve.tensor_reduce(smallest[:, :], small[:, :], AX.X, ALU.min))
            dve.tensor_scalar(aneg[:, :], aneg[:, :], -1.0, None, ALU.mult).then_inc(a_ready, 1)
            dve.wait_ge(weights_loaded, NW)
            dve.tensor_scalar(negd[:, :], dsk[:, :], -1.0, None, ALU.mult).then_inc(conv_diag, 1)
            link(dve.tensor_copy(modr[:, :, :], cb[0][0:BATCH, :].rearrange("p (a c) -> p a c", a=4)))
            for a in (0, 3):
                link(dve.scalar_tensor_tensor(gabs[:, a, :], modr[:, a, :], -1.0, modr[:, a, :], ALU.mult, ALU.max))
                link(dve.tensor_scalar(gabs[:, a, :], gabs[:, a, :], 0.25, None, ALU.max))
                link(dve.tensor_scalar(gsgn[:, a, :], modr[:, a, :], 0.0, 2.0, ALU.is_ge, ALU.mult))
                link(dve.scalar_tensor_tensor(modr[:, a, :], gsgn[:, a, :], 1.0, gabs[:, a, :], ALU.subtract, ALU.mult))
            link(dve.tensor_scalar(modr[:, 2, :], modr[:, 2, :], 1.0, None, ALU.add))
            dve.tensor_copy(sel8, ident[0:BATCH, 0:BATCH].rearrange("p (b a) -> p b a", a=1).broadcast_to([BATCH, BATCH, P])
                            ).then_inc(mod_rows, 1)
            for b in range(GB):
                a_u(b)
            dve.wait_ge(pro_products, 2)
            dve.tensor_scalar(flag[:, :], yp[0:1, 3 * P:3 * P + 1], 2.0, None, ALU.mult).then_inc(flag_set, 1)
            dve.tensor_copy(wgt[:, :], yp[:, P:2 * P]).then_inc(pro_copied, 1)
            for b in range(GB):
                a_gate(b)
            link(dve.tensor_tensor(slow[:, :], araw[:, :], nottiny[:, :], ALU.mult))
            link(dve.tensor_tensor(slow[:, :], slow[:, :], tiny[:, :], ALU.add))
            link(dve.tensor_tensor(slow[:, :], slow[:, :], small[:, :], ALU.mult))
            for b in range(GB):
                a_t1(b)
            for b in range(GB):
                a_base(b)
            for b in range(GB):
                a_split(b)
            for b in range(GB):
                a_dt(b)

            def fold_gates():
                dve.wait_ge(mod_copied, 2 * BATCH)
                link(dve.tensor_scalar(wo[:, :], wo[:, :], 0.25, None, ALU.mult))
                dve.tensor_tensor(woga[:, :, :], wo[:, :].rearrange("p (a c) -> p a c", a=1).broadcast_to([P, BATCH, P]),
                                  gab, ALU.mult).then_inc(wout_ready, 1)

            dve.wait_ge(flag_set, 1)
            smalls = dve.value_load(flag[0:1, 0:1])

            def small_a(g):
                step = [g * (GB + 5 * GB * NST)]

                def then(ins):
                    step[0] += 1
                    ins.then_inc(small_chain, 1)
                    dve.wait_ge(small_chain, step[0])

                with dve.If(smalls > 0):
                    dve.wait_ge(dt_ready, GB * (g + 1))
                    dve.sem_inc(small_go, 1)
                    for j in range(GB):
                        then(dve.tensor_tensor(rem[:, j, :], dtb[:, g % 2, j, 0:SEQ], ub[:, j, 0:SEQ], ALU.mult))
                    for i in range(GB * NST):
                        n, j = divmod(i, GB)
                        k = g * GB * NST + i
                        dve.wait_ge(small_decay, k + 1)
                        then(dve.scalar_tensor_tensor(lnx[:, j, :], expx[:, j, :], 1.0, ub[:, j, 0:SEQ],
                                                      ALU.subtract, ALU.mult))
                        then(dve.tensor_scalar(lnx[:, j, :], lnx[:, j, :], nottiny[:, n:n + 1], None, ALU.mult))
                        then(dve.scalar_tensor_tensor(lnx[:, j, :], rem[:, j, :], tiny[:, n:n + 1], lnx[:, j, :],
                                                      ALU.mult, ALU.add))
                        then(dve.tensor_tensor_scan(th[:, j, :], expx[:, j, :], lnx[:, j, :], 0.0, ALU.mult, ALU.add))
                        dve.wait_ge(small_C, k + 1)
                        then(dve.tensor_tensor(lnx[:, j, :], th[:, j, :], cc[:, :], ALU.mult))
                        dve.scalar_tensor_tensor(base[:, g % 2, j, :], lnx[:, j, :], slow[:, n:n + 1],
                                                 base[:, g % 2, j, :], ALU.mult, ALU.add).then_inc(small_used, 1)
                        dve.wait_ge(small_used, k + 1)

            for m in range(SLOTS_B):
                g, n = divmod(m, NST)
                if n == 0 and g < GROUPS:
                    small_a(g)
                if m < STEPS:
                    b_scan_(m)
                if 0 < g < GROUPS and n == C_AT["yd"]:
                    c_yd_(g - 1)
                if m == 1:
                    fold_gates()
                if 1 <= m <= STEPS:
                    b_mult(m - 1)
                if g and g < GROUPS:
                    for j in range(GB):
                        if n == C_AT["res"] + j:
                            c_res(GB * (g - 1) + j)
                        if n == C_AT["norm"] + j:
                            c_norm(GB * (g - 1) + j)
                        if n == C_AT["nm"] + j:
                            c_nm_(GB * (g - 1) + j)
                    if n == C_AT["router"]:
                        c_router(g - 1)
                    if n == C_AT["slots"]:
                        c_slots(g - 1)
                if g + 1 < GROUPS:
                    for j in range(GB):
                        b, p = GB * (g + 1) + j, n - A_APART * j
                        if p == A_AT["stats"]:
                            a_stats(b)
                        if p == A_AT["nm"]:
                            a_nm(b)
                        if p == A_AT["u"]:
                            a_u(b)
                        if p == A_AT["gate"]:
                            a_gate(b)
                        if p == A_AT["base"]:
                            a_base(b)
                        if p == A_AT["t1"]:
                            a_t1(b)
                        if p == A_AT["split"]:
                            a_split(b)
                    if n == DT_AT:
                        a_dt(GB * g + GB)
                        a_dt(GB * g + GB + 1)
            g = GROUPS - 1
            dve.wait_ge(summed, STEPS)
            dve.wait_ge(gated, g)
            dve.wait_ge(logits_ready, g)
            dve.wait_ge(h2_ready, GB * g)
            for j in range(GB):
                t = slice(j * SEQ, (j + 1) * SEQ)
                link(dve.tensor_tensor(yd[:, t], yp[:, t], base[:, g % 2, j, :], ALU.subtract))
                dve.tensor_tensor(yg[:, t], yd[:, t], gate[:, g % 2, t], ALU.mult).then_inc(gated, 1)
            for b in range(GB * g, BATCH):
                c_res(b)
                c_norm(b)
            for b in range(GB * g, BATCH):
                c_nm_(b)
            b = BATCH - 1
            j = slice(4 * (b % GB), 4 * (b % GB) + 4)
            dve.wait_ge(normed_c, b + 1)
            link(dve.tensor_tensor(xn2[:, j, :], xn2[:, j, :], modb[:, b, 1:2, :].broadcast_to([P, 4, P]), ALU.mult))
            dve.tensor_tensor(h2[:, j, :], xn2[:, j, :], modb[:, b, 0:1, :].broadcast_to([P, 4, P]),
                              ALU.add).then_inc(h2_last, 1)
            c_router(g)
            c_slots(g)
            experts_vector(dve)

        @block.tensor
        def _(pe):
            def a_xT(b):
                pe.wait_ge(normed_a, b + 1)
                if b >= GB:
                    pe.wait_ge(abs_ready, b)
                    pe.wait_ge(relu_ready, b)
                for j in range(4):
                    last = pe.transpose(bank(b, 0)[:, j * P:(j + 1) * P], xn[:, 4 * (b % GB) + j, :], ident[:, :])
                last.then_inc(turned_a, 1)

            def a_proj(b, i, w, done):
                pe.matmul(bank(b, i), w, hT[:, b % GB, HPAD:], start=True, stop=True).then_inc(done, 1)

            def a_z(b):
                if b >= GB:
                    pe.wait_ge(C_copied, b)
                pe.wait_ge(hT_ready, b + 1)
                a_proj(b, 1, wz[:, :], z_ready)

            def a_conv(b, taps=range(KCONV)):
                if taps[0] == 0:
                    pe.wait_ge(hT_ready, b + 1)
                    pe.wait_ge(conv_diag, 1)
                for k in taps:
                    last = pe.matmul(bank(b, 0)[:, :], dconv[:, k, :], hT[:, b % GB, k:k + SEQ],
                                     start=(k == 0), stop=(k == KCONV - 1))
                if k == KCONV - 1:
                    last.then_inc(conv_ready, 1)

            def a_G(b):
                pe.wait_ge(gate_ready, b + 1)
                a_proj(b, 1, wgt[:, :], G_ready)

            def a_dtx(b):
                pe.wait_ge(u_ready, b + 1)
                a_proj(b, 0, wdtp[:, :], dtx_ready)

            def a_C(b):
                pe.wait_ge(G_used, b + 1)
                for t in range(4):
                    last = pe.matmul(bank(b, 1)[:, t * NST:(t + 1) * NST], hT[:, b % GB, HPAD + t * P:HPAD + (t + 1) * P],
                                     wct[:, :], start=True, stop=True)
                last.then_inc(C_ready, 1)

            def a_cT(b):
                pe.wait_ge(C_split, b + 1)
                v = bank(b, 1)[0:NPART * NST, 128:128 + SEQ // 2].bitcast(BF16)
                for t in range(4):
                    last = pe.transpose(v[:, t * P:(t + 1) * P],
                                        cs[:, 4 * (b % GB) + t, :, :].rearrange("p c n -> p (c n)"), identb[:, :])
                last.then_inc(C_turned, 1)

            def b_cb_(h):
                m, j = divmod(h, GB)
                g, n = divmod(m, NST)
                if n == 0 and j == 0:
                    pe.wait_ge(C_copied, GB * (g + 1))
                if h == 0:
                    pe.wait_ge(mod_copied, 2 * BATCH)
                if h >= 3:
                    k, i = divmod(h - 3, GB)
                    if on_pool(k):
                        pe.wait_ge(C_spread_copied, GB * pool_before(k) + i + 1)
                    else:
                        pe.wait_ge(dve_product, GB * dve_before(k) + i + 1)
                pe.matmul(cb[h % 3], sel[:, n, :], ct3[:, g * GT + j * SEQ:g * GT + (j + 1) * SEQ],
                          start=True, stop=True).then_inc(C_spread, 1)

            def b_sum_(m):
                g, n = divmod(m, NST)
                if m == 0:
                    pe.wait_ge(weight_diag, 1)
                    pe.wait_ge(pro_copied, 4)
                if on_pool(m):
                    pe.wait_ge(pool_product, pool_before(m) + 1)
                    src = pp[:, pool_before(m) % RING_P, :]
                else:
                    pe.wait_ge(dve_product, GB * (dve_before(m) + 1))
                    src = pd[:, dve_before(m) % RING_P, :]
                place = SUM_PLACE[m] % NST
                if place == 0 and g:
                    pe.wait_ge(y_ready, g)
                for j in range(GB):
                    last = pe.matmul(yp[:, j * SEQ:(j + 1) * SEQ], diag[:, n, :], src[:, j * SEQ:(j + 1) * SEQ],
                                     start=(place == 0), stop=(place == NST - 1))
                last.then_inc(summed, 1)

            def c_out(b):
                pe.wait_ge(gated, b // GB + 1 + (b == BATCH - 1))
                if b == 0:
                    pe.wait_ge(wout_ready, 1)
                if b == BATCH - 1:
                    pe.wait_ge(relu_ready, BATCH)
                elif b % GB:
                    pe.wait_ge(x2_ready, b)
                elif b:
                    pe.wait_ge(routed, b // GB)
                for i in range(4):
                    t = (4 * (b % GB) + i) * P
                    last = pe.matmul(cbank(b)[:, i * P:(i + 1) * P], yg[:, t:t + P], woga[:, b, :], start=True, stop=True)
                last.then_inc(projected, 1)

            def c_trans(b):
                if b == BATCH - 1:
                    pe.wait_ge(h2_last, 1)
                else:
                    pe.wait_ge(h2_ready, b + 1)
                pe.wait_ge(x2_ready, GB * (b // GB + 1))
                if b % GB and b < BATCH - 1:
                    pe.wait_ge(h2T_ready, b)
                for i in range(4):
                    last = pe.transpose(cbank(b)[:, i * P:(i + 1) * P], h2[:, 4 * (b % GB) + i, :], ident[:, :])
                last.then_inc(h2_turned, 1)

            def c_logits(g, tiles=range(GTILES)):
                pe.wait_ge(h2T_ready, GB * g + tiles[-1] // 4 + 1)
                for i in tiles:
                    last = pe.matmul(cc[:, i * NEXP:(i + 1) * NEXP], h2T[:, i * P:(i + 1) * P], gw[:, :],
                                     start=True, stop=True)
                if i == GTILES - 1:
                    last.then_inc(logits_ready, 1)

            def c_rank(g):
                pe.wait_ge(onehot_ready, g + 1)
                if g:
                    pe.wait_ge(routed, g)
                rk = cc[:, 256:256 + GTILES * NEXP].rearrange("p (i n) -> p i n", n=NEXP)
                pe.matmul(rk, tri[:, :], oh[:, :, :], start=True, stop=False, skip_group_check=True)
                for i in range(GTILES - 1):
                    pe.matmul(rk[:, i + 1:, :], ones[:, :], oh[:, i:i + 1, :].broadcast_to([P, GTILES - 1 - i, NEXP]),
                              start=False, stop=False, skip_group_check=True)
                pe.matmul(rk, ones[:, :], seenb[:, :].rearrange("p (a n) -> p a n", a=1).broadcast_to([P, GTILES, NEXP]),
                          start=False, stop=True, skip_group_check=True).then_inc(ranks_ready, 1)

            zeros512 = hT[:, 0, 0:1].broadcast_to([P, SEQ])

            def keep_warm(n):
                for _ in range(n):
                    pe.matmul(cb[2][0:GTILES, :], halfneg[:, :], zeros512, start=True, stop=True)

            pe.wait_ge(consts_set, 7)
            keep_warm(WARM_START)
            pe.wait_ge(first_loaded, NW0)
            pe.wait_ge(silu_c, 1)
            pe.matmul(yp[:, 0:BATCH], wm[:, 0:P], silc[:, :], start=True, stop=True)
            pe.matmul(yp[:, BATCH:2 * BATCH], wm[:, P:2 * P], silc[:, :], start=True, stop=True)
            pe.matmul(cb[0][0:BATCH, :], silc[:, :], wm[:, 2 * P:6 * P], start=True, stop=True)
            pe.matmul(yp[:, 2 * P:3 * P], wp[:, :], wdt[:, :], start=True, stop=True).then_inc(pro_products, 1)
            a_xT(0)
            a_xT(1)
            for b in range(GB):
                a_conv(b)
            pe.wait_ge(a_ready, 1)
            pe.wait_ge(weights_loaded, NW)
            pe.matmul(yp[0:1, 3 * P:3 * P + 1], smallest[:, :], halfneg[:, 0:1], start=True, stop=True)
            pe.matmul(yp[:, P:2 * P], wc[:, :], ainvT[:, :], start=True, stop=True).then_inc(pro_products, 1)
            for b in range(GB):
                a_z(b)
            def p_modp(b):
                pe.wait_ge(mod_rows, 1)
                if b >= 3:
                    pe.wait_ge(mod_copied, 2 * (b - 2))
                pe.matmul(cb[b % 3], sel8[:, b, :], modr[:, :, :], start=True, stop=True).then_inc(mod_spread, 1)

            for b in range(GB):
                a_dtx(b)
            for b in range(3):
                p_modp(b)
            pe.wait_ge(pro_copied, 4)
            for b in range(GB):
                a_G(b)
            for b in range(3, BATCH):
                p_modp(b)
            for b in range(GB):
                a_C(b)
            pe.wait_ge(consts_set, 8)
            for b in range(GB):
                a_cT(b)
            pe.wait_ge(flag_set, 1)
            smalls = pe.value_load(flag[0:1, 0:1])

            def small_a(g):
                with pe.If(smalls > 0):
                    pe.wait_ge(C_copied, GB * (g + 1))
                    pe.wait_ge(small_go, g + 1)
                    for i in range(GB * NST):
                        n, j = divmod(i, GB)
                        k = g * GB * NST + i
                        if k:
                            pe.wait_ge(small_used, k)
                        pe.matmul(cc[:, :], sel[:, n, :], ct3[:, g * GT + j * SEQ:g * GT + (j + 1) * SEQ],
                                  start=True, stop=True).then_inc(small_C, 1)
                    pe.wait_ge(small_used, (g + 1) * GB * NST)

            for m in range(SLOTS_B):
                g, n = divmod(m, NST)
                if n == 0 and g < GROUPS:
                    small_a(g)
                halves = [h for h in (GB * m - 1 + C_AHEAD, GB * m + C_AHEAD) if 0 <= h < GB * STEPS]
                for h in halves[:1]:
                    b_cb_(h)
                for k in sums_at(m):
                    b_sum_(k)
                for h in halves[1:]:
                    b_cb_(h)
                if g and g < GROUPS:
                    for j in range(GB):
                        if n == C_AT["out"] + j:
                            c_out(GB * (g - 1) + j)
                        if n == C_AT["trans"] + j:
                            c_trans(GB * (g - 1) + j)
                    if n == C_AT["logits"]:
                        c_logits(g - 1)
                    if n == C_AT["rank"]:
                        c_rank(g - 1)
                if g + 1 < GROUPS:
                    for j in range(GB):
                        b, p = GB * (g + 1) + j, n - A_APART * j
                        if p == A_AT["xT"]:
                            a_xT(b)
                        if p == A_AT["conv"]:
                            a_conv(b, range(CONV_CUT))
                        if p == A_AT["conv2"]:
                            a_conv(b, range(CONV_CUT, KCONV))
                        if p == A_AT["z"]:
                            a_z(b)
                        if p == A_AT["dtx"]:
                            a_dtx(b)
                        if p == A_AT["G"]:
                            a_G(b)
                        if p == A_AT["C"]:
                            a_C(b)
                        if p == A_AT["cT"]:
                            a_cT(b)
            g = GROUPS - 1
            for b in range(GB * g, BATCH):
                c_out(b)
            keep_warm(WARM_PROJ)
            for b in range(GB * g, BATCH):
                c_trans(b)
                if b == BATCH - 1:
                    c_logits(g, range(0, 4))
                    c_logits(g, range(4, GTILES))
            c_rank(g)
            keep_warm(WARM_ROUTED)
            experts_tensor(pe)


def kernel(**inputs):
    import concourse.bacc as bacc
    from concourse.bass_utils import run_bass_kernel_spmd
    import ml_dtypes

    nc = bacc.Bacc("TRN2", target_bir_lowering=False, num_devices=1)
    a = {k: np.asarray(v) for k, v in inputs.items()}
    one = np.arange(NPART * NST)
    i = np.arange(P)
    arrays = {
        "x": a["L0_attn_x"], "w_zT": a["L0_attn_W_z"].T, "w_params": a["L0_attn_W_params"],
        "w_paramsT": a["L0_attn_W_params"].T, "conv_w": a["L0_attn_conv_w"], "w_dtT": a["L0_attn_W_dt"].T,
        "b_dt": a["L0_attn_b_dt"], "a_log": a["L0_attn_A_log"], "a_logT": a["L0_attn_A_log"].T,
        "d_skip": a["L0_attn_D"], "w_outT": a["L0_attn_W_out"].T, "gate_wT": a["L0_ffn_gate_w"].T,
        "w1": a["L0_ffn_w1"], "w2": a["L0_ffn_w2"], "cT": a["L0_c"].T, "wmod": a["L0_wmod"],
        "ident_in": np.eye(P, dtype=np.float32),
        "sel_in": np.ascontiguousarray(np.broadcast_to((one[:, None] % NST == np.arange(NST))[:, :, None],
                                                       (NPART * NST, NST, P))).astype(ml_dtypes.bfloat16),
        "tri_in": (i[:, None] < i[None, :]).astype(ml_dtypes.bfloat16),
        "em16_in": np.broadcast_to(np.arange(NEXP, dtype=np.float32) - NEXP, (P, NEXP)),
        "tok_in": (SLOTS + i[:, None] + P * np.arange(TILES)[None, :]).astype(np.float32),
    }
    arrays = {k: np.ascontiguousarray(v) for k, v in arrays.items()}
    args = [nc.dram_tensor(k, v.shape, mybir.dt.from_np(v.dtype), kind="ExternalInput").ap() for k, v in arrays.items()]
    out = nc.dram_tensor("out", (BATCH, SEQ, E), F32, kind="ExternalOutput").ap()
    build(nc, *args, out)
    r = run_bass_kernel_spmd(nc, [arrays], core_ids=[0])
    return r.results[0]["out"]
```
